# Optimizing a Trainium2 kernel written in Bass

```python
import numpy as np
import jax
import jax.numpy as jnp

def _softmax(x, axis=-1):
    return jax.nn.softmax(x, axis=axis)

def _gelu(x):
    return jax.nn.gelu(x, approximate=True)

def _silu(x):
    return jax.nn.silu(x)

def _sigmoid(x):
    return jax.nn.sigmoid(x)

def _layernorm(x, axis=-1, eps=1e-05):
    m = jnp.mean(x, axis=axis, keepdims=True)
    v = jnp.var(x, axis=axis, keepdims=True)
    return (x - m) / jnp.sqrt(v + eps)

def _scatter_add(tgt, idx, src, axis=0):
    return tgt.at[idx].add(src)

def _segment_sum(src, seg, n):
    return jax.ops.segment_sum(src, seg, n)
kernel_name = 'mk_flamingo_gated_d1_seqx_r4_477e85'

def setup_inputs(seed: int=0):
    np.random.seed(seed)
    _w = jnp.asarray

    def _rec_inputs():
        import jax
        import jax.numpy as jnp
        _rk = jax.random.key(seed)
        x = -9.806e-05 + 1 * jax.random.normal(jax.random.fold_in(_rk, 1), (1, 2048, 256), jnp.float32)
        _lenS = 2048 - jax.random.randint(jax.random.fold_in(_rk, 7), (1,), 0, max(1, 2048 // 4) + 1, jnp.int32)
        _lenS2 = 1601 - jax.random.randint(jax.random.fold_in(_rk, 8), (1,), 0, max(1, 1601 // 4) + 1, jnp.int32)
        _ctx_1024P = jax.random.normal(jax.random.fold_in(_rk, 11), (1, 16, 256), jnp.float32)
        _ctx_1024c = jax.random.dirichlet(jax.random.fold_in(_rk, 511), 0.3 * jnp.ones((16,), jnp.float32), (1, 1601))
        _ctx_1024t = jnp.einsum('bsk,bkd->bsd', _ctx_1024c, _ctx_1024P)
        _ctx_1024t = _ctx_1024t * jax.lax.rsqrt(jnp.mean(jnp.square(_ctx_1024t)) + 1e-12) * 0.953939
        ctx_1024 = -1.52775e-05 + 0.999936 * (_ctx_1024t + 0.3 * jax.random.normal(jax.random.fold_in(_rk, 611), (1, 1601, 256), jnp.float32))
        _g = jax.random.normal(jax.random.fold_in(_rk, 9001), (2, 1), jnp.float32)
        _g = jnp.sign(_g) * jnp.maximum(jnp.abs(_g), 1.0) + (_g == 0) * 1.0
        g_xattn = _g[0]
        g_ffn = _g[1]
        return (x, ctx_1024, g_xattn, g_ffn)
    x, ctx_1024, g_xattn, g_ffn = _rec_inputs()

    def _L0_xattn_setup():
        import jax, jax.numpy as jnp
        import numpy as np
        D = 256
        NUM_ITERS = 3
        EPS = 1e-06
        SCALE = D ** (-0.5)

        def rmsnorm(x, w, eps=EPS):
            return x * jax.lax.rsqrt(jnp.mean(x * x, axis=-1, keepdims=True) + eps) * w

        def gru_cell(x, h, wih, whh, bih, bhh):
            gx = x @ wih.T + bih
            gh = h @ whh.T + bhh
            xr, xz, xn = jnp.split(gx, 3, axis=-1)
            hr, hz, hn = jnp.split(gh, 3, axis=-1)
            r = jax.nn.sigmoid(xr + hr)
            z = jax.nn.sigmoid(xz + hz)
            n = jnp.tanh(xn + r * hn)
            return (1.0 - z) * n + z * h
        key = jax.random.key(seed)
        ks = jax.random.split(key, 8)
        B, K, M, d = (8, 64, 1024, D)
        w_std = d ** (-0.5)
        return {'slots': jax.random.normal(ks[0], (B, K, d), jnp.float32), 'P': jax.random.normal(ks[1], (B, M, d), jnp.float32), 'Wq': jax.random.normal(ks[2], (d, d), jnp.float32) * w_std, 'Wk': jax.random.normal(ks[3], (d, d), jnp.float32) * w_std, 'Wv': jax.random.normal(ks[4], (d, d), jnp.float32) * w_std, 'gru_wih': jax.random.normal(ks[5], (3 * d, d), jnp.float32) * w_std, 'gru_whh': jax.random.normal(ks[6], (3 * d, d), jnp.float32) * w_std, 'gru_bih': jnp.zeros((3 * d,), jnp.float32), 'gru_bhh': jnp.zeros((3 * d,), jnp.float32), 'slot_norm_w': jnp.ones((d,), jnp.float32), 'input_norm_w': jnp.ones((d,), jnp.float32)}
    _L0_xattn_all = _L0_xattn_setup()
    _L0_xattn_in = {k: v for k, v in _L0_xattn_all.items() if k in ('Wq', 'Wk', 'Wv', 'gru_wih', 'gru_whh', 'gru_bih', 'gru_bhh', 'slot_norm_w', 'input_norm_w')}
    del _L0_xattn_all

    def _L0_ffn_setup():
        import jax, jax.numpy as jnp
        import numpy as np
        H = 256
        DFF = 1024
        E_ROUTED = 7
        TOP_K = 2

        def _swiglu(flat, gate_w, up_w, down_w):
            g = flat @ gate_w.T
            up = flat @ up_w.T
            return jax.nn.silu(g) * up @ down_w.T
        key = jax.random.key(seed)
        ks = jax.random.split(key, 8)
        s = 0.02
        return {'x': jax.random.normal(ks[0], (4, 512, H), jnp.float32), 'shared_up': jax.random.normal(ks[1], (DFF, H), jnp.float32) * s, 'shared_gate': jax.random.normal(ks[2], (DFF, H), jnp.float32) * s, 'shared_down': jax.random.normal(ks[3], (H, DFF), jnp.float32) * s, 'routed_up': jax.random.normal(ks[4], (E_ROUTED, DFF, H), jnp.float32) * s, 'routed_gate': jax.random.normal(ks[5], (E_ROUTED, DFF, H), jnp.float32) * s, 'routed_down': jax.random.normal(ks[6], (E_ROUTED, H, DFF), jnp.float32) * s, 'router_w': jax.random.normal(ks[7], (E_ROUTED, H), jnp.float32) * 0.02}
    _L0_ffn_all = _L0_ffn_setup()
    _L0_ffn_in = {k: v for k, v in _L0_ffn_all.items() if k in ('shared_up', 'shared_gate', 'shared_down', 'routed_up', 'routed_gate', 'routed_down', 'router_w')}
    del _L0_ffn_all
    return {'x': x, 'ctx_1024': ctx_1024, 'g_xattn': g_xattn, 'g_ffn': g_ffn, 'L0_xattn_Wq': _L0_xattn_in['Wq'], 'L0_xattn_Wk': _L0_xattn_in['Wk'], 'L0_xattn_Wv': _L0_xattn_in['Wv'], 'L0_xattn_gru_wih': _L0_xattn_in['gru_wih'], 'L0_xattn_gru_whh': _L0_xattn_in['gru_whh'], 'L0_xattn_gru_bih': _L0_xattn_in['gru_bih'], 'L0_xattn_gru_bhh': _L0_xattn_in['gru_bhh'], 'L0_xattn_slot_norm_w': _L0_xattn_in['slot_norm_w'], 'L0_xattn_input_norm_w': _L0_xattn_in['input_norm_w'], 'L0_ffn_shared_up': _L0_ffn_in['shared_up'], 'L0_ffn_shared_gate': _L0_ffn_in['shared_gate'], 'L0_ffn_shared_down': _L0_ffn_in['shared_down'], 'L0_ffn_routed_up': _L0_ffn_in['routed_up'], 'L0_ffn_routed_gate': _L0_ffn_in['routed_gate'], 'L0_ffn_routed_down': _L0_ffn_in['routed_down'], 'L0_ffn_router_w': _L0_ffn_in['router_w']}

def reference(x, ctx_1024, g_xattn, g_ffn, L0_xattn_Wq, L0_xattn_Wk, L0_xattn_Wv, L0_xattn_gru_wih, L0_xattn_gru_whh, L0_xattn_gru_bih, L0_xattn_gru_bhh, L0_xattn_slot_norm_w, L0_xattn_input_norm_w, L0_ffn_shared_up, L0_ffn_shared_gate, L0_ffn_shared_down, L0_ffn_routed_up, L0_ffn_routed_gate, L0_ffn_routed_down, L0_ffn_router_w):
    import jax
    import jax.numpy as jnp

    def _L0_xattn_ref(slots, P, Wq, Wk, Wv, gru_wih, gru_whh, gru_bih, gru_bhh, slot_norm_w, input_norm_w):
        import jax, jax.numpy as jnp
        import numpy as np
        D = 256
        NUM_ITERS = 3
        EPS = 1e-06
        SCALE = D ** (-0.5)

        def rmsnorm(x, w, eps=EPS):
            return x * jax.lax.rsqrt(jnp.mean(x * x, axis=-1, keepdims=True) + eps) * w

        def gru_cell(x, h, wih, whh, bih, bhh):
            gx = x @ wih.T + bih
            gh = h @ whh.T + bhh
            xr, xz, xn = jnp.split(gx, 3, axis=-1)
            hr, hz, hn = jnp.split(gh, 3, axis=-1)
            r = jax.nn.sigmoid(xr + hr)
            z = jax.nn.sigmoid(xz + hz)
            n = jnp.tanh(xn + r * hn)
            return (1.0 - z) * n + z * h
        Pn = rmsnorm(P, input_norm_w)
        k_proj = Pn @ Wk.T
        v_proj = Pn @ Wv.T
        for _ in range(NUM_ITERS):
            sn = rmsnorm(slots, slot_norm_w)
            q_proj = sn @ Wq.T
            scores = jnp.einsum('bkd,bmd->bkm', q_proj, k_proj) * SCALE
            attn = jax.nn.softmax(scores, axis=-2)
            attn = attn / (jnp.sum(attn, axis=-1, keepdims=True) + EPS)
            updates = jnp.einsum('bkm,bmd->bkd', attn, v_proj)
            slots = gru_cell(updates, slots, gru_wih, gru_whh, gru_bih, gru_bhh)
        return slots

    def _L0_ffn_ref(x, shared_up, shared_gate, shared_down, routed_up, routed_gate, routed_down, router_w):
        import jax, jax.numpy as jnp
        import numpy as np
        H = 256
        DFF = 1024
        E_ROUTED = 7
        TOP_K = 2

        def _swiglu(flat, gate_w, up_w, down_w):
            g = flat @ gate_w.T
            up = flat @ up_w.T
            return jax.nn.silu(g) * up @ down_w.T
        orig_shape = x.shape
        flat = x.reshape(-1, H)
        out = _swiglu(flat, shared_gate, shared_up, shared_down)
        logits = flat @ router_w.T
        probs = jax.nn.softmax(logits, axis=-1)
        top_vals, top_idx = jax.lax.top_k(probs, TOP_K)
        top_vals = top_vals / (top_vals.sum(-1, keepdims=True) + 1e-09)
        combine = jnp.sum(jax.nn.one_hot(top_idx, E_ROUTED, dtype=flat.dtype) * top_vals[..., None], axis=1)
        routed = jnp.zeros_like(flat)
        for e in range(E_ROUTED):
            eo = _swiglu(flat, routed_gate[e], routed_up[e], routed_down[e])
            routed = routed + combine[:, e:e + 1] * eo
        return (out + routed).reshape(orig_shape)
    x = x + jnp.tanh(g_xattn[0]) * _L0_xattn_ref(_layernorm(x, axis=-1), ctx_1024, L0_xattn_Wq, L0_xattn_Wk, L0_xattn_Wv, L0_xattn_gru_wih, L0_xattn_gru_whh, L0_xattn_gru_bih, L0_xattn_gru_bhh, L0_xattn_slot_norm_w, L0_xattn_input_norm_w)
    x = x + jnp.tanh(g_ffn[0]) * _L0_ffn_ref(_layernorm(x, axis=-1), L0_ffn_shared_up, L0_ffn_shared_gate, L0_ffn_shared_down, L0_ffn_routed_up, L0_ffn_routed_gate, L0_ffn_routed_down, L0_ffn_router_w)
    return x

_drawn_inputs = setup_inputs


def setup_inputs(seed=0):
    import zlib

    import numpy as np

    out = dict(_drawn_inputs(seed))
    spreads = {'L0_xattn_gru_bih': (0.0, 0.1),
     'L0_xattn_gru_bhh': (0.0, 0.271),
     'L0_xattn_slot_norm_w': (1.0, 0.6),
     'L0_xattn_input_norm_w': (1.0, 0.2)}
    factors = {'L0_ffn_routed_up': 2.945,
     'L0_ffn_routed_gate': 2.977,
     'L0_ffn_routed_down': 2.942,
     'L0_ffn_router_w': 3.511}
    for name, (base, spread) in spreads.items():
        noise = np.random.default_rng([zlib.crc32(name.encode()), seed]).standard_normal(out[name].shape)
        drawn = base * np.exp(spread * noise) if base else spread * noise
        out[name] = jnp.asarray(drawn.astype(out[name].dtype))
    for name, factor in factors.items():
        out[name] = (out[name] * factor).astype(out[name].dtype)
    return out
```

```python
import concourse.bass as bass
from concourse import mybir
from contextlib import ExitStack

F32 = mybir.dt.float32
F32R = mybir.dt.float32r
I32 = mybir.dt.int32
U32 = mybir.dt.uint32
ALU = mybir.AluOpType
ACT = mybir.ActivationFunctionType
AX = mybir.AxisListType

P = 128
S = 2048
M = 1601
D = 256
DH = D // P
CW = 512
NC = S // CW
NT = S // P
TPC = CW // P
MT = -(-M // P)
MPAD = M + 1
ITERS = 3
EPS_NORM = 1e-6
EPS_ATTN = 1e-6
EPS_LN = 1e-5
EPS_TOP = 1e-9
SCALE = float(D) ** -0.5
DFF = 1024
FT = DFF // P
ROUTED = 7
EXPERTS = ROUTED + 1
WCOLS = 3 * DH * DFF
PIECE = 768
PIECES = WCOLS // PIECE
UP_AT, DOWN_AT = DH * DFF, 2 * DH * DFF
MAGIC = float(0x5F3759DF)


class Store:
    pass


def rows_of(t):
    return min(P, M - t * P)


BLOCKS = [(0, 1, 2), (3, 4, 5), (6, 7, 8), (9, 10), (11, 12)]
E_SLOTS = 6
E_SLOT = {t: 3 * (b % 2) + i for b, ts in enumerate(BLOCKS) for i, t in enumerate(ts)}
ITEMS = [(b, c) for b in range(len(BLOCKS)) for c in range(NC)]
AFTER = {3: [0], 4: [1], 5: [2, 3], 6: [4], 7: [5], 8: [6, 7], 9: [8, 9], 10: [10, 11],
         11: [12, 13], 12: [14, 15]}
TAIL = [16, 17, 18, 19]
PAIRS = [(i, t) for i, (b, _) in enumerate(ITEMS) for t in BLOCKS[b]]
PAIRS_OF = {i: [n for n, (k, _) in enumerate(PAIRS) if k == i] for i in range(len(ITEMS))}
NPAIR, NITEM = len(PAIRS), len(ITEMS)
RING = 4


def rsqrt(nc, dve, g, y, x, n):
    i, t, u = g.ni[:, 0:n], g.na[:, 0:n], g.nb[:, 0:n]
    dve.drain()
    nc.vector.tensor_scalar(i, x.bitcast(I32), 1, None, ALU.logical_shift_right)
    dve.drain()
    nc.vector.tensor_scalar(y.bitcast(I32), i, -1.0, MAGIC, ALU.mult, ALU.add)
    for _ in range(4):
        dve.drain()
        nc.vector.tensor_tensor(t, y, y, ALU.mult)
        dve.drain()
        nc.vector.scalar_tensor_tensor(u, t, -0.5, x, ALU.mult, ALU.mult)
        dve.drain()
        nc.vector.scalar_tensor_tensor(y, u, 1.5, y, ALU.add, ALU.mult)
    dve.drain()

def diagonal(nc, g, dst, col, n):
    return nc.vector.tensor_tensor(dst, g.ident[:].unsqueeze(1).broadcast_to([P, n, P]),
                                   col.unsqueeze(2).broadcast_to([P, n, P]), ALU.mult)

def split3(nc, dst, w_hi, w_lo, m_hi, m_lo, start, stop):
    nc.tensor.matmul(dst, w_hi, m_hi, start=start, stop=False)
    nc.tensor.matmul(dst, w_lo, m_hi, start=False, stop=False)
    return nc.tensor.matmul(dst, w_hi, m_lo, start=False, stop=stop)


def build_kernel(nc, a, out):
    g = Store()
    with ExitStack() as ctx:
        base = -(-nc.sbuf_base // 32) * 32

        def place(name, shape, dt, at):
            return nc.alloc_sbuf_tensor_at(name, shape, dt, offset=base + at)

        def semaphores(*names):
            return [ctx.enter_context(nc.semaphore(n)) for n in names]

        g.psum = [ctx.enter_context(nc.psum_tensor(f"quad{i}", [P, 4, CW], F32)) for i in range(2)]

        g.h_at = 0
        g.acc_at = g.h_at + 2 * DH * S * 4
        g.rstd_at = g.acc_at + DH * S * 4
        g.k_at = g.rstd_at + S * 4
        g.k_size = -(-DH * MPAD * 4 // 32) * 32
        g.v_at = g.k_at + 2 * g.k_size
        g.v_size = MT * D * 4
        g.gw_at = g.v_at + 2 * g.v_size
        g.gw_size = DH * 3 * D * 4
        g.e_at = g.gw_at + 4 * g.gw_size
        g.racc_at = g.e_at + E_SLOTS * S * 4
        g.ring_at = g.racc_at + S * 4
        g.small_at = g.ring_at + RING * 2 * CW * 4
        small = [g.small_at]

        def tiny(name, shape, dt=F32):
            at = small[0]
            n = 4
            for k in shape[1:]:
                n *= k
            small[0] += -(-n // 32) * 32
            return place(name, shape, dt, at)

        g.h_hi = place("h_hi", [P, DH, S], F32R, g.h_at)
        g.h_lo = place("h_lo", [P, DH, S], F32R, g.h_at + DH * S * 4)
        g.acc = place("acc", [P, DH, S], F32, g.acc_at)
        g.rstd_all = place("rstd_all", [P, S], F32, g.rstd_at)
        g.k_hi = place("k_hi", [P, DH, MPAD], F32R, g.k_at)
        g.k_lo = place("k_lo", [P, DH, MPAD], F32R, g.k_at + g.k_size)
        g.v_hi = place("v_hi", [P, MT, D], F32R, g.v_at)
        g.v_lo = place("v_lo", [P, MT, D], F32R, g.v_at + g.v_size)
        g.wih_hi, g.wih_lo, g.whh_hi, g.whh_lo = (
            place(n, [P, DH, 3 * D], F32R, g.gw_at + i * g.gw_size)
            for i, n in enumerate(("wih_hi", "wih_lo", "whh_hi", "whh_lo")))
        g.E = place("E", [P, E_SLOTS, S], F32, g.e_at)
        g.racc = place("racc", [P, S], F32, g.racc_at)
        g.ring_hi = place("ring_hi", [P, RING, CW], F32R, g.ring_at)
        g.ring_lo = place("ring_lo", [P, RING, CW], F32R, g.ring_at + RING * CW * 4)

        g.ident = tiny("ident", [P, P])
        g.ones = tiny("ones", [P, P])
        g.tg_x = tiny("tg_x", [P, 1])
        g.tg_f = tiny("tg_f", [P, 1])
        g.bih = tiny("bih", [P, 3 * DH])
        g.bhh = tiny("bhh", [P, 3 * DH])
        g.b_gate = tiny("b_gate", [P, 2 * DH])
        g.w_in = tiny("w_in", [P, DH])
        g.w_slot = tiny("w_slot", [P, DH])
        g.k_scale = tiny("k_scale", [P, DH])
        g.rw_raw = tiny("rw_raw", [P, DH, 8])
        g.rw_hi = tiny("rw_hi", [P, DH, 8], F32R)
        g.rw_lo = tiny("rw_lo", [P, DH, 8], F32R)
        g.mean_var = tiny("mean_var", [P, NT, 2])
        g.rstd_col = tiny("rstd_col", [P, NT])
        g.nx = tiny("nx", [P, NT])
        g.ny = tiny("ny", [P, NT])
        g.na = tiny("na", [P, NT])
        g.nb = tiny("nb", [P, NT])
        g.ni = tiny("ni", [P, NT], I32)
        g.c_ssq = tiny("c_ssq", [P, NT])
        g.c_rstd = tiny("c_rstd", [P, NT])
        g.mx = tiny("mx", [P, 2, 2])
        g.neg_max = tiny("neg_max", [P, 2])
        g.zsum = tiny("zsum", [P, 2])
        g.rz = tiny("rz", [P, 1])

        g.place, g.semaphores, g.tiny = place, semaphores, tiny
        prepare(nc, a, g)
        attention(nc, g)
        handover(nc, a, g)
        experts(nc, a, g)
        finish(nc, out, g)


def prepare(nc, a, g):
    place, semaphores, psum = g.place, g.semaphores, g.psum
    E_AT, ACC_AT, RACC_AT, RING_AT = g.e_at, g.acc_at, g.racc_at, g.ring_at
    ident, ones = g.ident, g.ones
    h_hi, h_lo, k_hi, k_lo, v_hi, v_lo = g.h_hi, g.h_lo, g.k_hi, g.k_lo, g.v_hi, g.v_lo
    mean_var, rstd_col, c_ssq, c_rstd, nx = g.mean_var, g.rstd_col, g.c_ssq, g.c_rstd, g.nx

    x_rows = place("x_rows", [P, NT, D], F32, ACC_AT)
    at = E_AT
    ctx_rows = place("ctx_rows", [P, MT, D], F32, at)
    at += MT * D * 4
    p_hi = place("p_hi", [P, DH, MPAD], F32R, at)
    at += g.k_size
    p_lo = place("p_lo", [P, DH, MPAD], F32R, at)
    at += g.k_size
    wv_hi = place("wv_hi", [P, DH, D], F32R, at)
    wv_lo = place("wv_lo", [P, DH, D], F32R, at + 2048)
    kq_hi = place("kq_hi", [P, DH, D], F32R, at + 4096)
    kq_lo = place("kq_lo", [P, DH, D], F32R, at + 6144)
    wih = place("wih_raw", [P, DH, 3 * D], F32, RING_AT)
    whh = place("whh_raw", [P, DH, 3 * D], F32, RING_AT + 6144)
    scaled = place("scaled", [P, 2, CW], F32, RING_AT + 12288)
    wq = place("wq_raw", [P, DH, D], F32, RACC_AT)
    wk = place("wk_raw", [P, DH, D], F32, RACC_AT + 2048)
    wv = place("wv_raw", [P, DH, D], F32, RACC_AT + 4096)
    diag = place("diag0", [P, TPC, P], F32, RACC_AT + 6144)
    ln_stats = place("ln_stats", [P, NT, 6], F32, RACC_AT + 6144)
    junk = place("junk0", [P, D], F32, g.rstd_at)

    (ld_ctx, ld_x, ld_w, ld_small, ld_gw, const0, const1, sq_done, c_norm, ln_done, p_zero, w_hi_done,
     w_lo_done, kq_in, job_pe, job_scaled, job_hi, job_done, dg_done, spread_pe, spread_done, fin) = semaphores(
        "ld_ctx", "ld_x", "ld_w", "ld_small", "ld_gw", "const0", "const1", "sq_done", "c_norm", "ln_done",
        "p_zero", "w_hi_done", "w_lo_done", "kq_in", "job_pe", "job_scaled", "job_hi", "job_done",
        "dg_done", "spread_pe", "spread_done", "fin0")

    jobs = [("ctx", m, dh) for m in range(NC) for dh in range(DH)]
    jobs += [("kq", 0, ch) for ch in range(DH)]
    jobs += [("key", m, dh) for m in range(NC) for dh in range(DH)]
    jobs += [("value", t, 0) for t in range(MT)]
    jobs += [("slot", c, dh) for c in range(NC) for dh in range(DH)]

    def width(m, even=False):
        w = min(CW, M - m * CW)
        return w + (w % 2 if even else 0)

    def bank(n):
        return psum[n % 8 // 4][:, n % 4, :]

    def source(n):
        kind, m, dh = jobs[n]
        if kind == "value":
            return bank(n)[0:rows_of(m), 0:D]
        if kind == "kq":
            return bank(n)[:, 0:D]
        return bank(n)[:, 0:{"slot": CW, "ctx": width(m), "key": width(m, True)}[kind]]

    def target(n):
        kind, m, dh = jobs[n]
        if kind == "slot":
            return tuple(h[:, dh, m * CW:(m + 1) * CW] for h in (h_hi, h_lo))
        if kind == "ctx":
            return tuple(p[:, dh, m * CW:m * CW + width(m)] for p in (p_hi, p_lo))
        if kind == "kq":
            return kq_hi[:, dh, :], kq_lo[:, dh, :]
        if kind == "value":
            return v_hi[0:rows_of(m), m, :], v_lo[0:rows_of(m), m, :]
        return tuple(k[:, dh, m * CW:m * CW + width(m, True)] for k in (k_hi, k_lo))

    def scaled_jobs_to(n):
        return sum(jobs[i][0] in ("ctx", "key") for i in range(n))

    weights = [(wv, wv_hi, wv_lo), (wih, g.wih_hi, g.wih_lo), (whh, g.whh_hi, g.whh_lo)]

    with nc.Block() as block:
        @block.sync
        def _(sp):
            last = MT - 1
            for t0 in range(0, last, 4):
                sp.dma_start(ctx_rows[:, t0:t0 + 4, :], a["ctx"][t0 * P:(t0 + 4) * P, :].rearrange(
                    "(t p) d -> p t d", p=P)).then_inc(ld_ctx, 16)
            sp.dma_start(ctx_rows[0:rows_of(last), last, :], a["ctx"][last * P:M, :]).then_inc(ld_ctx, 16)
            for dst, name in ((wk, "wk"), (wq, "wq"), (wv, "wvT")):
                sp.dma_start(dst[:], a[name].rearrange("(h p) d -> p h d", p=P)).then_inc(ld_w, 16)
            for t0 in range(0, NT, 4):
                sp.dma_start(x_rows[:, t0:t0 + 4, :], a["x"][t0 * P:(t0 + 4) * P, :].rearrange(
                    "(t p) d -> p t d", p=P)).then_inc(ld_x, 16)
            for dst, name in ((wih, "wihT"), (whh, "whhT")):
                sp.dma_start(dst[:], a[name].rearrange("(h p) d -> p h d", p=P)).then_inc(ld_gw, 16)

        @block.gpsimd
        def _(pool):
            nc.gpsimd.memset(ident[:], 0.0).then_inc(const0, 1)
            nc.gpsimd.memset(ones[:], 1.0).then_inc(const1, 1)
            nc.gpsimd.memset(g.rw_raw[:], 0.0).then_inc(const1, 1)
            pool.wait_ge(const0, 1)
            nc.gpsimd.affine_select(out=ident[:], in_=ident[:], compare_op=ALU.not_equal, fill=1.0,
                                    base=0, pattern=[[-1, P]], channel_multiplier=1).then_inc(const1, 1)

        @block.scalar
        def _(act):
            for dst, name in ((g.w_in, "input_norm_w"), (g.w_slot, "slot_norm_w"), (g.bih, "bih"),
                              (g.bhh, "bhh"), (g.tg_x, "g_xattn"), (g.tg_f, "g_ffn")):
                act.dma_start(dst[:], a[name]).then_inc(ld_small, 16)
            act.wait_ge(const1, 3)
            act.dma_start(g.rw_raw[:, :, 0:ROUTED], a["routerT"].rearrange("(h p) e -> p h e", p=P)
                          ).then_inc(ld_small, 16)
            for t in range(MT):
                act.wait_ge(ld_ctx, 16 * 4)
                if t:
                    act.drain()
                r = rows_of(t)
                nc.scalar.activation(junk[0:r, :], ctx_rows[0:r, t, :], ACT.Square,
                                     accum_out=c_ssq[0:r, t:t + 1]).then_inc(sq_done, 1)
            act.wait_ge(ld_small, 16 * 7)
            act.drain()
            for t in (g.tg_x, g.tg_f):
                nc.scalar.activation(t[:], t[:], ACT.Tanh)
            nc.scalar.activation(g.rw_hi[:], g.rw_raw[:], ACT.Copy).then_inc(w_hi_done, 1)
            act.wait_ge(ld_w, 48)
            nc.scalar.activation(wv_hi[:], wv[:], ACT.Copy).then_inc(w_hi_done, 1)
            for n in range(len(jobs)):
                kind, m, dh = jobs[n]
                act.wait_ge(job_pe, n + 1)
                src = source(n)
                if kind in ("ctx", "key"):
                    k = scaled_jobs_to(n)
                    col = g.w_in if kind == "ctx" else g.k_scale
                    if kind == "key":
                        act.wait_ge(kq_in, 1)
                    if k >= 2:
                        act.wait_ge(job_done, [i for i in range(n) if jobs[i][0] in ("ctx", "key")][k - 2] + 1)
                    mid = scaled[:, k % 2, 0:src.shape[1]]
                    nc.scalar.activation(mid, src, ACT.Copy, scale=col[:, dh:dh + 1])
                    act.drain()
                    src = mid
                nc.scalar.activation(target(n)[0], src, ACT.Copy).then_inc(job_hi, 1)
                if n == 20:
                    act.wait_ge(ld_gw, 32)
                    nc.scalar.activation(g.wih_hi[:], wih[:], ACT.Copy).then_inc(w_hi_done, 1)
                    nc.scalar.activation(g.whh_hi[:], whh[:], ACT.Copy).then_inc(w_hi_done, 1)
            for c in range(NC):
                act.wait_ge(spread_pe, c + 1)
                nc.scalar.activation(g.rstd_all[:, c * CW:(c + 1) * CW], bank(len(jobs) + c), ACT.Copy
                                     ).then_inc(spread_done, 1)

        @block.vector
        def _(dve):
            for p in (p_hi, p_lo):
                nc.vector.memset(p[:, :, M:MPAD].bitcast(F32), 0.0).then_inc(p_zero, 1)
            dve.wait_ge(sq_done, MT)
            last = rows_of(MT - 1)
            dve.drain()
            nc.vector.memset(nx[:], 1.0)
            dve.drain()
            nc.vector.tensor_scalar(nx[:, 0:MT - 1], c_ssq[:, 0:MT - 1], 1.0 / D, EPS_NORM, ALU.mult, ALU.add)
            nc.vector.tensor_scalar(nx[0:last, MT - 1:MT], c_ssq[0:last, MT - 1:MT], 1.0 / D, EPS_NORM, ALU.mult, ALU.add)
            rsqrt(nc, dve, g, c_rstd[:, 0:MT], nx[:, 0:MT], MT)
            for t in range(MT):
                r = rows_of(t)
                nc.vector.tensor_scalar(ctx_rows[0:r, t, :], ctx_rows[0:r, t, :], c_rstd[0:r, t:t + 1], None,
                                        ALU.mult).then_inc(c_norm, 1)
            dve.wait_ge(ld_small, 16 * 7)
            nc.vector.tensor_scalar(g.k_scale[:], g.w_slot[:], SCALE, None, ALU.mult).then_inc(kq_in, 1)
            nc.vector.tensor_tensor(g.b_gate[:], g.bih[:, 0:2 * DH], g.bhh[:, 0:2 * DH], ALU.add)
            dve.drain()
            nc.vector.tensor_scalar(g.b_gate[:], g.b_gate[:], 0.5, None, ALU.mult)
            dve.wait_ge(w_hi_done, 1)
            nc.vector.tensor_tensor(g.rw_lo[:], g.rw_raw[:], g.rw_hi[:].bitcast(F32), ALU.subtract)
            dve.wait_ge(w_hi_done, 2)
            nc.vector.tensor_tensor(wv_lo[:], wv[:], wv_hi[:].bitcast(F32), ALU.subtract).then_inc(w_lo_done, 1)

            def low_part(n):
                kind = jobs[n][0]
                dve.wait_ge(job_hi, n + 1)
                hi, lo = target(n)
                src = source(n)
                if kind in ("ctx", "key"):
                    src = scaled[:, scaled_jobs_to(n) % 2, 0:src.shape[1]]
                nc.vector.tensor_tensor(lo, src, hi.bitcast(F32), ALU.subtract).then_inc(job_done, 1)

            first_slot = len(jobs) - NC * DH
            for n in range(8):
                low_part(n)
            dve.wait_ge(ld_x, 16 * 4)
            for t in range(NT):
                nc.vector.bn_stats(ln_stats[:, t, :], x_rows[:, t, :])
            dve.drain()
            for t in range(NT):
                nc.vector.bn_aggr(mean_var[:, t, :], ln_stats[:, t, :])
            dve.drain()
            nc.vector.tensor_scalar(nx[:], mean_var[:, :, 1], EPS_LN, None, ALU.add)
            rsqrt(nc, dve, g, rstd_col[:], nx[:], NT)
            for t in range(NT):
                ins = nc.vector.tensor_scalar(x_rows[:, t, :], x_rows[:, t, :], mean_var[:, t, 0:1],
                                              rstd_col[:, t:t + 1], ALU.subtract, ALU.mult)
                if t % TPC == TPC - 1:
                    ins.then_inc(ln_done, 1)
            nc.vector.tensor_tensor(c_ssq[:], rstd_col[:], rstd_col[:], ALU.mult)
            dve.drain()
            nc.vector.tensor_tensor(c_ssq[:], c_ssq[:], mean_var[:, :, 1], ALU.mult)
            dve.drain()
            nc.vector.tensor_scalar(nx[:], c_ssq[:], EPS_NORM, None, ALU.add)
            rsqrt(nc, dve, g, rstd_col[:], nx[:], NT)
            for n in range(8, len(jobs)):
                low_part(n)
                if n == 21:
                    dve.wait_ge(w_hi_done, 4)
                    nc.vector.tensor_tensor(g.wih_lo[:], wih[:], g.wih_hi[:].bitcast(F32), ALU.subtract)
                    nc.vector.tensor_tensor(g.whh_lo[:], whh[:], g.whh_hi[:].bitcast(F32), ALU.subtract)
            for c in range(NC):
                if c:
                    dve.wait_ge(spread_pe, c)
                diagonal(nc, g, diag[:], rstd_col[:, c * TPC:(c + 1) * TPC], TPC).then_inc(dg_done, 1)
            dve.drain()

        @block.tensor
        def _(pe):
            pe.wait_ge(const1, 3)
            for n, (kind, m, dh) in enumerate(jobs):
                b = bank(n)
                if n >= 8:
                    pe.wait_ge(job_done, n - 7)
                if kind == "ctx":
                    tiles = range(m * TPC, min((m + 1) * TPC, MT))
                    pe.wait_ge(c_norm, tiles[-1] + 1)
                    for i, t in enumerate(tiles):
                        r = rows_of(t)
                        ins = nc.tensor.transpose(b[:, i * P:i * P + r], ctx_rows[0:r, t, dh * P:(dh + 1) * P],
                                                  ident[0:r, 0:r])
                elif kind == "slot":
                    pe.wait_ge(ln_done, m + 1)
                    for i in range(TPC):
                        ins = nc.tensor.transpose(b[:, i * P:(i + 1) * P],
                                                  x_rows[:, m * TPC + i, dh * P:(dh + 1) * P], ident[:])
                elif kind == "kq":
                    pe.wait_ge(ld_w, 48)
                    for e in range(DH):
                        ins = nc.tensor.matmul(b[:, 0:D], wk[:, e, dh * P:(dh + 1) * P], wq[:, e, :],
                                               start=(e == 0), stop=(e == DH - 1))
                elif kind == "key":
                    pe.wait_ge(job_done, NC * DH + DH)
                    pe.wait_ge(p_zero, 2)
                    w = width(m, True)
                    for e in range(DH):
                        ins = split3(nc, b[:, 0:w], kq_hi[:, e, dh * P:(dh + 1) * P], kq_lo[:, e, dh * P:(dh + 1) * P],
                                     p_hi[:, e, m * CW:m * CW + w], p_lo[:, e, m * CW:m * CW + w],
                                     e == 0, e == DH - 1)
                else:
                    pe.wait_ge(w_lo_done, 1)
                    r = rows_of(m)
                    for e in range(DH):
                        ins = split3(nc, b[0:r, 0:D], p_hi[:, e, m * P:m * P + r], p_lo[:, e, m * P:m * P + r],
                                     wv_hi[:, e, :], wv_lo[:, e, :], e == 0, e == DH - 1)
                ins.then_inc(job_pe, 1)
            for c in range(NC):
                pe.wait_ge(job_done, len(jobs) + c - 7)
                pe.wait_ge(dg_done, c + 1)
                nc.tensor.matmul(bank(len(jobs) + c), ones[:], diag[:].rearrange("p a b -> p (a b)"),
                                 start=True, stop=True).then_inc(spread_pe, 1)


def attention(nc, g):
    place = g.place
    h_hi, h_lo, acc, rstd_all, k_hi, k_lo, v_hi, v_lo, E, racc, ring_hi, ring_lo = (
        g.h_hi, g.h_lo, g.acc, g.rstd_all, g.k_hi, g.k_lo, g.v_hi, g.v_lo, g.E, g.racc, g.ring_hi, g.ring_lo)
    scores, sums = g.psum
    mx, neg_max, zsum, rz, ones = g.mx, g.neg_max, g.zsum, g.rz, g.ones
    slot = lambda s: g.e_at + s * S * 4
    u_hi = place("u_hi", [P, 2, DH, CW], F32R, slot(2))
    u_lo = place("u_lo", [P, 2, DH, CW], F32R, slot(3))
    r_diag = place("r_diag", [P, NC, TPC, P], F32, slot(4))
    sq = place("sq", [P, DH, CW], F32, slot(4))
    h_new = place("h_new", [P, 2, DH, CW], F32, slot(5))
    n_diag = place("n_diag", [P, TPC, P], F32, slot(4) + 4096)
    t_r = place("t_r", [P, 2, CW], F32, slot(0))
    t_z = place("t_z", [P, 2, CW], F32, slot(0) + 4096)
    n_in = place("n_in", [P, 2, CW], F32, slot(1))
    n_out = place("n_out", [P, 2, CW], F32, slot(1) + 4096)
    diff = place("diff", [P, 2, CW], F32, g.ring_at)
    rsum = g.c_ssq
    rinv = g.c_rstd

    (score_pe, drained, nmax, exped, scaled, rsummed, hi_done, lo_done, pair_pe, item_done, rs_pe, rdiag_done,
     rspread_pe, rinv_done, u_done, u_hi_done, u_lo_done, hn_pe, r_pe, z_pe, xn_pe, tr_done, tz_done, n_in_done,
     n_done, diff_done, h_done, h_hi_done, h_lo_done, sq_done, ss_pe, ndiag_done, nspread_pe, rstd_done, seen
     ) = g.semaphores(
        "score_pe", "drained", "nmax", "exped", "scaled_e", "rsummed", "hi_done", "lo_done", "pair_pe", "item_done",
        "rs_pe", "rdiag_done", "rspread_pe", "rinv_done", "u_done", "u_hi_done", "u_lo_done", "hn_pe", "r_pe",
        "z_pe", "xn_pe", "tr_done", "tz_done", "n_in_done", "n_done", "diff_done", "h_done", "h_hi_done",
        "h_lo_done", "sq_done1", "ss_pe", "ndiag_done", "nspread_pe", "rstd_done", "seen")
    GRU = NC * DH

    def chunk(c):
        return slice(c * CW, (c + 1) * CW)

    def pairs_until(item):
        return PAIRS_OF[item][-1] + 1

    def last_use(t):
        return max(n for n, (_, k) in enumerate(PAIRS) if k == t) + 1

    def early(t):
        return [n for i in AFTER.get(t, []) for n in PAIRS_OF[i]][:RING - 1]

    def late(t):
        return [n for i in AFTER.get(t, []) for n in PAIRS_OF[i]][RING - 1:]

    def before_in_slot(t):
        return max((k for k in range(t) if E_SLOT[k] == E_SLOT[t]), default=None)

    with nc.Block() as block:
        @block.tensor
        def _(pe):
            def item(i, it):
                b, c = ITEMS[i]
                if i >= 2:
                    pe.wait_ge(item_done, it * NITEM + i - 1)
                for n in PAIRS_OF[i]:
                    t = PAIRS[n][1]
                    r = rows_of(t)
                    pe.wait_ge(hi_done, it * NPAIR + n + 1)
                    pe.wait_ge(lo_done, it * NPAIR + n + 1)
                    for dh in range(DH):
                        ins = split3(nc, sums[:, 2 * (i % 2) + dh, :], v_hi[0:r, t, dh * P:(dh + 1) * P],
                                     v_lo[0:r, t, dh * P:(dh + 1) * P], ring_hi[0:r, n % RING, :],
                                     ring_lo[0:r, n % RING, :], n == PAIRS_OF[i][0], n == PAIRS_OF[i][-1])
                    ins.then_inc(pair_pe, 1)

            def spread_rinv(c, it):
                pe.wait_ge(rdiag_done, it * NC + c + 1)
                if c == 0:
                    pass
                nc.tensor.matmul(scores[:, (c + 1) % 4, :], ones[:], r_diag[:, c].rearrange("p a b -> p (a b)"),
                                 start=True, stop=True).then_inc(rspread_pe, 1)

            def gates(q, it):
                c, j = q // DH, q % DH
                m_h = [(h_hi[:, e, chunk(c)], h_lo[:, e, chunk(c)]) for e in range(DH)]
                m_u = [(u_hi[:, c % 2, e, :], u_lo[:, c % 2, e, :]) for e in range(DH)]

                def product(bank, gate, w_hi, w_lo, moving, start, stop):
                    at = gate * D + j * P
                    for e in range(DH):
                        ins = split3(nc, scores[:, bank, :], w_hi[:, e, at:at + P], w_lo[:, e, at:at + P],
                                     *moving[e], start and e == 0, stop and e == DH - 1)
                    return ins

                if q == 0:
                    pe.wait_ge(rinv_done, it * NC + 4)
                else:
                    pe.wait_ge(n_in_done, it * GRU + q)
                product(0, 2, g.whh_hi, g.whh_lo, m_h, True, True).then_inc(hn_pe, 1)
                if q:
                    pe.wait_ge(tr_done, it * GRU + q)
                product(1, 0, g.whh_hi, g.whh_lo, m_h, True, False)
                if j == 0:
                    pe.wait_ge(u_hi_done, it * NC + c + 1)
                    pe.wait_ge(u_lo_done, it * NC + c + 1)
                product(1, 0, g.wih_hi, g.wih_lo, m_u, False, True).then_inc(r_pe, 1)
                if q:
                    pe.wait_ge(tz_done, it * GRU + q)
                product(2, 1, g.whh_hi, g.whh_lo, m_h, True, False)
                product(2, 1, g.wih_hi, g.wih_lo, m_u, False, True).then_inc(z_pe, 1)
                product(3, 2, g.wih_hi, g.wih_lo, m_u, True, True).then_inc(xn_pe, 1)

            def square_sums(c, it):
                pe.wait_ge(sq_done, it * NC + c + 1)
                for i in range(TPC):
                    for e in range(DH):
                        ins = nc.tensor.matmul(sums[:, 0, c * TPC + i:c * TPC + i + 1], sq[:, e, i * P:(i + 1) * P],
                                               ones[:, 0:1], start=(e == 0), stop=(e == DH - 1))
                ins.then_inc(ss_pe, 1)

            def spread_rstd(c, it):
                pe.wait_ge(ndiag_done, it * NC + c + 1)
                nc.tensor.matmul(sums[:, 2 + c % 2, :], ones[:], n_diag[:].rearrange("p a b -> p (a b)"),
                                 start=True, stop=True).then_inc(nspread_pe, 1)

            with pe.Fori(0, ITERS) as it:
                for t in range(MT):
                    r = rows_of(t)
                    for c in range(NC):
                        if t == 0:
                            pe.wait_ge(h_hi_done, it * NC + c + 1)
                            pe.wait_ge(h_lo_done, it * NC + c + 1)
                        elif c % 2 == 0:
                            pe.wait_ge(drained, it * 2 * MT + 2 * (t - 1) + c // 2 + 1)
                        for e in range(DH):
                            ks = slice(t * P, t * P + r)
                            ins = split3(nc, scores[0:r, c, :], k_hi[:, e, ks], k_lo[:, e, ks],
                                         h_hi[:, e, chunk(c)], h_lo[:, e, chunk(c)], e == 0, e == DH - 1)
                        if c % 2:
                            ins.then_inc(score_pe, 1)
                    for i in AFTER.get(t, []):
                        item(i, it)
                item(TAIL[0], it)
                item(TAIL[1], it)
                pe.wait_ge(rsummed, it * (MT - 1) + MT - 1)
                pe.wait_ge(drained, it * 2 * MT + 2 * MT)
                for i in range(NT):
                    ins = nc.tensor.matmul(scores[:, 0, i:i + 1], racc[:, i * P:(i + 1) * P], ones[:, 0:1],
                                           start=True, stop=True)
                ins.then_inc(rs_pe, 1)
                item(TAIL[2], it)
                spread_rinv(0, it)
                spread_rinv(1, it)
                item(TAIL[3], it)
                spread_rinv(2, it)
                spread_rinv(3, it)
                for q in range(GRU):
                    gates(q, it)
                    c = q // DH - 1
                    if c >= 0 and q % DH == 0:
                        square_sums(c, it)
                    if c >= 0 and q % DH == 1:
                        spread_rstd(c, it)
                square_sums(NC - 1, it)
                spread_rstd(NC - 1, it)

        @block.scalar
        def _(act):
            def high_part(n, it):
                i, t = PAIRS[n]
                r, c = rows_of(t), ITEMS[i][1]
                act.wait_ge(scaled, it * MT + t + 1)
                if n >= RING:
                    act.wait_ge(pair_pe, it * NPAIR + n - RING + 1)
                nc.scalar.activation(ring_hi[0:r, n % RING, :], E[0:r, E_SLOT[t], chunk(c)], ACT.Copy
                                     ).then_inc(hi_done, 1)

            def u_high(c, it):
                act.wait_ge(u_done, it * NC + c + 1)
                if c >= 2:
                    act.wait_ge(xn_pe, it * GRU + DH * (c - 1))
                nc.scalar.activation(u_hi[:, c % 2], acc[:, :, chunk(c)], ACT.Copy).then_inc(u_hi_done, 1)

            def new_slots(c, it):
                act.wait_ge(h_done, it * GRU + DH * (c + 1))
                nc.scalar.activation(h_hi[:, :, chunk(c)], h_new[:, c % 2], ACT.Copy).then_inc(h_hi_done, 1)
                if c:
                    act.wait_ge(ss_pe, it * NC + c)
                nc.scalar.activation(sq[:], h_new[:, c % 2], ACT.Square).then_inc(sq_done, 1)

            def rstd_copy(c, it):
                act.wait_ge(nspread_pe, it * NC + c + 1)
                nc.scalar.activation(rstd_all[:, chunk(c)], sums[:, 2 + c % 2, :], ACT.Copy).then_inc(rstd_done, 1)

            act.sem_inc(h_hi_done, NC)
            act.sem_inc(rstd_done, NC)
            with act.Fori(0, ITERS) as it:
                for t in range(MT):
                    r = rows_of(t)
                    for n in early(t):
                        high_part(n, it)
                    act.wait_ge(nmax, it * MT + t + 1)
                    nc.scalar.activation(E[0:r, E_SLOT[t], :], E[0:r, E_SLOT[t], :], ACT.Exp,
                                         bias=neg_max[0:r, t % 2:t % 2 + 1],
                                         accum_out=zsum[0:r, t % 2:t % 2 + 1]).then_inc(exped, 1)
                    for n in late(t):
                        high_part(n, it)
                for i in TAIL:
                    for n in PAIRS_OF[i]:
                        high_part(n, it)
                for c in range(NC):
                    act.wait_ge(rspread_pe, it * NC + c + 1)
                    nc.scalar.activation(racc[:, chunk(c)], scores[:, (c + 1) % 4, :], ACT.Copy).then_inc(rinv_done, 1)
                u_high(0, it)
                for q in range(GRU):
                    c, j = q // DH, q % DH
                    p = q % 2
                    if q >= 2:
                        act.wait_ge(n_in_done, it * GRU + q - 1)
                    act.wait_ge(r_pe, it * GRU + q + 1)
                    nc.scalar.activation(t_r[:, p], scores[:, 1, :], ACT.Tanh, bias=g.b_gate[:, j:j + 1],
                                         scale=0.5).then_inc(tr_done, 1)
                    if q >= 2:
                        act.wait_ge(h_done, it * GRU + q - 1)
                    act.wait_ge(z_pe, it * GRU + q + 1)
                    nc.scalar.activation(t_z[:, p], scores[:, 2, :], ACT.Tanh, bias=g.b_gate[:, DH + j:DH + j + 1],
                                         scale=0.5).then_inc(tz_done, 1)
                    if c and j == 0:
                        new_slots(c - 1, it)
                    act.wait_ge(n_in_done, it * GRU + q + 1)
                    nc.scalar.activation(n_out[:, p], n_in[:, p], ACT.Tanh, bias=g.bih[:, 2 * DH + j:2 * DH + j + 1]
                                         ).then_inc(n_done, 1)
                    if c and j == 1:
                        rstd_copy(c - 1, it)
                    if j == 0 and c + 1 < NC:
                        u_high(c + 1, it)
                new_slots(NC - 1, it)
                rstd_copy(NC - 1, it)

        @block.vector
        def _(dve):
            def low_part(n, it):
                i, t = PAIRS[n]
                r, c = rows_of(t), ITEMS[i][1]
                dve.wait_ge(hi_done, it * NPAIR + n + 1)
                nc.vector.tensor_tensor(ring_lo[0:r, n % RING, :], E[0:r, E_SLOT[t], chunk(c)],
                                        ring_hi[0:r, n % RING, :].bitcast(F32), ALU.subtract).then_inc(lo_done, 1)

            def add_sums(i, it):
                b, c = ITEMS[i]
                dve.wait_ge(pair_pe, it * NPAIR + pairs_until(i))
                src = sums[:, 2 * (i % 2):2 * (i % 2) + DH, :]
                dst = acc[:, :, chunk(c)]
                if b == 0:
                    nc.vector.tensor_copy(dst, src).then_inc(item_done, 1)
                else:
                    nc.vector.tensor_tensor(dst, src, dst, ALU.add).then_inc(item_done, 1)

            def u_sums(c, it):
                dve.wait_ge(rinv_done, it * NC + c + 1)
                nc.vector.tensor_tensor(acc[:, :, chunk(c)], acc[:, :, chunk(c)],
                                        racc[:, chunk(c)].unsqueeze(1).broadcast_to([P, DH, CW]), ALU.mult
                                        ).then_inc(u_done, 1)

            def low_slots(c, it):
                dve.wait_ge(h_hi_done, it * NC + NC + c + 1)
                nc.vector.tensor_tensor(h_lo[:, :, chunk(c)], h_new[:, c % 2], h_hi[:, :, chunk(c)].bitcast(F32),
                                        ALU.subtract).then_inc(h_lo_done, 1)

            def rstd(c, it):
                dve.wait_ge(ss_pe, it * NC + c + 1)
                if c:
                    dve.wait_ge(nspread_pe, it * NC + c)
                nc.vector.tensor_scalar(g.nx[:, 0:TPC], sums[:, 0, c * TPC:(c + 1) * TPC], 1.0 / D, EPS_NORM,
                                        ALU.mult, ALU.add)
                rsqrt(nc, dve, g, g.ny[:, 0:TPC], g.nx[:, 0:TPC], TPC)
                diagonal(nc, g, n_diag[:], g.ny[:, 0:TPC], TPC).then_inc(ndiag_done, 1)

            dve.sem_inc(h_lo_done, NC)
            with dve.Fori(0, ITERS) as it:
                for t in range(MT):
                    r, s, p = rows_of(t), E_SLOT[t], t % 2
                    dve.drain()
                    for n in early(t):
                        low_part(n, it)
                    if t == 0:
                        dve.wait_ge(rstd_done, it * NC + NC)
                    if before_in_slot(t) is not None:
                        k = before_in_slot(t)
                        dve.wait_ge(hi_done, it * NPAIR + last_use(k))
                        dve.wait_ge(rsummed, it * (MT - 1) + max(k, 1))
                    for i in range(2):
                        dve.wait_ge(score_pe, it * 2 * MT + 2 * t + i + 1)
                        dve.sem_inc(seen, 1)
                        half = slice(i * 2 * CW, (i + 1) * 2 * CW)
                        nc.vector.tensor_tensor_reduce(
                            out=E[0:r, s, half], in0=scores[0:r, 2 * i:2 * i + 2, :].rearrange("p a b -> p (a b)"),
                            in1=rstd_all[0:r, half], scale=1.0, scalar=-3e38, op0=ALU.mult, op1=ALU.max,
                            accum_out=mx[0:r, p, i:i + 1]).then_inc(drained, 1)
                    dve.drain()
                    nc.vector.tensor_scalar(neg_max[0:r, p:p + 1], mx[0:r, p, 0:1], mx[0:r, p, 1:2], -1.0,
                                            ALU.max, ALU.mult).then_inc(nmax, 1)
                    for n in late(t):
                        low_part(n, it)
                    dve.wait_ge(exped, it * MT + t + 1)
                    nc.vector.reciprocal(rz[0:r, :], zsum[0:r, p:p + 1])
                    dve.drain()
                    nc.vector.tensor_scalar(E[0:r, s, :], E[0:r, s, :], rz[0:r, :], None, ALU.mult
                                            ).then_inc(scaled, 1)
                    for i in AFTER.get(t, []):
                        add_sums(i, it)
                dve.drain()
                for i in TAIL[0:3]:
                    for n in PAIRS_OF[i]:
                        low_part(n, it)
                    if i == TAIL[1]:
                        add_sums(TAIL[0], it)
                dve.wait_ge(rs_pe, it + 1)
                nc.vector.tensor_scalar(rsum[:], scores[:, 0, 0:NT], EPS_ATTN, None, ALU.add)
                dve.drain()
                nc.vector.reciprocal(rinv[:], rsum[:])
                dve.drain()
                for c in range(NC):
                    diagonal(nc, g, r_diag[:, c], rinv[:, c * TPC:(c + 1) * TPC], TPC).then_inc(rdiag_done, 1)
                add_sums(TAIL[1], it)
                for n in PAIRS_OF[TAIL[3]]:
                    low_part(n, it)
                add_sums(TAIL[2], it)
                add_sums(TAIL[3], it)
                dve.drain()
                u_sums(0, it)
                for q in range(GRU):
                    c, j, p = q // DH, q % DH, q % 2
                    if c and j == 1:
                        rstd(c - 1, it)
                    b_hn = g.bhh[:, 2 * DH + j:2 * DH + j + 1]
                    dve.wait_ge(hn_pe, it * GRU + q + 1)
                    dve.wait_ge(tr_done, it * GRU + q + 1)
                    if q >= 2:
                        dve.wait_ge(n_done, it * GRU + q - 1)
                    nc.vector.scalar_tensor_tensor(n_in[:, p], scores[:, 0, :], b_hn, t_r[:, p], ALU.add, ALU.mult)
                    dve.drain()
                    nc.vector.scalar_tensor_tensor(n_in[:, p], scores[:, 0, :], b_hn, n_in[:, p], ALU.add, ALU.add)
                    dve.drain()
                    dve.wait_ge(xn_pe, it * GRU + q + 1)
                    nc.vector.scalar_tensor_tensor(n_in[:, p], n_in[:, p], 0.5, scores[:, 3, :], ALU.mult, ALU.add
                                                   ).then_inc(n_in_done, 1)
                    if c and j == 0:
                        low_slots(c - 1, it)
                    if j == 0 and c + 1 < NC:
                        u_sums(c + 1, it)
                    dve.wait_ge(diff_done, it * GRU + q + 1)
                    dve.wait_ge(tz_done, it * GRU + q + 1)
                    nc.vector.scalar_tensor_tensor(diff[:, p], t_z[:, p], 1.0, diff[:, p], ALU.add, ALU.mult)
                    dve.drain()
                    if c >= 2 and j == 0:
                        dve.wait_ge(sq_done, it * NC + c - 1)
                    nc.vector.scalar_tensor_tensor(h_new[:, c % 2, j], diff[:, p], 0.5, n_out[:, p],
                                                   ALU.mult, ALU.add).then_inc(h_done, 1)
                low_slots(NC - 1, it)
                rstd(NC - 1, it)

        @block.gpsimd
        def _(pool):
            def u_low(c, it):
                pool.wait_ge(u_hi_done, it * NC + c + 1)
                for e in range(DH):
                    ins = nc.gpsimd.tensor_tensor(u_lo[:, c % 2, e, :], acc[:, e, chunk(c)],
                                                  u_hi[:, c % 2, e, :].bitcast(F32), ALU.subtract)
                ins.then_inc(u_lo_done, 1)

            with pool.Fori(0, ITERS) as it:
                for t in range(1, MT):
                    r = rows_of(t)
                    pool.wait_ge(scaled, it * MT + t + 1)
                    first = E[0:r, E_SLOT[0], :] if t == 1 else racc[0:r, :]
                    nc.gpsimd.tensor_tensor(racc[0:r, :], first, E[0:r, E_SLOT[t], :], ALU.add).then_inc(rsummed, 1)
                    pool.drain()
                u_low(0, it)
                for q in range(GRU):
                    c, j, p = q // DH, q % DH, q % 2
                    pool.wait_ge(n_done, it * GRU + q + 1)
                    if q >= 2:
                        pool.wait_ge(h_done, it * GRU + q - 1)
                    nc.gpsimd.tensor_tensor(diff[:, p], h_hi[:, j, chunk(c)].bitcast(F32), n_out[:, p], ALU.subtract)
                    pool.drain()
                    nc.gpsimd.tensor_tensor(diff[:, p], diff[:, p], h_lo[:, j, chunk(c)].bitcast(F32), ALU.add
                                            ).then_inc(diff_done, 1)
                    if j == 0 and c + 1 < NC:
                        u_low(c + 1, it)


def weight_piece(nc, a, eng, step, g, w, expert, piece, count, base):
    cols = slice(piece * PIECE, (piece + 1) * PIECE)
    k, raw = count % 2, g.w_raw[:, count % 2, :]
    if step == "load":
        if not (isinstance(base, int) and base == 0 and count < 2):
            eng.wait_ge(g.w_lo_done, base + count - 1)
        eng.dma_start(raw, a["w"][expert, :, cols]).then_inc(g.w_loaded[k], 16)
    elif step == "high":
        eng.wait_ge(g.w_loaded[k], (base + count - k) * 8 + 16)
        nc.scalar.activation(g.w_hi[w][:, cols], raw, ACT.Copy).then_inc(g.w_hi_done, 1)
    else:
        eng.wait_ge(g.w_hi_done, base + count + 1)
        nc.vector.tensor_tensor(g.w_lo[w][:, cols], raw, g.w_hi[w][:, cols].bitcast(F32), ALU.subtract
                                ).then_inc(g.w_lo_done, 1)


def handover(nc, a, g):
    place = g.place
    g.x1 = place("x1", [P, NT, D], F32, g.acc_at)
    at = g.rstd_at
    g.xn_hi = place("xn_hi", [P, DH, S], F32R, at)
    g.xn_lo = place("xn_lo", [P, DH, S], F32R, at + 16384)
    at += 32768
    g.w_hi, g.w_lo = [], []
    for w in range(2):
        g.w_hi.append(place(f"w_hi{w}", [P, WCOLS], F32R, at))
        g.w_lo.append(place(f"w_lo{w}", [P, WCOLS], F32R, at + WCOLS * 4))
        at += 2 * WCOLS * 4
    g.w_raw = place("w_raw", [P, 2, PIECE], F32, at)
    g.tmp_at = at = at + 2 * PIECE * 4
    h32 = place("h32", [P, 2, DH, CW], F32, at)
    x_in = place("x_in", [P, 2, TPC, D], F32, at + 8192)
    xn = place("xn", [P, TPC, D], F32, at + 16384)
    g.facc = place("facc", [P, DH, S], F32, g.h_at)
    g.combine = place("combine", [P, 2, S], F32, g.h_at + DH * S * 4)
    tiny = g.tiny
    stats = tiny("stats", [P, TPC, 6])
    probs = tiny("probs", [P, NT, 8])
    best = tiny("best", [P, NT, 8])
    best_at = tiny("best_at", [P, NT, 8], U32)
    where = tiny("where", [P, NT, 2])
    chosen = place("chosen", [P, NT, 8], F32, at + 20480)
    comb = place("comb", [P, NT, 8], F32, at + 20992)
    numbers = tiny("numbers", [P, 8])
    row = g.c_ssq
    comb_rows = place("comb_rows", [8, S], F32, g.tmp_at)
    g.comb_dram = nc.dram_tensor("comb_dram", (EXPERTS, S), F32).ap()
    g.w_loaded = g.semaphores("w_loaded0", "w_loaded1")
    g.w_hi_done, g.w_lo_done = g.semaphores("w_hi_done1", "w_lo_done1")
    ld_x = g.semaphores("ld_x_even", "ld_x_odd")
    (h_sum, rows_pe, x1_done, norm_done, cols_pe, hi_done, lo_done, logit_pe, logit_done, max_done, exp_done,
     comb_done, combt_pe, combt_done, combt_out, iota_done) = g.semaphores(
        "h_sum", "rows_pe", "x1_done", "norm_done", "cols_pe", "hi_done1", "lo_done1", "logit_pe",
        "logit_done", "max_done", "exp_done", "comb_done", "combt_pe", "combt_done", "combt_out", "iota_done")
    low, high = g.psum
    flat = lambda x: x.rearrange("p a b -> p (a b)")

    with nc.Block() as block:
        @block.sync
        def _(sp):
            for c in range(NC):
                if c >= 2:
                    sp.wait_ge(x1_done, c - 1)
                sp.dma_start(x_in[:, c % 2], a["x"][c * CW:(c + 1) * CW, :].rearrange("(t p) d -> p t d", p=P)
                             ).then_inc(ld_x[c % 2], 16)
                for i in range(2):
                    weight_piece(nc, a, sp, "load", g, 0, 0, 2 * c + i, 2 * c + i, 0)
            sp.wait_ge(combt_done, 2)
            sp.dma_start(g.comb_dram, comb_rows[:]).then_inc(combt_out, 16)
            sp.wait_ge(combt_out, 16)

        @block.gpsimd
        def _(pool):
            for e in range(8):
                ins = nc.gpsimd.memset(numbers[:, e:e + 1], float(e))
            ins.then_inc(iota_done, 1)

        @block.scalar
        def _(act):
            for c in range(NC):
                act.wait_ge(cols_pe, c + 1)
                nc.scalar.activation(g.xn_hi[:, :, c * CW:(c + 1) * CW], high[:, 0:DH, :], ACT.Copy).then_inc(hi_done, 1)
                for i in range(2):
                    weight_piece(nc, a, act, "high", g, 0, 0, 2 * c + i, 2 * c + i, 0)
            act.wait_ge(max_done, 1)
            nc.scalar.activation(flat(probs[:, :, 0:8]), flat(probs[:, :, 0:8]), ACT.Exp).then_inc(exp_done, 1)

        @block.vector
        def _(dve):
            def slots(c):
                if c >= 2:
                    dve.wait_ge(rows_pe, c - 1)
                cs = slice(c * CW, (c + 1) * CW)
                nc.vector.tensor_tensor(h32[:, c % 2], g.h_hi[:, :, cs].bitcast(F32), g.h_lo[:, :, cs].bitcast(F32),
                                        ALU.add).then_inc(h_sum, 1)

            slots(0)
            for c in range(NC):
                cs = slice(c * CW, (c + 1) * CW)
                if c + 1 < NC:
                    slots(c + 1)
                dve.wait_ge(ld_x[c % 2], 16 * (c // 2 + 1))
                dve.wait_ge(rows_pe, c + 1)
                x1 = g.x1[:, c * TPC:(c + 1) * TPC, :]
                nc.vector.scalar_tensor_tensor(flat(x1), flat(low[:, 2 * (c % 2):2 * (c % 2) + 2, :]), g.tg_x[:],
                                               flat(x_in[:, c % 2]), ALU.mult, ALU.add).then_inc(x1_done, 1)
                dve.drain()
                for i in range(TPC):
                    nc.vector.bn_stats(stats[:, i, :], x1[:, i, :])
                dve.drain()
                mv = g.mean_var[:, c * TPC:(c + 1) * TPC, :]
                for i in range(TPC):
                    nc.vector.bn_aggr(mv[:, i, :], stats[:, i, :])
                dve.drain()
                nc.vector.tensor_scalar(g.nx[:, 0:TPC], mv[:, :, 1], EPS_LN, None, ALU.add)
                rsqrt(nc, dve, g, g.ny[:, 0:TPC], g.nx[:, 0:TPC], TPC)
                if c:
                    dve.wait_ge(cols_pe, c)
                for i in range(TPC):
                    ins = nc.vector.tensor_scalar(xn[:, i, :], x1[:, i, :], mv[:, i, 0:1], g.ny[:, i:i + 1],
                                                  ALU.subtract, ALU.mult)
                ins.then_inc(norm_done, 1)
                for i in range(2):
                    weight_piece(nc, a, dve, "low", g, 0, 0, 2 * c + i, 2 * c + i, 0)
                dve.wait_ge(hi_done, c + 1)
                nc.vector.tensor_tensor(g.xn_lo[:, :, cs], high[:, 0:DH, :], g.xn_hi[:, :, cs].bitcast(F32),
                                        ALU.subtract).then_inc(lo_done, 1)
            dve.wait_ge(logit_pe, NT)
            logits = high[:, 2, 0:NT * 8].rearrange("p (t e) -> p t e", e=8)
            valid = probs[:, :, 0:ROUTED]
            nc.vector.memset(probs[:], 0.0)
            nc.vector.reduce_max(row[:], logits[:, :, 0:ROUTED], AX.X)
            dve.drain()
            nc.vector.tensor_tensor(valid, logits[:, :, 0:ROUTED], row[:].unsqueeze(2).broadcast_to([P, NT, ROUTED]),
                                    ALU.subtract).then_inc(max_done, 1)
            dve.wait_ge(exp_done, 1)
            nc.vector.reduce_sum(row[:], valid, AX.X)
            dve.drain()
            nc.vector.reciprocal(g.ny[:], row[:])
            dve.drain()
            nc.vector.tensor_tensor(valid, valid, g.ny[:].unsqueeze(2).broadcast_to([P, NT, ROUTED]), ALU.mult)
            nc.vector.memset(probs[:, :, ROUTED:8], -1.0)
            dve.drain()
            for t in range(NT):
                nc.vector.max(best[:, t, :], probs[:, t, :])
            dve.drain()
            for t in range(NT):
                nc.vector.max_index(best_at[:, t, :], best[:, t, :], probs[:, t, :])
            nc.vector.tensor_tensor(row[:], best[:, :, 0], best[:, :, 1], ALU.add)
            dve.drain()
            nc.vector.tensor_copy(where[:], best_at[:, :, 0:2])
            nc.vector.tensor_scalar(row[:], row[:], EPS_TOP, 2.0, ALU.add, ALU.mult)
            dve.drain()
            nc.vector.reciprocal(g.ny[:], row[:])
            dve.drain()
            nc.vector.tensor_tensor(best[:, :, 0:2], best[:, :, 0:2], g.ny[:].unsqueeze(2).broadcast_to([P, NT, 2]),
                                    ALU.mult)
            nc.vector.memset(comb[:, :, 0:1], 0.5)
            dve.wait_ge(iota_done, 1)
            routed = comb[:, :, 1:8]
            for k in range(2):
                dst = routed if k == 0 else chosen[:, :, 0:ROUTED]
                nc.vector.tensor_tensor(dst, numbers[:, 0:ROUTED].unsqueeze(1).broadcast_to([P, NT, ROUTED]),
                                        where[:, :, k:k + 1].broadcast_to([P, NT, ROUTED]), ALU.is_equal)
                dve.drain()
                nc.vector.tensor_tensor(dst, dst, best[:, :, k:k + 1].broadcast_to([P, NT, ROUTED]), ALU.mult)
                dve.drain()
            nc.vector.tensor_tensor(routed, routed, chosen[:, :, 0:ROUTED], ALU.add).then_inc(comb_done, 1)
            for i in range(2):
                dve.wait_ge(combt_pe, i + 1)
                nc.vector.tensor_copy(comb_rows[:, i * 1024:(i + 1) * 1024],
                                      flat(low[0:8, 2 * i:2 * i + 2, :])).then_inc(combt_done, 1)

        @block.tensor
        def _(pe):
            def normalised(c):
                pe.wait_ge(norm_done, c + 1)
                if c:
                    pe.wait_ge(lo_done, c)
                for e in range(DH):
                    for i in range(TPC):
                        ins = nc.tensor.transpose(high[:, e, i * P:(i + 1) * P], xn[:, i, e * P:(e + 1) * P], g.ident[:])
                ins.then_inc(cols_pe, 1)
                pe.wait_ge(lo_done, c + 1)
                for i in range(TPC):
                    t = c * TPC + i
                    ts = slice(t * P, (t + 1) * P)
                    for e in range(DH):
                        ins = split3(nc, high[:, 2, t * 8:(t + 1) * 8], g.xn_hi[:, e, ts], g.xn_lo[:, e, ts],
                                     g.rw_hi[:, e, :], g.rw_lo[:, e, :], e == 0, e == DH - 1)
                    ins.then_inc(logit_pe, 1)

            for c in range(NC):
                pe.wait_ge(h_sum, c + 1)
                if c >= 2:
                    pe.wait_ge(x1_done, c - 1)
                for i in range(TPC):
                    for e in range(DH):
                        ins = nc.tensor.transpose(low[:, 2 * (c % 2) + i // 2, (i % 2) * D + e * P:(i % 2) * D + (e + 1) * P],
                                                  h32[:, c % 2, e, i * P:(i + 1) * P], g.ident[:])
                ins.then_inc(rows_pe, 1)
                if c:
                    normalised(c - 1)
            normalised(NC - 1)
            pe.wait_ge(comb_done, 1)
            for t in range(NT):
                ins = nc.tensor.transpose(low[0:8, t // 4, (t % 4) * P:(t % 4 + 1) * P], comb[:, t, :], g.ident[:])
                if t % 8 == 7:
                    ins.then_inc(combt_pe, 1)


def experts(nc, a, g):
    at = g.tmp_at
    t_g, act_g, hid, hid_hi, hid_lo = (g.place(n, [P, 2, CW], dt, at + i * 4096) for i, (n, dt) in enumerate(
        (("t_g", F32), ("act_g", F32), ("hid", F32), ("hid_hi", F32R), ("hid_lo", F32R))))
    UNITS = 2 * NC
    STEPS = UNITS * FT
    PAIR_LOOPS = EXPERTS // 2
    (gate_pe, up_pe, tanh_done, act_done, hid_done, hi_done, lo_done, down_pe, out_done, cleared, passed) = g.semaphores(
        "gate_pe", "up_pe", "tanh_done", "act_done", "hid_done", "hid_hi_done", "hid_lo_done", "down_pe", "out_done",
        "cleared", "passed")
    comb_in = g.semaphores("comb_in0", "comb_in1")
    gates, outs = g.psum

    def chunk(c):
        return slice(c * CW, (c + 1) * CW)

    def pair_of_experts(eng, body):
        with eng.Fori(0, PAIR_LOOPS - 1) as n:
            body(n, False)
        body(PAIR_LOOPS - 1, True)

    with nc.Block() as block:
        @block.sync
        def _(sp):
            sp.dma_start(g.combine[:, 0, :], g.comb_dram[0:1, :].broadcast_to([P, S])).then_inc(comb_in[0], 16)

            def body(n, last):
                for v in range(UNITS):
                    w, c = v // NC, v % NC
                    if last and w == 1:
                        continue
                    e = 2 * n + w + 1 if last else sp.snap(2 * n + w + 1)
                    if c == 0:
                        if v:
                            sp.wait_ge(down_pe, n * STEPS + v * FT)
                        else:
                            sp.wait_ge(gate_pe, n * STEPS + 1)
                        sp.sem_inc(passed, 1)
                    for i in range(2):
                        weight_piece(nc, a, sp, "load", g, 1 - w, e, 2 * c + i,
                                     PIECES * (w + 1) + 2 * c + i, n * 2 * PIECES)
                    if c == 1:
                        if w:
                            sp.wait_ge(out_done, n * UNITS + NC * w)
                        else:
                            sp.wait_ge(act_done, n * STEPS + 1)
                        sp.sem_inc(passed, 1)
                        sp.dma_start(g.combine[:, 1 - w, :], g.comb_dram[bass.ds(e, 1), :].broadcast_to([P, S])
                                     ).then_inc(comb_in[1 - w], 16)

            pair_of_experts(sp, body)

        @block.tensor
        def _(pe):
            def body(n, last):
                def down(k):
                    v, f = k // FT, k % FT
                    w = v // NC
                    pe.wait_ge(hi_done, n * STEPS + k + 1)
                    pe.wait_ge(lo_done, n * STEPS + k + 1)
                    if f == 0 and v >= 2:
                        pe.wait_ge(out_done, n * UNITS + v - 1)
                    for e in range(DH):
                        cols = slice(DOWN_AT + f * D + e * P, DOWN_AT + f * D + (e + 1) * P)
                        ins = split3(nc, outs[:, 2 * (v % 2) + e, :], g.w_hi[w][:, cols], g.w_lo[w][:, cols],
                                     hid_hi[:, k % 2, :], hid_lo[:, k % 2, :], f == 0, f == FT - 1)
                    ins.then_inc(down_pe, 1)

                def up_or_gate(k, bank, first):
                    v, f = k // FT, k % FT
                    w, c = v // NC, v % NC
                    for e in range(DH):
                        cols = slice(first + e * DFF + f * P, first + e * DFF + (f + 1) * P)
                        ins = split3(nc, gates[:, bank, :], g.w_hi[w][:, cols], g.w_lo[w][:, cols],
                                     g.xn_hi[:, e, chunk(c)], g.xn_lo[:, e, chunk(c)], e == 0, e == DH - 1)
                    return ins

                for k in range(STEPS):
                    if k % (FT * NC) == 0:
                        pe.wait_ge(g.w_lo_done, n * 2 * PIECES + PIECES * (k // (FT * NC) + 1))
                    if k >= 2:
                        pe.wait_ge(act_done, n * STEPS + k - 1)
                    up_or_gate(k, k % 2, 0).then_inc(gate_pe, 1)
                    if k >= 2:
                        pe.wait_ge(hid_done, n * STEPS + k - 1)
                    up_or_gate(k, 2 + k % 2, UP_AT).then_inc(up_pe, 1)
                    if k:
                        down(k - 1)
                down(STEPS - 1)

            pair_of_experts(pe, body)

        @block.scalar
        def _(act):
            def body(n, last):
                for k in range(STEPS + 1):
                    if k:
                        m = k - 1
                        if m >= 2:
                            act.wait_ge(down_pe, n * STEPS + m - 1)
                        act.wait_ge(hid_done, n * STEPS + m + 1)
                        nc.scalar.activation(hid_hi[:, m % 2], hid[:, m % 2], ACT.Copy).then_inc(hi_done, 1)
                    if k < STEPS:
                        if k >= 2:
                            act.wait_ge(act_done, n * STEPS + k - 1)
                        act.wait_ge(gate_pe, n * STEPS + k + 1)
                        nc.scalar.activation(t_g[:, k % 2], gates[:, k % 2, :], ACT.Tanh, scale=0.5
                                             ).then_inc(tanh_done, 1)
                    v, f = k // FT, k % FT
                    w, c = v // NC, v % NC
                    if k < STEPS and f in (2, 5) and not (last and w == 1):
                        i = 2 * c + (f == 5)
                        weight_piece(nc, a, act, "high", g, 1 - w, None, i, PIECES * (w + 1) + i, n * 2 * PIECES)

            pair_of_experts(act, body)

        @block.vector
        def _(dve):
            nc.vector.memset(g.facc[:], 0.0).then_inc(cleared, 1)
            dve.wait_ge(cleared, 1)

            def body(n, last):
                def add_out(v):
                    w, c = v // NC, v % NC
                    if c == 0:
                        dve.wait_ge(comb_in[w], n * 16 + 16)
                    dve.wait_ge(down_pe, n * STEPS + (v + 1) * FT)
                    src = outs[:, 2 * (v % 2):2 * (v % 2) + 2, :]
                    dst = g.facc[:, :, chunk(c)]
                    nc.vector.tensor_tensor(src, src, g.combine[:, w, chunk(c)].unsqueeze(1).broadcast_to([P, DH, CW]),
                                            ALU.mult)
                    dve.drain()
                    nc.vector.tensor_tensor(dst, src, dst, ALU.add).then_inc(out_done, 1)

                for k in range(STEPS):
                    v, f = k // FT, k % FT
                    w, c = v // NC, v % NC
                    dve.wait_ge(tanh_done, n * STEPS + k + 1)
                    nc.vector.scalar_tensor_tensor(act_g[:, k % 2], t_g[:, k % 2], 1.0, gates[:, k % 2, :],
                                                   ALU.add, ALU.mult).then_inc(act_done, 1)
                    dve.drain()
                    if k >= 2:
                        dve.wait_ge(lo_done, n * STEPS + k - 1)
                    dve.wait_ge(up_pe, n * STEPS + k + 1)
                    nc.vector.tensor_tensor(hid[:, k % 2], act_g[:, k % 2], gates[:, 2 + k % 2, :], ALU.mult
                                            ).then_inc(hid_done, 1)
                    if f == 1 and v:
                        add_out(v - 1)
                    if f in (3, 6) and not (last and w == 1):
                        i = 2 * c + (f == 6)
                        weight_piece(nc, a, dve, "low", g, 1 - w, None, i, PIECES * (w + 1) + i, n * 2 * PIECES)
                add_out(UNITS - 1)
                dve.drain()

            pair_of_experts(dve, body)

        @block.gpsimd
        def _(pool):
            def body(n, last):
                for k in range(STEPS):
                    pool.wait_ge(hi_done, n * STEPS + k + 1)
                    nc.gpsimd.tensor_tensor(hid_lo[:, k % 2], hid[:, k % 2], hid_hi[:, k % 2].bitcast(F32),
                                            ALU.subtract).then_inc(lo_done, 1)

            pair_of_experts(pool, body)


def finish(nc, out, g):
    res = g.place("res", [P, 2, TPC, D], F32, g.tmp_at)
    back_pe, res_done = g.semaphores("back_pe", "res_done")
    stored = g.semaphores("stored_even", "stored_odd")
    flat = lambda x: x.rearrange("p a b -> p (a b)")
    with nc.Block() as block:
        @block.tensor
        def _(pe):
            for c in range(NC):
                if c >= 4:
                    pe.wait_ge(res_done, c - 3)
                quad, half = g.psum[c // 2 % 2], 2 * (c % 2)
                for i in range(TPC):
                    for e in range(DH):
                        ins = nc.tensor.transpose(quad[:, half + i // 2, (i % 2) * D + e * P:(i % 2) * D + (e + 1) * P],
                                                  g.facc[:, e, (c * TPC + i) * P:(c * TPC + i + 1) * P], g.ident[:])
                ins.then_inc(back_pe, 1)

        @block.vector
        def _(dve):
            for c in range(NC):
                quad, half = g.psum[c // 2 % 2], 2 * (c % 2)
                dve.wait_ge(back_pe, c + 1)
                if c >= 2:
                    dve.wait_ge(stored[c % 2], 16 * (c // 2))
                nc.vector.scalar_tensor_tensor(flat(res[:, c % 2]), flat(quad[:, half:half + 2, :]), g.tg_f[:],
                                               flat(g.x1[:, c * TPC:(c + 1) * TPC, :]), ALU.mult, ALU.add
                                               ).then_inc(res_done, 1)

        @block.sync
        def _(sp):
            for c in range(NC):
                sp.wait_ge(res_done, c + 1)
                sp.dma_start(out[c * CW:(c + 1) * CW, :].rearrange("(t p) d -> p t d", p=P), res[:, c % 2]
                             ).then_inc(stored[c % 2], 16)
            for k in stored:
                sp.wait_ge(k, 16 * NC // 2)


def kernel(**inputs):
    import numpy as _np
    import concourse.bacc as _bacc
    from concourse import mybir as _mybir
    from concourse.bass_utils import run_bass_kernel_spmd as _run

    x = {k: _np.asarray(v) for k, v in inputs.items()}

    def halves(v):
        return v.reshape(-1, P).T

    def packed(gate, up, down):
        parts = [gate.T.reshape(DH, P, DFF), up.T.reshape(DH, P, DFF)]
        cols = [p.transpose(1, 0, 2).reshape(P, DH * DFF) for p in parts]
        cols.append(down.T.reshape(FT, P, D).transpose(1, 0, 2).reshape(P, FT * D))
        return _np.concatenate(cols, axis=1)

    w = [packed(x["L0_ffn_shared_gate"], x["L0_ffn_shared_up"], x["L0_ffn_shared_down"])]
    w += [packed(x["L0_ffn_routed_gate"][e], x["L0_ffn_routed_up"][e], x["L0_ffn_routed_down"][e])
          for e in range(ROUTED)]
    arrays = {
        "x": x["x"][0], "ctx": x["ctx_1024"][0],
        "g_xattn": _np.broadcast_to(x["g_xattn"].reshape(1, 1), (P, 1)),
        "g_ffn": _np.broadcast_to(x["g_ffn"].reshape(1, 1), (P, 1)),
        "wq": x["L0_xattn_Wq"], "wk": x["L0_xattn_Wk"], "wvT": x["L0_xattn_Wv"].T,
        "wihT": x["L0_xattn_gru_wih"].T, "whhT": x["L0_xattn_gru_whh"].T,
        "bih": halves(x["L0_xattn_gru_bih"]), "bhh": halves(x["L0_xattn_gru_bhh"]),
        "slot_norm_w": halves(x["L0_xattn_slot_norm_w"]), "input_norm_w": halves(x["L0_xattn_input_norm_w"]),
        "routerT": x["L0_ffn_router_w"].T, "w": _np.stack(w),
    }
    nc = _bacc.Bacc("TRN2", target_bir_lowering=False, num_devices=1)
    feeds, aps = {}, {}
    for name, v in arrays.items():
        v = _np.ascontiguousarray(v)
        feeds[f"in_{name}"] = v
        aps[name] = nc.dram_tensor(f"in_{name}", v.shape, _mybir.dt.from_np(v.dtype), kind="ExternalInput").ap()
    out = nc.dram_tensor("out", (S, D), _mybir.dt.float32, kind="ExternalOutput").ap()
    build_kernel(nc, aps, out)
    r = _run(nc, [feeds], core_ids=[0])
    return r.results[0]["out"].reshape(1, S, D)
```

```python
import concourse.bass as bass
from concourse import mybir
from contextlib import ExitStack

F32 = mybir.dt.float32
F32R = mybir.dt.float32r
I32 = mybir.dt.int32
U32 = mybir.dt.uint32
ALU = mybir.AluOpType
ACT = mybir.ActivationFunctionType
AX = mybir.AxisListType

P = 128
S = 2048
M = 1601
D = 256
DH = D // P
CW = 512
NC = S // CW
NT = S // P
TPC = CW // P
MT = -(-M // P)
MPAD = M + 1
ITERS = 3
EPS_NORM = 1e-6
EPS_ATTN = 1e-6
EPS_LN = 1e-5
EPS_TOP = 1e-9
SCALE = float(D) ** -0.5
DFF = 1024
FT = DFF // P
ROUTED = 7
EXPERTS = ROUTED + 1
WCOLS = 3 * DH * DFF
PIECE = 768
PIECES = WCOLS // PIECE
RAW = 4
UP_AT, DOWN_AT = DH * DFF, 2 * DH * DFF
SLOT_UNITS = 2 * S // CW + ROUTED - 1
UNITS = NC + SLOT_UNITS
PLACES = UNITS * CW
MAGIC = float(0x5F3759DF)


class Store:
    pass


def rows_of(t):
    return min(P, M - t * P)


BLOCKS = [(0, 1, 2), (3, 4, 5), (6, 7, 8), (9, 10), (11, 12)]
E_SLOTS = 6
E_SLOT = {t: 3 * (b % 2) + i for b, ts in enumerate(BLOCKS) for i, t in enumerate(ts)}
ITEMS = [(b, c) for b in range(len(BLOCKS)) for c in range(NC)]
AFTER = {3: [0], 4: [1], 5: [2, 3], 6: [4], 7: [5], 8: [6, 7], 9: [8, 9], 10: [10, 11],
         11: [12, 13], 12: [14, 15]}
TAIL = [16, 17, 18, 19]
PAIRS = [(i, t) for i, (b, _) in enumerate(ITEMS) for t in BLOCKS[b]]
PAIRS_OF = {i: [n for n, (k, _) in enumerate(PAIRS) if k == i] for i in range(len(ITEMS))}
NPAIR, NITEM = len(PAIRS), len(ITEMS)
RING = 4


def rsqrt(nc, dve, g, y, x, n):
    i, t, u = g.ni[:, 0:n], g.na[:, 0:n], g.nb[:, 0:n]
    dve.drain()
    nc.vector.tensor_scalar(i, x.bitcast(I32), 1, None, ALU.logical_shift_right)
    dve.drain()
    nc.vector.tensor_scalar(y.bitcast(I32), i, -1.0, MAGIC, ALU.mult, ALU.add)
    for _ in range(4):
        dve.drain()
        nc.vector.tensor_tensor(t, y, y, ALU.mult)
        dve.drain()
        nc.vector.scalar_tensor_tensor(u, t, -0.5, x, ALU.mult, ALU.mult)
        dve.drain()
        nc.vector.scalar_tensor_tensor(y, u, 1.5, y, ALU.add, ALU.mult)
    dve.drain()

def diagonal(nc, g, dst, col, n):
    return nc.vector.tensor_tensor(dst, g.ident[:].unsqueeze(1).broadcast_to([P, n, P]),
                                   col.unsqueeze(2).broadcast_to([P, n, P]), ALU.mult)

def split3(nc, dst, w_hi, w_lo, m_hi, m_lo, start, stop):
    nc.tensor.matmul(dst, w_hi, m_hi, start=start, stop=False)
    nc.tensor.matmul(dst, w_lo, m_hi, start=False, stop=False)
    return nc.tensor.matmul(dst, w_hi, m_lo, start=False, stop=stop)


def build_kernel(nc, a, out):
    g = Store()
    with ExitStack() as ctx:
        base = -(-nc.sbuf_base // 32) * 32

        def place(name, shape, dt, at):
            return nc.alloc_sbuf_tensor_at(name, shape, dt, offset=base + at)

        def semaphores(*names):
            return [ctx.enter_context(nc.semaphore(n)) for n in names]

        g.psum = [ctx.enter_context(nc.psum_tensor(f"quad{i}", [P, 4, CW], F32)) for i in range(2)]

        g.h_at = 0
        g.acc_at = g.h_at + 2 * DH * S * 4
        g.rstd_at = g.acc_at + DH * S * 4
        g.k_at = g.rstd_at + S * 4
        g.k_size = -(-DH * MPAD * 4 // 32) * 32
        g.v_at = g.k_at + 2 * g.k_size
        g.v_size = MT * D * 4
        g.gw_at = g.v_at + 2 * g.v_size
        g.gw_size = DH * 3 * D * 4
        g.e_at = g.gw_at + 4 * g.gw_size
        g.racc_at = g.e_at + E_SLOTS * S * 4
        g.ring_at = g.racc_at + S * 4
        g.small_at = g.ring_at + RING * 2 * CW * 4
        small = [g.small_at]

        def tiny(name, shape, dt=F32):
            at = small[0]
            n = 4
            for k in shape[1:]:
                n *= k
            small[0] += -(-n // 32) * 32
            return place(name, shape, dt, at)

        g.h_hi = place("h_hi", [P, DH, S], F32R, g.h_at)
        g.h_lo = place("h_lo", [P, DH, S], F32R, g.h_at + DH * S * 4)
        g.acc = place("acc", [P, DH, S], F32, g.acc_at)
        g.rstd_all = place("rstd_all", [P, S], F32, g.rstd_at)
        g.k_hi = place("k_hi", [P, DH, MPAD], F32R, g.k_at)
        g.k_lo = place("k_lo", [P, DH, MPAD], F32R, g.k_at + g.k_size)
        g.v_hi = place("v_hi", [P, MT, D], F32R, g.v_at)
        g.v_lo = place("v_lo", [P, MT, D], F32R, g.v_at + g.v_size)
        g.wih_hi, g.wih_lo, g.whh_hi, g.whh_lo = (
            place(n, [P, DH, 3 * D], F32R, g.gw_at + i * g.gw_size)
            for i, n in enumerate(("wih_hi", "wih_lo", "whh_hi", "whh_lo")))
        g.E = place("E", [P, E_SLOTS, S], F32, g.e_at)
        g.racc = place("racc", [P, S], F32, g.racc_at)
        g.ring_hi = place("ring_hi", [P, RING, CW], F32R, g.ring_at)
        g.ring_lo = place("ring_lo", [P, RING, CW], F32R, g.ring_at + RING * CW * 4)

        g.ident = tiny("ident", [P, P])
        g.ones = tiny("ones", [P, P])
        g.tg_x = tiny("tg_x", [P, 1])
        g.tg_f = tiny("tg_f", [P, 1])
        g.bih = tiny("bih", [P, 3 * DH])
        g.bhh = tiny("bhh", [P, 3 * DH])
        g.b_gate = tiny("b_gate", [P, 2 * DH])
        g.w_in = tiny("w_in", [P, DH])
        g.w_slot = tiny("w_slot", [P, DH])
        g.k_scale = tiny("k_scale", [P, DH])
        g.rw_raw = tiny("rw_raw", [P, DH, 8])
        g.rw_hi = tiny("rw_hi", [P, DH, 8], F32R)
        g.rw_lo = tiny("rw_lo", [P, DH, 8], F32R)
        g.mean_var = tiny("mean_var", [P, NT, 2])
        g.rstd_col = tiny("rstd_col", [P, NT])
        g.nx = tiny("nx", [P, NT])
        g.ny = tiny("ny", [P, NT])
        g.na = tiny("na", [P, NT])
        g.nb = tiny("nb", [P, NT])
        g.ni = tiny("ni", [P, NT], I32)
        g.c_ssq = tiny("c_ssq", [P, NT])
        g.c_rstd = tiny("c_rstd", [P, NT])
        g.mx = tiny("mx", [P, 2, 2])
        g.neg_max = tiny("neg_max", [P, 2])
        g.zsum = tiny("zsum", [P, 2])
        g.rz = tiny("rz", [P, 1])
        g.zeros = tiny("zeros", [P, P])
        g.in_dram = nc.dram_tensor("expert_in", (PLACES, D), F32).ap()
        g.out_dram = nc.dram_tensor("expert_out", (PLACES, D), F32).ap()
        g.cleared = semaphores("cleared")[0]

        g.place, g.semaphores, g.tiny = place, semaphores, tiny
        prepare(nc, a, g)
        attention(nc, g)
        handover(nc, a, g)
        experts(nc, a, g)
        finish(nc, out, g)


def prepare(nc, a, g):
    place, semaphores, psum = g.place, g.semaphores, g.psum
    E_AT, ACC_AT, RACC_AT, RING_AT = g.e_at, g.acc_at, g.racc_at, g.ring_at
    ident, ones = g.ident, g.ones
    h_hi, h_lo, k_hi, k_lo, v_hi, v_lo = g.h_hi, g.h_lo, g.k_hi, g.k_lo, g.v_hi, g.v_lo
    mean_var, rstd_col, c_ssq, c_rstd, nx = g.mean_var, g.rstd_col, g.c_ssq, g.c_rstd, g.nx

    x_rows = place("x_rows", [P, NT, D], F32, ACC_AT)
    at = E_AT
    ctx_rows = place("ctx_rows", [P, MT, D], F32, at)
    at += MT * D * 4
    p_hi = place("p_hi", [P, DH, MPAD], F32R, at)
    at += g.k_size
    p_lo = place("p_lo", [P, DH, MPAD], F32R, at)
    at += g.k_size
    wv_hi = place("wv_hi", [P, DH, D], F32R, at)
    wv_lo = place("wv_lo", [P, DH, D], F32R, at + 2048)
    kq_hi = place("kq_hi", [P, DH, D], F32R, at + 4096)
    kq_lo = place("kq_lo", [P, DH, D], F32R, at + 6144)
    wih = place("wih_raw", [P, DH, 3 * D], F32, RING_AT)
    whh = place("whh_raw", [P, DH, 3 * D], F32, RING_AT + 6144)
    scaled = place("scaled", [P, 2, CW], F32, RING_AT + 12288)
    wq = place("wq_raw", [P, DH, D], F32, RACC_AT)
    wk = place("wk_raw", [P, DH, D], F32, RACC_AT + 2048)
    wv = place("wv_raw", [P, DH, D], F32, RACC_AT + 4096)
    diag = place("diag0", [P, TPC, P], F32, RACC_AT + 6144)
    ln_stats = place("ln_stats", [P, NT, 6], F32, RACC_AT + 6144)
    junk = place("junk0", [P, D], F32, g.rstd_at)

    (ld_ctx, ld_x, ld_w, ld_small, ld_gw, const0, const1, sq_done, c_norm, ln_done, p_zero, w_hi_done,
     w_lo_done, kq_in, job_pe, job_scaled, job_hi, job_done, dg_done, spread_pe, spread_done, zeroed) = semaphores(
        "ld_ctx", "ld_x", "ld_w", "ld_small", "ld_gw", "const0", "const1", "sq_done", "c_norm", "ln_done",
        "p_zero", "w_hi_done", "w_lo_done", "kq_in", "job_pe", "job_scaled", "job_hi", "job_done",
        "dg_done", "spread_pe", "spread_done", "zeroed")

    jobs = [("ctx", m, dh) for m in range(NC) for dh in range(DH)]
    jobs += [("kq", 0, ch) for ch in range(DH)]
    jobs += [("key", m, dh) for m in range(NC) for dh in range(DH)]
    jobs += [("value", t, 0) for t in range(MT)]
    jobs += [("slot", c, dh) for c in range(NC) for dh in range(DH)]

    def width(m, even=False):
        w = min(CW, M - m * CW)
        return w + (w % 2 if even else 0)

    def bank(n):
        return psum[n % 8 // 4][:, n % 4, :]

    def source(n):
        kind, m, dh = jobs[n]
        if kind == "value":
            return bank(n)[0:rows_of(m), 0:D]
        if kind == "kq":
            return bank(n)[:, 0:D]
        return bank(n)[:, 0:{"slot": CW, "ctx": width(m), "key": width(m, True)}[kind]]

    def target(n):
        kind, m, dh = jobs[n]
        if kind == "slot":
            return tuple(h[:, dh, m * CW:(m + 1) * CW] for h in (h_hi, h_lo))
        if kind == "ctx":
            return tuple(p[:, dh, m * CW:m * CW + width(m)] for p in (p_hi, p_lo))
        if kind == "kq":
            return kq_hi[:, dh, :], kq_lo[:, dh, :]
        if kind == "value":
            return v_hi[0:rows_of(m), m, :], v_lo[0:rows_of(m), m, :]
        return tuple(k[:, dh, m * CW:m * CW + width(m, True)] for k in (k_hi, k_lo))

    def scaled_jobs_to(n):
        return sum(jobs[i][0] in ("ctx", "key") for i in range(n))

    weights = [(wv, wv_hi, wv_lo), (wih, g.wih_hi, g.wih_lo), (whh, g.whh_hi, g.whh_lo)]

    with nc.Block() as block:
        @block.sync
        def _(sp):
            last = MT - 1
            for t0 in range(0, last, 4):
                sp.dma_start(ctx_rows[:, t0:t0 + 4, :], a["ctx"][t0 * P:(t0 + 4) * P, :].rearrange(
                    "(t p) d -> p t d", p=P)).then_inc(ld_ctx, 16)
            sp.dma_start(ctx_rows[0:rows_of(last), last, :], a["ctx"][last * P:M, :]).then_inc(ld_ctx, 16)
            for dst, name in ((wk, "wk"), (wq, "wq"), (wv, "wvT")):
                sp.dma_start(dst[:], a[name].rearrange("(h p) d -> p h d", p=P)).then_inc(ld_w, 16)
            for t0 in range(0, NT, 4):
                sp.dma_start(x_rows[:, t0:t0 + 4, :], a["x"][t0 * P:(t0 + 4) * P, :].rearrange(
                    "(t p) d -> p t d", p=P)).then_inc(ld_x, 16)
            for dst, name in ((wih, "wihT"), (whh, "whhT")):
                sp.dma_start(dst[:], a[name].rearrange("(h p) d -> p h d", p=P)).then_inc(ld_gw, 16)
            sp.wait_ge(zeroed, 1)
            for h in range(D // P):
                n = SLOT_UNITS * CW // P
                sp.dma_start(g.in_dram[S:PLACES, h * P:(h + 1) * P].rearrange("(t p) d -> p t d", p=P),
                             g.zeros[:].unsqueeze(1).broadcast_to([P, n, P])).then_inc(g.cleared, 16)

        @block.gpsimd
        def _(pool):
            nc.gpsimd.memset(ident[:], 0.0).then_inc(const0, 1)
            nc.gpsimd.memset(ones[:], 1.0).then_inc(const1, 1)
            nc.gpsimd.memset(g.zeros[:], 0.0).then_inc(zeroed, 1)
            nc.gpsimd.memset(g.rw_raw[:], 0.0).then_inc(const1, 1)
            pool.wait_ge(const0, 1)
            nc.gpsimd.affine_select(out=ident[:], in_=ident[:], compare_op=ALU.not_equal, fill=1.0,
                                    base=0, pattern=[[-1, P]], channel_multiplier=1).then_inc(const1, 1)

        @block.scalar
        def _(act):
            for dst, name in ((g.w_in, "input_norm_w"), (g.w_slot, "slot_norm_w"), (g.bih, "bih"),
                              (g.bhh, "bhh"), (g.tg_x, "g_xattn"), (g.tg_f, "g_ffn")):
                act.dma_start(dst[:], a[name]).then_inc(ld_small, 16)
            act.wait_ge(const1, 3)
            act.dma_start(g.rw_raw[:, :, 0:ROUTED], a["routerT"].rearrange("(h p) e -> p h e", p=P)
                          ).then_inc(ld_small, 16)
            for t in range(MT):
                act.wait_ge(ld_ctx, 16 * 4)
                if t:
                    act.drain()
                r = rows_of(t)
                nc.scalar.activation(junk[0:r, :], ctx_rows[0:r, t, :], ACT.Square,
                                     accum_out=c_ssq[0:r, t:t + 1]).then_inc(sq_done, 1)
            act.wait_ge(ld_small, 16 * 7)
            act.drain()
            for t in (g.tg_x, g.tg_f):
                nc.scalar.activation(t[:], t[:], ACT.Tanh)
            nc.scalar.activation(g.rw_hi[:], g.rw_raw[:], ACT.Copy).then_inc(w_hi_done, 1)
            act.wait_ge(ld_w, 48)
            nc.scalar.activation(wv_hi[:], wv[:], ACT.Copy).then_inc(w_hi_done, 1)
            for n in range(len(jobs)):
                kind, m, dh = jobs[n]
                act.wait_ge(job_pe, n + 1)
                src = source(n)
                if kind in ("ctx", "key"):
                    k = scaled_jobs_to(n)
                    col = g.w_in if kind == "ctx" else g.k_scale
                    if kind == "key":
                        act.wait_ge(kq_in, 1)
                    if k >= 2:
                        act.wait_ge(job_done, [i for i in range(n) if jobs[i][0] in ("ctx", "key")][k - 2] + 1)
                    mid = scaled[:, k % 2, 0:src.shape[1]]
                    nc.scalar.activation(mid, src, ACT.Copy, scale=col[:, dh:dh + 1])
                    act.drain()
                    src = mid
                nc.scalar.activation(target(n)[0], src, ACT.Copy).then_inc(job_hi, 1)
                if n == 20:
                    act.wait_ge(ld_gw, 32)
                    nc.scalar.activation(g.wih_hi[:], wih[:], ACT.Copy).then_inc(w_hi_done, 1)
                    nc.scalar.activation(g.whh_hi[:], whh[:], ACT.Copy).then_inc(w_hi_done, 1)
            for c in range(NC):
                act.wait_ge(spread_pe, c + 1)
                nc.scalar.activation(g.rstd_all[:, c * CW:(c + 1) * CW], bank(len(jobs) + c), ACT.Copy
                                     ).then_inc(spread_done, 1)

        @block.vector
        def _(dve):
            for p in (p_hi, p_lo):
                nc.vector.memset(p[:, :, M:MPAD].bitcast(F32), 0.0).then_inc(p_zero, 1)
            dve.wait_ge(sq_done, MT)
            last = rows_of(MT - 1)
            dve.drain()
            nc.vector.memset(nx[:], 1.0)
            dve.drain()
            nc.vector.tensor_scalar(nx[:, 0:MT - 1], c_ssq[:, 0:MT - 1], 1.0 / D, EPS_NORM, ALU.mult, ALU.add)
            nc.vector.tensor_scalar(nx[0:last, MT - 1:MT], c_ssq[0:last, MT - 1:MT], 1.0 / D, EPS_NORM, ALU.mult, ALU.add)
            rsqrt(nc, dve, g, c_rstd[:, 0:MT], nx[:, 0:MT], MT)
            for t in range(MT):
                r = rows_of(t)
                nc.vector.tensor_scalar(ctx_rows[0:r, t, :], ctx_rows[0:r, t, :], c_rstd[0:r, t:t + 1], None,
                                        ALU.mult).then_inc(c_norm, 1)
            dve.wait_ge(ld_small, 16 * 7)
            nc.vector.tensor_scalar(g.k_scale[:], g.w_slot[:], SCALE, None, ALU.mult).then_inc(kq_in, 1)
            nc.vector.tensor_tensor(g.b_gate[:], g.bih[:, 0:2 * DH], g.bhh[:, 0:2 * DH], ALU.add)
            dve.drain()
            nc.vector.tensor_scalar(g.b_gate[:], g.b_gate[:], 0.5, None, ALU.mult)
            dve.wait_ge(w_hi_done, 1)
            nc.vector.tensor_tensor(g.rw_lo[:], g.rw_raw[:], g.rw_hi[:].bitcast(F32), ALU.subtract)
            dve.wait_ge(w_hi_done, 2)
            nc.vector.tensor_tensor(wv_lo[:], wv[:], wv_hi[:].bitcast(F32), ALU.subtract).then_inc(w_lo_done, 1)

            def low_part(n):
                kind = jobs[n][0]
                dve.wait_ge(job_hi, n + 1)
                hi, lo = target(n)
                src = source(n)
                if kind in ("ctx", "key"):
                    src = scaled[:, scaled_jobs_to(n) % 2, 0:src.shape[1]]
                nc.vector.tensor_tensor(lo, src, hi.bitcast(F32), ALU.subtract).then_inc(job_done, 1)

            first_slot = len(jobs) - NC * DH
            for n in range(8):
                low_part(n)
            dve.wait_ge(ld_x, 16 * 4)
            for t in range(NT):
                nc.vector.bn_stats(ln_stats[:, t, :], x_rows[:, t, :])
            dve.drain()
            for t in range(NT):
                nc.vector.bn_aggr(mean_var[:, t, :], ln_stats[:, t, :])
            dve.drain()
            nc.vector.tensor_scalar(nx[:], mean_var[:, :, 1], EPS_LN, None, ALU.add)
            rsqrt(nc, dve, g, rstd_col[:], nx[:], NT)
            for t in range(NT):
                ins = nc.vector.tensor_scalar(x_rows[:, t, :], x_rows[:, t, :], mean_var[:, t, 0:1],
                                              rstd_col[:, t:t + 1], ALU.subtract, ALU.mult)
                if t % TPC == TPC - 1:
                    ins.then_inc(ln_done, 1)
            nc.vector.tensor_tensor(c_ssq[:], rstd_col[:], rstd_col[:], ALU.mult)
            dve.drain()
            nc.vector.tensor_tensor(c_ssq[:], c_ssq[:], mean_var[:, :, 1], ALU.mult)
            dve.drain()
            nc.vector.tensor_scalar(nx[:], c_ssq[:], EPS_NORM, None, ALU.add)
            rsqrt(nc, dve, g, rstd_col[:], nx[:], NT)
            for n in range(8, len(jobs)):
                low_part(n)
                if n == 21:
                    dve.wait_ge(w_hi_done, 4)
                    nc.vector.tensor_tensor(g.wih_lo[:], wih[:], g.wih_hi[:].bitcast(F32), ALU.subtract)
                    nc.vector.tensor_tensor(g.whh_lo[:], whh[:], g.whh_hi[:].bitcast(F32), ALU.subtract)
            for c in range(NC):
                if c:
                    dve.wait_ge(spread_pe, c)
                diagonal(nc, g, diag[:], rstd_col[:, c * TPC:(c + 1) * TPC], TPC).then_inc(dg_done, 1)
            dve.drain()

        @block.tensor
        def _(pe):
            pe.wait_ge(const1, 3)
            for n, (kind, m, dh) in enumerate(jobs):
                b = bank(n)
                if n >= 8:
                    pe.wait_ge(job_done, n - 7)
                if kind == "ctx":
                    tiles = range(m * TPC, min((m + 1) * TPC, MT))
                    pe.wait_ge(c_norm, tiles[-1] + 1)
                    for i, t in enumerate(tiles):
                        r = rows_of(t)
                        ins = nc.tensor.transpose(b[:, i * P:i * P + r], ctx_rows[0:r, t, dh * P:(dh + 1) * P],
                                                  ident[0:r, 0:r])
                elif kind == "slot":
                    pe.wait_ge(ln_done, m + 1)
                    for i in range(TPC):
                        ins = nc.tensor.transpose(b[:, i * P:(i + 1) * P],
                                                  x_rows[:, m * TPC + i, dh * P:(dh + 1) * P], ident[:])
                elif kind == "kq":
                    pe.wait_ge(ld_w, 48)
                    for e in range(DH):
                        ins = nc.tensor.matmul(b[:, 0:D], wk[:, e, dh * P:(dh + 1) * P], wq[:, e, :],
                                               start=(e == 0), stop=(e == DH - 1))
                elif kind == "key":
                    pe.wait_ge(job_done, NC * DH + DH)
                    pe.wait_ge(p_zero, 2)
                    w = width(m, True)
                    for e in range(DH):
                        ins = split3(nc, b[:, 0:w], kq_hi[:, e, dh * P:(dh + 1) * P], kq_lo[:, e, dh * P:(dh + 1) * P],
                                     p_hi[:, e, m * CW:m * CW + w], p_lo[:, e, m * CW:m * CW + w],
                                     e == 0, e == DH - 1)
                else:
                    pe.wait_ge(w_lo_done, 1)
                    r = rows_of(m)
                    for e in range(DH):
                        ins = split3(nc, b[0:r, 0:D], p_hi[:, e, m * P:m * P + r], p_lo[:, e, m * P:m * P + r],
                                     wv_hi[:, e, :], wv_lo[:, e, :], e == 0, e == DH - 1)
                ins.then_inc(job_pe, 1)
            for c in range(NC):
                pe.wait_ge(job_done, len(jobs) + c - 7)
                pe.wait_ge(dg_done, c + 1)
                nc.tensor.matmul(bank(len(jobs) + c), ones[:], diag[:].rearrange("p a b -> p (a b)"),
                                 start=True, stop=True).then_inc(spread_pe, 1)


def attention(nc, g):
    place = g.place
    h_hi, h_lo, acc, rstd_all, k_hi, k_lo, v_hi, v_lo, E, racc, ring_hi, ring_lo = (
        g.h_hi, g.h_lo, g.acc, g.rstd_all, g.k_hi, g.k_lo, g.v_hi, g.v_lo, g.E, g.racc, g.ring_hi, g.ring_lo)
    scores, sums = g.psum
    mx, neg_max, zsum, rz, ones = g.mx, g.neg_max, g.zsum, g.rz, g.ones
    slot = lambda s: g.e_at + s * S * 4
    u_hi = place("u_hi", [P, 2, DH, CW], F32R, slot(2))
    u_lo = place("u_lo", [P, 2, DH, CW], F32R, slot(3))
    r_diag = place("r_diag", [P, NC, TPC, P], F32, slot(4))
    sq = place("sq", [P, DH, CW], F32, slot(4))
    h_new = place("h_new", [P, 2, DH, CW], F32, slot(5))
    n_diag = place("n_diag", [P, TPC, P], F32, slot(4) + 4096)
    t_r = place("t_r", [P, 2, CW], F32, slot(0))
    t_z = place("t_z", [P, 2, CW], F32, slot(0) + 4096)
    n_in = place("n_in", [P, 2, CW], F32, slot(1))
    n_out = place("n_out", [P, 2, CW], F32, slot(1) + 4096)
    diff = place("diff", [P, 2, CW], F32, g.ring_at)
    rsum = g.c_ssq
    rinv = g.c_rstd

    (score_pe, drained, nmax, exped, scaled, rsummed, hi_done, lo_done, pair_pe, item_done, rs_pe, rdiag_done,
     rspread_pe, rinv_done, u_done, u_hi_done, u_lo_done, hn_pe, r_pe, z_pe, xn_pe, tr_done, tz_done, n_in_done,
     n_done, diff_done, h_done, h_hi_done, h_lo_done, sq_done, ss_pe, ndiag_done, nspread_pe, rstd_done, seen
     ) = g.semaphores(
        "score_pe", "drained", "nmax", "exped", "scaled_e", "rsummed", "hi_done", "lo_done", "pair_pe", "item_done",
        "rs_pe", "rdiag_done", "rspread_pe", "rinv_done", "u_done", "u_hi_done", "u_lo_done", "hn_pe", "r_pe",
        "z_pe", "xn_pe", "tr_done", "tz_done", "n_in_done", "n_done", "diff_done", "h_done", "h_hi_done",
        "h_lo_done", "sq_done1", "ss_pe", "ndiag_done", "nspread_pe", "rstd_done", "seen")
    GRU = NC * DH

    def chunk(c):
        return slice(c * CW, (c + 1) * CW)

    def pairs_until(item):
        return PAIRS_OF[item][-1] + 1

    def last_use(t):
        return max(n for n, (_, k) in enumerate(PAIRS) if k == t) + 1

    def early(t):
        return [n for i in AFTER.get(t, []) for n in PAIRS_OF[i]][:RING - 1]

    def late(t):
        return [n for i in AFTER.get(t, []) for n in PAIRS_OF[i]][RING - 1:]

    def before_in_slot(t):
        return max((k for k in range(t) if E_SLOT[k] == E_SLOT[t]), default=None)

    with nc.Block() as block:
        @block.tensor
        def _(pe):
            def item(i, it):
                b, c = ITEMS[i]
                if i >= 2:
                    pe.wait_ge(item_done, it * NITEM + i - 1)
                for n in PAIRS_OF[i]:
                    t = PAIRS[n][1]
                    r = rows_of(t)
                    pe.wait_ge(hi_done, it * NPAIR + n + 1)
                    pe.wait_ge(lo_done, it * NPAIR + n + 1)
                    for dh in range(DH):
                        ins = split3(nc, sums[:, 2 * (i % 2) + dh, :], v_hi[0:r, t, dh * P:(dh + 1) * P],
                                     v_lo[0:r, t, dh * P:(dh + 1) * P], ring_hi[0:r, n % RING, :],
                                     ring_lo[0:r, n % RING, :], n == PAIRS_OF[i][0], n == PAIRS_OF[i][-1])
                    ins.then_inc(pair_pe, 1)

            def spread_rinv(c, it):
                pe.wait_ge(rdiag_done, it * NC + c + 1)
                if c == 0:
                    pass
                nc.tensor.matmul(scores[:, (c + 1) % 4, :], ones[:], r_diag[:, c].rearrange("p a b -> p (a b)"),
                                 start=True, stop=True).then_inc(rspread_pe, 1)

            def gates(q, it):
                c, j = q // DH, q % DH
                m_h = [(h_hi[:, e, chunk(c)], h_lo[:, e, chunk(c)]) for e in range(DH)]
                m_u = [(u_hi[:, c % 2, e, :], u_lo[:, c % 2, e, :]) for e in range(DH)]

                def product(bank, gate, w_hi, w_lo, moving, start, stop):
                    at = gate * D + j * P
                    for e in range(DH):
                        ins = split3(nc, scores[:, bank, :], w_hi[:, e, at:at + P], w_lo[:, e, at:at + P],
                                     *moving[e], start and e == 0, stop and e == DH - 1)
                    return ins

                if q == 0:
                    pe.wait_ge(rinv_done, it * NC + 4)
                else:
                    pe.wait_ge(n_in_done, it * GRU + q)
                product(0, 2, g.whh_hi, g.whh_lo, m_h, True, True).then_inc(hn_pe, 1)
                if q:
                    pe.wait_ge(tr_done, it * GRU + q)
                product(1, 0, g.whh_hi, g.whh_lo, m_h, True, False)
                if j == 0:
                    pe.wait_ge(u_hi_done, it * NC + c + 1)
                    pe.wait_ge(u_lo_done, it * NC + c + 1)
                product(1, 0, g.wih_hi, g.wih_lo, m_u, False, True).then_inc(r_pe, 1)
                if q:
                    pe.wait_ge(tz_done, it * GRU + q)
                product(2, 1, g.whh_hi, g.whh_lo, m_h, True, False)
                product(2, 1, g.wih_hi, g.wih_lo, m_u, False, True).then_inc(z_pe, 1)
                product(3, 2, g.wih_hi, g.wih_lo, m_u, True, True).then_inc(xn_pe, 1)

            def square_sums(c, it):
                pe.wait_ge(sq_done, it * NC + c + 1)
                for i in range(TPC):
                    for e in range(DH):
                        ins = nc.tensor.matmul(sums[:, 0, c * TPC + i:c * TPC + i + 1], sq[:, e, i * P:(i + 1) * P],
                                               ones[:, 0:1], start=(e == 0), stop=(e == DH - 1))
                ins.then_inc(ss_pe, 1)

            def spread_rstd(c, it):
                pe.wait_ge(ndiag_done, it * NC + c + 1)
                nc.tensor.matmul(sums[:, 2 + c % 2, :], ones[:], n_diag[:].rearrange("p a b -> p (a b)"),
                                 start=True, stop=True).then_inc(nspread_pe, 1)

            with pe.Fori(0, ITERS) as it:
                for t in range(MT):
                    r = rows_of(t)
                    for c in range(NC):
                        if t == 0:
                            pe.wait_ge(h_hi_done, it * NC + c + 1)
                            pe.wait_ge(h_lo_done, it * NC + c + 1)
                        elif c % 2 == 0:
                            pe.wait_ge(drained, it * 2 * MT + 2 * (t - 1) + c // 2 + 1)
                        for e in range(DH):
                            ks = slice(t * P, t * P + r)
                            ins = split3(nc, scores[0:r, c, :], k_hi[:, e, ks], k_lo[:, e, ks],
                                         h_hi[:, e, chunk(c)], h_lo[:, e, chunk(c)], e == 0, e == DH - 1)
                        if c % 2:
                            ins.then_inc(score_pe, 1)
                    for i in AFTER.get(t, []):
                        item(i, it)
                item(TAIL[0], it)
                item(TAIL[1], it)
                pe.wait_ge(rsummed, it * (MT - 1) + MT - 1)
                pe.wait_ge(drained, it * 2 * MT + 2 * MT)
                for i in range(NT):
                    ins = nc.tensor.matmul(scores[:, 0, i:i + 1], racc[:, i * P:(i + 1) * P], ones[:, 0:1],
                                           start=True, stop=True)
                ins.then_inc(rs_pe, 1)
                item(TAIL[2], it)
                spread_rinv(0, it)
                spread_rinv(1, it)
                item(TAIL[3], it)
                spread_rinv(2, it)
                spread_rinv(3, it)
                for q in range(GRU):
                    gates(q, it)
                    c = q // DH - 1
                    if c >= 0 and q % DH == 0:
                        square_sums(c, it)
                    if c >= 0 and q % DH == 1:
                        spread_rstd(c, it)
                square_sums(NC - 1, it)
                spread_rstd(NC - 1, it)

        @block.scalar
        def _(act):
            def high_part(n, it):
                i, t = PAIRS[n]
                r, c = rows_of(t), ITEMS[i][1]
                act.wait_ge(scaled, it * MT + t + 1)
                if n >= RING:
                    act.wait_ge(pair_pe, it * NPAIR + n - RING + 1)
                nc.scalar.activation(ring_hi[0:r, n % RING, :], E[0:r, E_SLOT[t], chunk(c)], ACT.Copy
                                     ).then_inc(hi_done, 1)

            def u_high(c, it):
                act.wait_ge(u_done, it * NC + c + 1)
                if c >= 2:
                    act.wait_ge(xn_pe, it * GRU + DH * (c - 1))
                nc.scalar.activation(u_hi[:, c % 2], acc[:, :, chunk(c)], ACT.Copy).then_inc(u_hi_done, 1)

            def new_slots(c, it):
                act.wait_ge(h_done, it * GRU + DH * (c + 1))
                nc.scalar.activation(h_hi[:, :, chunk(c)], h_new[:, c % 2], ACT.Copy).then_inc(h_hi_done, 1)
                if c:
                    act.wait_ge(ss_pe, it * NC + c)
                nc.scalar.activation(sq[:], h_new[:, c % 2], ACT.Square).then_inc(sq_done, 1)

            def rstd_copy(c, it):
                act.wait_ge(nspread_pe, it * NC + c + 1)
                nc.scalar.activation(rstd_all[:, chunk(c)], sums[:, 2 + c % 2, :], ACT.Copy).then_inc(rstd_done, 1)

            act.sem_inc(h_hi_done, NC)
            act.sem_inc(rstd_done, NC)
            with act.Fori(0, ITERS) as it:
                for t in range(MT):
                    r = rows_of(t)
                    for n in early(t):
                        high_part(n, it)
                    act.wait_ge(nmax, it * MT + t + 1)
                    nc.scalar.activation(E[0:r, E_SLOT[t], :], E[0:r, E_SLOT[t], :], ACT.Exp,
                                         bias=neg_max[0:r, t % 2:t % 2 + 1],
                                         accum_out=zsum[0:r, t % 2:t % 2 + 1]).then_inc(exped, 1)
                    for n in late(t):
                        high_part(n, it)
                for i in TAIL:
                    for n in PAIRS_OF[i]:
                        high_part(n, it)
                for c in range(NC):
                    act.wait_ge(rspread_pe, it * NC + c + 1)
                    nc.scalar.activation(racc[:, chunk(c)], scores[:, (c + 1) % 4, :], ACT.Copy).then_inc(rinv_done, 1)
                u_high(0, it)
                for q in range(GRU):
                    c, j = q // DH, q % DH
                    p = q % 2
                    if q >= 2:
                        act.wait_ge(n_in_done, it * GRU + q - 1)
                    act.wait_ge(r_pe, it * GRU + q + 1)
                    nc.scalar.activation(t_r[:, p], scores[:, 1, :], ACT.Tanh, bias=g.b_gate[:, j:j + 1],
                                         scale=0.5).then_inc(tr_done, 1)
                    if q >= 2:
                        act.wait_ge(h_done, it * GRU + q - 1)
                    act.wait_ge(z_pe, it * GRU + q + 1)
                    nc.scalar.activation(t_z[:, p], scores[:, 2, :], ACT.Tanh, bias=g.b_gate[:, DH + j:DH + j + 1],
                                         scale=0.5).then_inc(tz_done, 1)
                    if c and j == 0:
                        new_slots(c - 1, it)
                    act.wait_ge(n_in_done, it * GRU + q + 1)
                    nc.scalar.activation(n_out[:, p], n_in[:, p], ACT.Tanh, bias=g.bih[:, 2 * DH + j:2 * DH + j + 1]
                                         ).then_inc(n_done, 1)
                    if c and j == 1:
                        rstd_copy(c - 1, it)
                    if j == 0 and c + 1 < NC:
                        u_high(c + 1, it)
                new_slots(NC - 1, it)
                rstd_copy(NC - 1, it)

        @block.vector
        def _(dve):
            def low_part(n, it):
                i, t = PAIRS[n]
                r, c = rows_of(t), ITEMS[i][1]
                dve.wait_ge(hi_done, it * NPAIR + n + 1)
                nc.vector.tensor_tensor(ring_lo[0:r, n % RING, :], E[0:r, E_SLOT[t], chunk(c)],
                                        ring_hi[0:r, n % RING, :].bitcast(F32), ALU.subtract).then_inc(lo_done, 1)

            def add_sums(i, it):
                b, c = ITEMS[i]
                dve.wait_ge(pair_pe, it * NPAIR + pairs_until(i))
                src = sums[:, 2 * (i % 2):2 * (i % 2) + DH, :]
                dst = acc[:, :, chunk(c)]
                if b == 0:
                    nc.vector.tensor_copy(dst, src).then_inc(item_done, 1)
                else:
                    nc.vector.tensor_tensor(dst, src, dst, ALU.add).then_inc(item_done, 1)

            def u_sums(c, it):
                dve.wait_ge(rinv_done, it * NC + c + 1)
                nc.vector.tensor_tensor(acc[:, :, chunk(c)], acc[:, :, chunk(c)],
                                        racc[:, chunk(c)].unsqueeze(1).broadcast_to([P, DH, CW]), ALU.mult
                                        ).then_inc(u_done, 1)

            def low_slots(c, it):
                dve.wait_ge(h_hi_done, it * NC + NC + c + 1)
                nc.vector.tensor_tensor(h_lo[:, :, chunk(c)], h_new[:, c % 2], h_hi[:, :, chunk(c)].bitcast(F32),
                                        ALU.subtract).then_inc(h_lo_done, 1)

            def rstd(c, it):
                dve.wait_ge(ss_pe, it * NC + c + 1)
                if c:
                    dve.wait_ge(nspread_pe, it * NC + c)
                nc.vector.tensor_scalar(g.nx[:, 0:TPC], sums[:, 0, c * TPC:(c + 1) * TPC], 1.0 / D, EPS_NORM,
                                        ALU.mult, ALU.add)
                rsqrt(nc, dve, g, g.ny[:, 0:TPC], g.nx[:, 0:TPC], TPC)
                diagonal(nc, g, n_diag[:], g.ny[:, 0:TPC], TPC).then_inc(ndiag_done, 1)

            dve.sem_inc(h_lo_done, NC)
            with dve.Fori(0, ITERS) as it:
                for t in range(MT):
                    r, s, p = rows_of(t), E_SLOT[t], t % 2
                    dve.drain()
                    for n in early(t):
                        low_part(n, it)
                    if t == 0:
                        dve.wait_ge(rstd_done, it * NC + NC)
                    if before_in_slot(t) is not None:
                        k = before_in_slot(t)
                        dve.wait_ge(hi_done, it * NPAIR + last_use(k))
                        dve.wait_ge(rsummed, it * (MT - 1) + max(k, 1))
                    for i in range(2):
                        dve.wait_ge(score_pe, it * 2 * MT + 2 * t + i + 1)
                        dve.sem_inc(seen, 1)
                        half = slice(i * 2 * CW, (i + 1) * 2 * CW)
                        nc.vector.tensor_tensor_reduce(
                            out=E[0:r, s, half], in0=scores[0:r, 2 * i:2 * i + 2, :].rearrange("p a b -> p (a b)"),
                            in1=rstd_all[0:r, half], scale=1.0, scalar=-3e38, op0=ALU.mult, op1=ALU.max,
                            accum_out=mx[0:r, p, i:i + 1]).then_inc(drained, 1)
                    dve.drain()
                    nc.vector.tensor_scalar(neg_max[0:r, p:p + 1], mx[0:r, p, 0:1], mx[0:r, p, 1:2], -1.0,
                                            ALU.max, ALU.mult).then_inc(nmax, 1)
                    for n in late(t):
                        low_part(n, it)
                    dve.wait_ge(exped, it * MT + t + 1)
                    nc.vector.reciprocal(rz[0:r, :], zsum[0:r, p:p + 1])
                    dve.drain()
                    nc.vector.tensor_scalar(E[0:r, s, :], E[0:r, s, :], rz[0:r, :], None, ALU.mult
                                            ).then_inc(scaled, 1)
                    for i in AFTER.get(t, []):
                        add_sums(i, it)
                dve.drain()
                for i in TAIL[0:3]:
                    for n in PAIRS_OF[i]:
                        low_part(n, it)
                    if i == TAIL[1]:
                        add_sums(TAIL[0], it)
                dve.wait_ge(rs_pe, it + 1)
                nc.vector.tensor_scalar(rsum[:], scores[:, 0, 0:NT], EPS_ATTN, None, ALU.add)
                dve.drain()
                nc.vector.reciprocal(rinv[:], rsum[:])
                dve.drain()
                for c in range(NC):
                    diagonal(nc, g, r_diag[:, c], rinv[:, c * TPC:(c + 1) * TPC], TPC).then_inc(rdiag_done, 1)
                add_sums(TAIL[1], it)
                for n in PAIRS_OF[TAIL[3]]:
                    low_part(n, it)
                add_sums(TAIL[2], it)
                add_sums(TAIL[3], it)
                dve.drain()
                u_sums(0, it)
                for q in range(GRU):
                    c, j, p = q // DH, q % DH, q % 2
                    if c and j == 1:
                        rstd(c - 1, it)
                    b_hn = g.bhh[:, 2 * DH + j:2 * DH + j + 1]
                    dve.wait_ge(hn_pe, it * GRU + q + 1)
                    dve.wait_ge(tr_done, it * GRU + q + 1)
                    if q >= 2:
                        dve.wait_ge(n_done, it * GRU + q - 1)
                    nc.vector.scalar_tensor_tensor(n_in[:, p], scores[:, 0, :], b_hn, t_r[:, p], ALU.add, ALU.mult)
                    dve.drain()
                    nc.vector.scalar_tensor_tensor(n_in[:, p], scores[:, 0, :], b_hn, n_in[:, p], ALU.add, ALU.add)
                    dve.drain()
                    dve.wait_ge(xn_pe, it * GRU + q + 1)
                    nc.vector.scalar_tensor_tensor(n_in[:, p], n_in[:, p], 0.5, scores[:, 3, :], ALU.mult, ALU.add
                                                   ).then_inc(n_in_done, 1)
                    if c and j == 0:
                        low_slots(c - 1, it)
                    if j == 0 and c + 1 < NC:
                        u_sums(c + 1, it)
                    dve.wait_ge(diff_done, it * GRU + q + 1)
                    dve.wait_ge(tz_done, it * GRU + q + 1)
                    nc.vector.scalar_tensor_tensor(diff[:, p], t_z[:, p], 1.0, diff[:, p], ALU.add, ALU.mult)
                    dve.drain()
                    if c >= 2 and j == 0:
                        dve.wait_ge(sq_done, it * NC + c - 1)
                    nc.vector.scalar_tensor_tensor(h_new[:, c % 2, j], diff[:, p], 0.5, n_out[:, p],
                                                   ALU.mult, ALU.add).then_inc(h_done, 1)
                low_slots(NC - 1, it)
                rstd(NC - 1, it)

        @block.gpsimd
        def _(pool):
            def u_low(c, it):
                pool.wait_ge(u_hi_done, it * NC + c + 1)
                for e in range(DH):
                    ins = nc.gpsimd.tensor_tensor(u_lo[:, c % 2, e, :], acc[:, e, chunk(c)],
                                                  u_hi[:, c % 2, e, :].bitcast(F32), ALU.subtract)
                ins.then_inc(u_lo_done, 1)

            with pool.Fori(0, ITERS) as it:
                for t in range(1, MT):
                    r = rows_of(t)
                    pool.wait_ge(scaled, it * MT + t + 1)
                    first = E[0:r, E_SLOT[0], :] if t == 1 else racc[0:r, :]
                    nc.gpsimd.tensor_tensor(racc[0:r, :], first, E[0:r, E_SLOT[t], :], ALU.add).then_inc(rsummed, 1)
                    pool.drain()
                u_low(0, it)
                for q in range(GRU):
                    c, j, p = q // DH, q % DH, q % 2
                    pool.wait_ge(n_done, it * GRU + q + 1)
                    if q >= 2:
                        pool.wait_ge(h_done, it * GRU + q - 1)
                    nc.gpsimd.tensor_tensor(diff[:, p], h_hi[:, j, chunk(c)].bitcast(F32), n_out[:, p], ALU.subtract)
                    pool.drain()
                    nc.gpsimd.tensor_tensor(diff[:, p], diff[:, p], h_lo[:, j, chunk(c)].bitcast(F32), ALU.add
                                            ).then_inc(diff_done, 1)
                    if j == 0 and c + 1 < NC:
                        u_low(c + 1, it)


def weight_piece(nc, a, eng, step, g, w, expert, cols, count, base=0):
    k = count % RAW
    raw = g.w_raw[:, k, :]
    if step == "load":
        if count >= RAW:
            eng.wait_ge(g.w_lo_done, count - RAW + 1)
        eng.dma_start(raw, a["w"][expert, :, cols] if isinstance(expert, int)
                      else a["w"][bass.ds(expert, 1), :, cols].rearrange("e p c -> (e p) c")
                      ).then_inc(g.w_loaded[k], 16)
    elif step == "high":
        eng.wait_ge(g.w_loaded[k], base * (16 // RAW) + (count - k) * (16 // RAW) + 16)
        nc.scalar.activation(g.w_hi[w][:, cols], raw, ACT.Copy).then_inc(g.w_hi_done, 1)
    else:
        eng.wait_ge(g.w_hi_done, base + count + 1)
        nc.vector.tensor_tensor(g.w_lo[w][:, cols], raw, g.w_hi[w][:, cols].bitcast(F32), ALU.subtract
                                ).then_inc(g.w_lo_done, 1)


def piece_cols(i):
    return slice(i * PIECE, (i + 1) * PIECE)


def handover(nc, a, g):
    place = g.place
    g.x1 = place("x1", [P, NT, D], F32, g.acc_at)
    at = g.rstd_at
    g.xn = place("xn", [P, NT, D], F32, at)
    at += NT * D * 4
    g.w_raw = place("w_raw", [P, RAW, PIECE], F32, at)
    at += RAW * PIECE * 4
    g.w_hi, g.w_lo = [], []
    for w in range(2):
        g.w_hi.append(place(f"w_hi{w}", [P, WCOLS], F32R, at))
        g.w_lo.append(place(f"w_lo{w}", [P, WCOLS], F32R, at + WCOLS * 4))
        at += 2 * WCOLS * 4
    xn_hi = place("xn_hi", [P, 2, DH, CW], F32R, at - 16384)
    xn_lo = place("xn_lo", [P, 2, DH, CW], F32R, at - 8192)
    g.tmp_at = at
    h32 = place("h32", [P, 2, DH, CW], F32, at)
    x_in = place("x_in", [P, 2, TPC, D], F32, at + 8192)
    at += 16384
    probs, best, chosen0, chosen1, taken, count, before, pos = (
        place(n, [P, NT, 8], F32, at + i * 512) for i, n in enumerate(
            ("probs", "best", "chosen0", "chosen1", "taken", "count", "before", "pos")))
    best_at = place("best_at", [P, NT, 8], U32, at + 4096)
    tri = place("tri", [P, P], F32, at + 4608)
    tiny = g.tiny
    stats = tiny("stats", [P, TPC, 6])
    where = tiny("where", [P, NT, 2])
    numbers = tiny("numbers", [P, 8])
    unit_no = tiny("unit_no", [P, SLOT_UNITS])
    unit_of = tiny("unit_of", [P, SLOT_UNITS])
    total = tiny("total", [P, 8])
    first = tiny("first", [P, 8])
    after = tiny("after", [P, 8])
    g.place_of = tiny("place_of", [P, 2, NT], U32)
    g.share = tiny("share", [P, 2, NT])
    g.expert_of = tiny("expert_of", [P, UNITS], I32)
    row = g.c_ssq
    g.w_loaded = g.semaphores(*(f"w_loaded{i}" for i in range(RAW)))
    g.w_hi_done, g.w_lo_done, g.rows_stored = g.semaphores("w_hi_done1", "w_lo_done1", "rows_stored")
    ld_x = g.semaphores("ld_x_even", "ld_x_odd")
    (h_sum, rows_pe, x1_done, norm_done, cols_pe, hi_done, lo_done, logit_pe, max_done, exp_done,
     taken_done, rank_pe, consts, tri_zero) = g.semaphores(
        "h_sum", "rows_pe", "x1_done", "norm_done", "cols_pe", "hi_done1", "lo_done1", "logit_pe",
        "max_done", "exp_done", "taken_done", "rank_pe", "consts", "tri_zero")
    low, high = g.psum
    flat = lambda x: x.rearrange("p a b -> p (a b)")

    with nc.Block() as block:
        @block.sync
        def _(sp):
            for c in range(NC):
                if c >= 2:
                    sp.wait_ge(x1_done, c - 1)
                sp.dma_start(x_in[:, c % 2], a["x"][c * CW:(c + 1) * CW, :].rearrange("(t p) d -> p t d", p=P)
                             ).then_inc(ld_x[c % 2], 16)
                for i in range(2 * c, 2 * c + 2):
                    weight_piece(nc, a, sp, "load", g, 0, 0, piece_cols(i), i)
            for c in range(NC):
                sp.wait_ge(norm_done, c + 1)
                sp.dma_start(g.in_dram[c * CW:(c + 1) * CW, :].rearrange("(t p) d -> p t d", p=P),
                             g.xn[:, c * TPC:(c + 1) * TPC, :]).then_inc(g.rows_stored, 16)

        @block.gpsimd
        def _(pool):
            for e in range(8):
                nc.gpsimd.memset(numbers[:, e:e + 1], float(e)).then_inc(consts, 1)
            for u in range(SLOT_UNITS):
                nc.gpsimd.memset(unit_no[:, u:u + 1], float(u)).then_inc(consts, 1)
            nc.gpsimd.memset(tri[:], 1.0).then_inc(tri_zero, 1)
            pool.wait_ge(tri_zero, 1)
            nc.gpsimd.affine_select(out=tri[:], in_=tri[:], compare_op=ALU.is_gt, fill=0.0,
                                    base=0, pattern=[[1, P]], channel_multiplier=-1).then_inc(consts, 1)

        @block.scalar
        def _(act):
            for c in range(NC):
                act.wait_ge(cols_pe, c + 1)
                if c >= 2:
                    act.wait_ge(logit_pe, (c - 1) * TPC)
                nc.scalar.activation(xn_hi[:, c % 2], high[:, 0:DH, :], ACT.Copy).then_inc(hi_done, 1)
                for i in range(2 * c, 2 * c + 2):
                    weight_piece(nc, a, act, "high", g, 0, 0, piece_cols(i), i)
            act.wait_ge(max_done, 1)
            nc.scalar.activation(flat(probs[:, :, 0:8]), flat(probs[:, :, 0:8]), ACT.Exp).then_inc(exp_done, 1)

        @block.vector
        def _(dve):
            def slots(c):
                if c >= 2:
                    dve.wait_ge(rows_pe, c - 1)
                cs = slice(c * CW, (c + 1) * CW)
                nc.vector.tensor_tensor(h32[:, c % 2], g.h_hi[:, :, cs].bitcast(F32), g.h_lo[:, :, cs].bitcast(F32),
                                        ALU.add).then_inc(h_sum, 1)

            slots(0)
            for c in range(NC):
                if c + 1 < NC:
                    slots(c + 1)
                dve.wait_ge(ld_x[c % 2], 16 * (c // 2 + 1))
                dve.wait_ge(rows_pe, c + 1)
                x1 = g.x1[:, c * TPC:(c + 1) * TPC, :]
                nc.vector.scalar_tensor_tensor(flat(x1), flat(low[:, 2 * (c % 2):2 * (c % 2) + 2, :]), g.tg_x[:],
                                               flat(x_in[:, c % 2]), ALU.mult, ALU.add).then_inc(x1_done, 1)
                dve.drain()
                for i in range(TPC):
                    nc.vector.bn_stats(stats[:, i, :], x1[:, i, :])
                dve.drain()
                mv = g.mean_var[:, c * TPC:(c + 1) * TPC, :]
                for i in range(TPC):
                    nc.vector.bn_aggr(mv[:, i, :], stats[:, i, :])
                dve.drain()
                nc.vector.tensor_scalar(g.nx[:, 0:TPC], mv[:, :, 1], EPS_LN, None, ALU.add)
                rsqrt(nc, dve, g, g.ny[:, 0:TPC], g.nx[:, 0:TPC], TPC)
                for i in range(TPC):
                    ins = nc.vector.tensor_scalar(g.xn[:, c * TPC + i, :], x1[:, i, :], mv[:, i, 0:1], g.ny[:, i:i + 1],
                                                  ALU.subtract, ALU.mult)
                ins.then_inc(norm_done, 1)
                for i in range(2 * c, 2 * c + 2):
                    weight_piece(nc, a, dve, "low", g, 0, 0, piece_cols(i), i)
                dve.wait_ge(hi_done, c + 1)
                nc.vector.tensor_tensor(xn_lo[:, c % 2], high[:, 0:DH, :], xn_hi[:, c % 2].bitcast(F32),
                                        ALU.subtract).then_inc(lo_done, 1)
            dve.wait_ge(logit_pe, NT)
            logits = high[:, 2, 0:NT * 8].rearrange("p (t e) -> p t e", e=8)
            valid = probs[:, :, 0:ROUTED]

            def wide(x):
                return x.unsqueeze(2).broadcast_to([P, NT, ROUTED])

            nc.vector.memset(probs[:], 0.0)
            nc.vector.reduce_max(row[:], logits[:, :, 0:ROUTED], AX.X)
            dve.drain()
            nc.vector.tensor_tensor(valid, logits[:, :, 0:ROUTED], wide(row[:]), ALU.subtract).then_inc(max_done, 1)
            dve.wait_ge(exp_done, 1)
            nc.vector.reduce_sum(row[:], valid, AX.X)
            dve.drain()
            nc.vector.reciprocal(g.ny[:], row[:])
            dve.drain()
            nc.vector.tensor_tensor(valid, valid, wide(g.ny[:]), ALU.mult)
            nc.vector.memset(probs[:, :, ROUTED:8], -1.0)
            dve.drain()
            for t in range(NT):
                nc.vector.max(best[:, t, :], probs[:, t, :])
            dve.drain()
            for t in range(NT):
                nc.vector.max_index(best_at[:, t, :], best[:, t, :], probs[:, t, :])
            nc.vector.tensor_tensor(row[:], best[:, :, 0], best[:, :, 1], ALU.add)
            dve.drain()
            nc.vector.tensor_copy(where[:], best_at[:, :, 0:2])
            dve.wait_ge(consts, 8 + SLOT_UNITS + 1)
            dve.drain()
            chosen = [chosen0[:, :, 0:ROUTED], chosen1[:, :, 0:ROUTED]]
            for k in range(2):
                nc.vector.tensor_tensor(chosen[k], numbers[:, 0:ROUTED].unsqueeze(1).broadcast_to([P, NT, ROUTED]),
                                        wide(where[:, :, k]), ALU.is_equal)
            dve.drain()
            nc.vector.tensor_tensor(taken[:, :, 0:ROUTED], chosen[0], chosen[1], ALU.add).then_inc(taken_done, 1)
            nc.vector.tensor_scalar(row[:], row[:], EPS_TOP, 2.0, ALU.add, ALU.mult)
            dve.drain()
            nc.vector.reciprocal(g.ny[:], row[:])
            dve.drain()
            for k in range(2):
                nc.vector.scalar_tensor_tensor(g.share[:, k, :], best[:, :, k], g.tg_f[:], g.ny[:], ALU.mult, ALU.mult)
            dve.wait_ge(rank_pe, 1)
            counts = low[:, 1, 0:NT * ROUTED].rearrange("p (t e) -> p t e", e=ROUTED)
            ranks = low[:, 0, 0:NT * ROUTED].rearrange("p (t e) -> p t e", e=ROUTED)
            nc.vector.memset(before[:, 0, :], 0.0)
            nc.vector.memset(first[:], 0.0)
            nc.vector.memset(after[:], 0.0)
            for t in range(1, NT + 1):
                dve.drain()
                dst = before[:, t, 0:ROUTED] if t < NT else total[:, 0:ROUTED]
                nc.vector.tensor_tensor(dst, before[:, t - 1, 0:ROUTED], counts[:, t - 1, :], ALU.add)
            for j in range(NC):
                dve.drain()
                nc.vector.scalar_tensor_tensor(after[:, 0:ROUTED], total[:, 0:ROUTED], float(j * CW), after[:, 0:ROUTED],
                                               ALU.is_gt, ALU.add)
            for e in range(1, ROUTED):
                dve.drain()
                nc.vector.tensor_tensor(after[:, e:e + 1], after[:, e - 1:e], after[:, e:e + 1], ALU.add)
            dve.drain()
            nc.vector.tensor_scalar(first[:, 1:ROUTED], after[:, 0:ROUTED - 1], float(CW), None, ALU.mult)
            dve.drain()
            nc.vector.tensor_scalar(first[:], first[:], float(S), None, ALU.add)
            nc.vector.tensor_tensor(before[:, :, 0:ROUTED], before[:, :, 0:ROUTED], ranks, ALU.add)
            dve.drain()
            nc.vector.tensor_tensor(before[:, :, 0:ROUTED], before[:, :, 0:ROUTED],
                                    first[:, 0:ROUTED].unsqueeze(1).broadcast_to([P, NT, ROUTED]), ALU.add)
            dve.drain()
            for k in range(2):
                nc.vector.tensor_tensor(pos[:, :, 0:ROUTED], before[:, :, 0:ROUTED], chosen[k], ALU.mult)
                dve.drain()
                nc.vector.reduce_sum(row[:], pos[:, :, 0:ROUTED], AX.X)
                dve.drain()
                nc.vector.tensor_copy(g.place_of[:, k, :], row[:])
                dve.drain()
            nc.vector.memset(unit_of[:], 0.0)
            for e in range(ROUTED - 1):
                dve.drain()
                nc.vector.scalar_tensor_tensor(unit_of[:], unit_no[:], after[:, e:e + 1], unit_of[:], ALU.is_ge, ALU.add)
            nc.vector.memset(g.expert_of[:, 0:NC], 0)
            dve.drain()
            nc.vector.tensor_scalar(g.expert_of[:, NC:UNITS], unit_of[:], 1.0, None, ALU.add)
            dve.drain()

        @block.tensor
        def _(pe):
            def normalised(c):
                pe.wait_ge(norm_done, c + 1)
                if c:
                    pe.wait_ge(lo_done, c)
                for e in range(DH):
                    for i in range(TPC):
                        ins = nc.tensor.transpose(high[:, e, i * P:(i + 1) * P],
                                                  g.xn[:, c * TPC + i, e * P:(e + 1) * P], g.ident[:])
                ins.then_inc(cols_pe, 1)
                pe.wait_ge(lo_done, c + 1)
                for i in range(TPC):
                    t = c * TPC + i
                    ts = slice(i * P, (i + 1) * P)
                    for e in range(DH):
                        ins = split3(nc, high[:, 2, t * 8:(t + 1) * 8], xn_hi[:, c % 2, e, ts], xn_lo[:, c % 2, e, ts],
                                     g.rw_hi[:, e, :], g.rw_lo[:, e, :], e == 0, e == DH - 1)
                    ins.then_inc(logit_pe, 1)

            for c in range(NC):
                pe.wait_ge(h_sum, c + 1)
                if c >= 2:
                    pe.wait_ge(x1_done, c - 1)
                for i in range(TPC):
                    for e in range(DH):
                        ins = nc.tensor.transpose(low[:, 2 * (c % 2) + i // 2, (i % 2) * D + e * P:(i % 2) * D + (e + 1) * P],
                                                  h32[:, c % 2, e, i * P:(i + 1) * P], g.ident[:])
                ins.then_inc(rows_pe, 1)
                if c:
                    normalised(c - 1)
            normalised(NC - 1)
            pe.wait_ge(taken_done, 1)
            pe.wait_ge(x1_done, NC)
            nc.tensor.matmul(low[:, 0, 0:NT * ROUTED], tri[:], taken[:, :, 0:ROUTED], start=True, stop=True)
            nc.tensor.matmul(low[:, 1, 0:NT * ROUTED], g.ones[:], taken[:, :, 0:ROUTED], start=True, stop=True
                             ).then_inc(rank_pe, 1)


def experts(nc, a, g):
    t_g, act_g, hid, hid_hi, hid_lo = (g.place(n, [P, 2, CW], dt, g.tmp_at + i * 4096) for i, (n, dt) in enumerate(
        (("t_g", F32), ("act_g", F32), ("hid", F32), ("hid_hi", F32R), ("hid_lo", F32R))))
    x_hi = g.place("x_hi", [P, 2, DH, CW], F32R, g.h_at)
    x_lo = g.place("x_lo", [P, 2, DH, CW], F32R, g.h_at + 8192)
    y_cols = g.place("y_cols", [P, DH, CW], F32, g.h_at + 16384)
    x_rows = g.place("ex_rows", [P, 2, TPC, D], F32, g.h_at + 20480)
    y_rows = g.place("y_rows", [P, TPC, D], F32, g.h_at + 28672)
    TURNS = UNITS // 2
    STEPS = 2 * FT
    (gate_pe, up_pe, tanh_done, act_done, hid_done, hi_done, lo_done, down_pe, y_cols_done, y_rows_pe, y_rows_done,
     x_cols_pe, x_hi_done, x_lo_done, stored, scattered, began) = g.semaphores(
        "gate_pe", "up_pe", "tanh_done", "act_done", "hid_done", "hid_hi_done", "hid_lo_done", "down_pe",
        "y_cols_done", "y_rows_pe", "y_rows_done", "x_cols_pe", "x_hi_done", "x_lo_done", "stored", "scattered", "began")
    x_loaded = g.semaphores("x_loaded0", "x_loaded1")
    gates, outs = g.psum
    y_bank, turned = outs[:, 0:2, :], outs[:, 2:4, :]
    flat = lambda x: x.rearrange("p a b -> p (a b)")
    assert UNITS % 2 == 0

    def turns(eng, body):
        body(0, True, False)
        with eng.Fori(1, TURNS - 1) as n:
            body(n, False, False)
        body(TURNS - 1, False, True)

    def rows(dram, u):
        return dram[u * CW:(u + 1) * CW, :].rearrange("(t p) d -> p t d", p=P)

    with nc.Block() as block:
        @block.sync
        def _(sp):
            def load_rows(u):
                if u >= 2:
                    sp.wait_ge(x_cols_pe, u - 1)
                if u == NC:
                    sp.wait_ge(scattered, 16 * 2 * NT)
                sp.dma_start(x_rows[:, u % 2], rows(g.in_dram, u)).then_inc(x_loaded[u % 2], 16)

            sp.wait_ge(g.rows_stored, 16 * NC)
            load_rows(0)
            load_rows(1)
            for u in range(UNITS):
                if u + 1 < UNITS:
                    e = sp.value_load(g.expert_of[0:1, u + 1:u + 2], min_val=0, max_val=ROUTED)
                    for i in range(PIECES):
                        weight_piece(nc, a, sp, "load", g, 1 - u % 2, e, piece_cols(i), PIECES * (u + 1) + i)
                        if i == 5 and u:
                            sp.wait_ge(y_rows_done, u)
                            sp.dma_start(rows(g.out_dram, u - 1), y_rows[:]).then_inc(stored, 16)
                        if i == 6 and 1 <= u < UNITS - 1:
                            load_rows(u + 1)
            for u in range(UNITS - 2, UNITS):
                sp.wait_ge(y_rows_done, u + 1)
                sp.dma_start(rows(g.out_dram, u), y_rows[:]).then_inc(stored, 16)
            sp.wait_ge(stored, 16 * UNITS)

        @block.tensor
        def _(pe):
            def x_transposes(n, v):
                if not (isinstance(n, int) and 2 * n + v < 2):
                    pe.wait_ge(y_rows_done, 2 * n + v - 1)
                pe.wait_ge(x_loaded[v % 2], (n + v // 2) * 16 + 16)
                for e in range(DH):
                    for i in range(TPC):
                        ins = nc.tensor.transpose(turned[:, e, i * P:(i + 1) * P], x_rows[:, v % 2, i, e * P:(e + 1) * P],
                                                  g.ident[:])
                ins.then_inc(x_cols_pe, 1)

            def y_transposes(n, v, last=False):
                pe.wait_ge(y_cols_done, 2 * n + v + 1)
                if not last:
                    pe.wait_ge(x_lo_done, 2 * n + v + 2)
                for i in range(TPC):
                    for e in range(DH):
                        ins = nc.tensor.transpose(turned[:, i // 2, (i % 2) * D + e * P:(i % 2) * D + (e + 1) * P],
                                                  y_cols[:, e, i * P:(i + 1) * P], g.ident[:])
                ins.then_inc(y_rows_pe, 1)

            def down(n, k, started):
                w, f = k // FT % 2, k % FT
                pe.wait_ge(hi_done, n * STEPS + k + 1)
                pe.wait_ge(lo_done, n * STEPS + k + 1)
                if f == 0 and started:
                    pe.wait_ge(y_cols_done, 2 * n + k // FT)
                for e in range(DH):
                    cols = slice(DOWN_AT + f * D + e * P, DOWN_AT + f * D + (e + 1) * P)
                    ins = split3(nc, y_bank[:, e, :], g.w_hi[w][:, cols], g.w_lo[w][:, cols],
                                 hid_hi[:, k % 2, :], hid_lo[:, k % 2, :], f == 0, f == FT - 1)
                ins.then_inc(down_pe, 1)

            def up_or_gate(k, bank, first):
                w, f = k // FT, k % FT
                for e in range(DH):
                    cols = slice(first + e * DFF + f * P, first + e * DFF + (f + 1) * P)
                    ins = split3(nc, gates[:, bank, :], g.w_hi[w][:, cols], g.w_lo[w][:, cols],
                                 x_hi[:, w, e, :], x_lo[:, w, e, :], e == 0, e == DH - 1)
                return ins

            def body(n, begins, ends):
                for k in range(STEPS):
                    v, f = k // FT, k % FT
                    if f == 0:
                        pe.wait_ge(g.w_lo_done, (2 * n + v + 1) * PIECES)
                        pe.wait_ge(x_lo_done, 2 * n + v + 1)
                    if not (begins and k < 2):
                        pe.wait_ge(act_done, n * STEPS + k - 1)
                    up_or_gate(k, k % 2, 0).then_inc(gate_pe, 1)
                    if not (begins and k < 2):
                        pe.wait_ge(hid_done, n * STEPS + k - 1)
                    up_or_gate(k, 2 + k % 2, UP_AT).then_inc(up_pe, 1)
                    if k:
                        down(n, k - 1, not begins or v > 0)
                    elif not begins:
                        down(n - 1, STEPS - 1, True)
                    if f == 2 and not (begins and v == 0):
                        y_transposes(n + (v - 1) // 2, (v - 1) % 2)
                    if f == 4 and not (ends and v == 1):
                        x_transposes(n, v + 1)

            pe.wait_ge(x_loaded[0], 16)
            x_transposes(0, 0)
            turns(pe, body)
            down(TURNS - 1, STEPS - 1, True)
            y_transposes(TURNS - 1, 1, True)

        @block.scalar
        def _(act):
            def high(n, k):
                if not (isinstance(n, int) and n * STEPS + k < 2):
                    act.wait_ge(down_pe, n * STEPS + k - 1)
                act.wait_ge(hid_done, n * STEPS + k + 1)
                nc.scalar.activation(hid_hi[:, k % 2], hid[:, k % 2], ACT.Copy).then_inc(hi_done, 1)

            def take_y_cols(n, v, begins):
                act.wait_ge(down_pe, n * STEPS + (v + 1) * FT)
                if not begins:
                    act.wait_ge(y_rows_pe, 2 * n + v)
                nc.scalar.activation(y_cols[:], y_bank, ACT.Copy).then_inc(y_cols_done, 1)

            def take_y_rows(n, v, begins):
                act.wait_ge(y_rows_pe, 2 * n + v + 1)
                if not begins:
                    act.wait_ge(stored, (2 * n + v) * 16)
                nc.scalar.activation(flat(y_rows[:]), flat(turned), ACT.Copy).then_inc(y_rows_done, 1)

            def x_high(n, v):
                act.wait_ge(x_cols_pe, 2 * n + v + 1)
                nc.scalar.activation(x_hi[:, v % 2], turned, ACT.Copy).then_inc(x_hi_done, 1)

            def body(n, begins, ends):
                for k in range(STEPS):
                    v, f = k // FT, k % FT
                    if k:
                        high(n, k - 1)
                    elif not begins:
                        high(n - 1, STEPS - 1)
                    if not (begins and k < 2):
                        act.wait_ge(act_done, n * STEPS + k - 1)
                    act.wait_ge(gate_pe, n * STEPS + k + 1)
                    nc.scalar.activation(t_g[:, k % 2], gates[:, k % 2, :], ACT.Tanh, scale=0.5).then_inc(tanh_done, 1)
                    if f == 0 and not (begins and v == 0):
                        take_y_cols(n + (v - 1) // 2, (v - 1) % 2, begins)
                    if f == 3 and not (begins and v == 0):
                        take_y_rows(n + (v - 1) // 2, (v - 1) % 2, begins)
                    if not (ends and v == 1):
                        weight_piece(nc, a, act, "high", g, 1 - v, None, piece_cols(f), PIECES * (v + 1) + f,
                                     n * 2 * PIECES)
                        if f == 5:
                            x_high(n, v + 1)

            x_high(0, 0)
            turns(act, body)
            high(TURNS - 1, STEPS - 1)
            take_y_cols(TURNS - 1, 1, False)
            take_y_rows(TURNS - 1, 1, False)

        @block.vector
        def _(dve):
            def x_low(n, v):
                dve.wait_ge(x_hi_done, 2 * n + v + 1)
                nc.vector.tensor_tensor(x_lo[:, v % 2], turned, x_hi[:, v % 2].bitcast(F32), ALU.subtract
                                        ).then_inc(x_lo_done, 1)

            def body(n, begins, ends):
                for k in range(STEPS):
                    v, f = k // FT, k % FT
                    dve.wait_ge(tanh_done, n * STEPS + k + 1)
                    nc.vector.scalar_tensor_tensor(act_g[:, k % 2], t_g[:, k % 2], 1.0, gates[:, k % 2, :],
                                                   ALU.add, ALU.mult).then_inc(act_done, 1)
                    dve.drain()
                    if not (begins and k < 2):
                        dve.wait_ge(lo_done, n * STEPS + k - 1)
                    dve.wait_ge(up_pe, n * STEPS + k + 1)
                    nc.vector.tensor_tensor(hid[:, k % 2], act_g[:, k % 2], gates[:, 2 + k % 2, :], ALU.mult
                                            ).then_inc(hid_done, 1)
                    if not (ends and v == 1):
                        weight_piece(nc, a, dve, "low", g, 1 - v, None, piece_cols(f), PIECES * (v + 1) + f,
                                     n * 2 * PIECES)
                        if f == 5:
                            x_low(n, v + 1)

            x_low(0, 0)
            turns(dve, body)

        @block.gpsimd
        def _(pool):
            def scatter(i):
                k, t = i % 2, i // 2
                nc.gpsimd.indirect_dma_start(
                    g.in_dram[:, :], bass.IndirectOffsetOnAxis(ap=g.place_of[:, k, t:t + 1], axis=0),
                    g.xn[:, t, :], None).then_inc(scattered, 16)

            def body(n, begins, ends):
                for k in range(STEPS):
                    pool.wait_ge(hi_done, n * STEPS + k + 1)
                    nc.gpsimd.tensor_tensor(hid_lo[:, k % 2], hid[:, k % 2], hid_hi[:, k % 2].bitcast(F32),
                                            ALU.subtract).then_inc(lo_done, 1)
                    if begins:
                        scatter(2 * k)
                        scatter(2 * k + 1)

            pool.wait_ge(g.cleared, 16 * (D // P))
            turns(pool, body)


def finish(nc, out, g):
    DEPTH = 4
    y_in = g.place("y_in", [P, DEPTH, 3, D], F32, g.h_at)
    half = g.rz
    got = [g.semaphores(f"got{i}")[0] for i in range(DEPTH)]
    got_shared = [g.semaphores(f"got_shared{i}")[0] for i in range(DEPTH)]
    (res_done, stored) = g.semaphores("res_done", "stored_out")
    with nc.Block() as block:
        @block.gpsimd
        def _(pool):
            for t in range(NT):
                if t >= DEPTH:
                    pool.wait_ge(res_done, t - DEPTH + 1)
                for k in range(2):
                    nc.gpsimd.indirect_dma_start(
                        y_in[:, t % DEPTH, 1 + k, :], None, g.out_dram[:, :],
                        bass.IndirectOffsetOnAxis(ap=g.place_of[:, k, t:t + 1], axis=0)).then_inc(got[t % DEPTH], 16)

        @block.sync
        def _(sp):
            for t in range(NT):
                if t >= DEPTH:
                    sp.wait_ge(res_done, t - DEPTH + 1)
                sp.dma_start(y_in[:, t % DEPTH, 0, :], g.out_dram[t * P:(t + 1) * P, :]).then_inc(got_shared[t % DEPTH], 16)

        @block.vector
        def _(dve):
            nc.vector.tensor_scalar(half[:], g.tg_f[:], 0.5, None, ALU.mult)
            dve.drain()
            for t in range(NT):
                d = t % DEPTH
                res = g.x1[:, t, :]
                dve.wait_ge(got_shared[d], 16 * (t // DEPTH + 1))
                nc.vector.scalar_tensor_tensor(res, y_in[:, d, 0, :], half[:], res, ALU.mult, ALU.add)
                dve.wait_ge(got[d], 32 * (t // DEPTH + 1))
                for k in range(2):
                    dve.drain()
                    ins = nc.vector.scalar_tensor_tensor(res, y_in[:, d, 1 + k, :], g.share[:, k, t:t + 1], res,
                                                         ALU.mult, ALU.add)
                ins.then_inc(res_done, 1)

        @block.scalar
        def _(act):
            for t in range(NT):
                act.wait_ge(res_done, t + 1)
                act.dma_start(out[t * P:(t + 1) * P, :], g.x1[:, t, :]).then_inc(stored, 16)
            act.wait_ge(stored, 16 * NT)


def kernel(**inputs):
    import numpy as _np
    import concourse.bacc as _bacc
    from concourse import mybir as _mybir
    from concourse.bass_utils import run_bass_kernel_spmd as _run

    x = {k: _np.asarray(v) for k, v in inputs.items()}

    def halves(v):
        return v.reshape(-1, P).T

    def packed(gate, up, down):
        parts = [gate.T.reshape(DH, P, DFF), up.T.reshape(DH, P, DFF)]
        cols = [p.transpose(1, 0, 2).reshape(P, DH * DFF) for p in parts]
        cols.append(down.T.reshape(FT, P, D).transpose(1, 0, 2).reshape(P, FT * D))
        return _np.concatenate(cols, axis=1)

    w = [packed(x["L0_ffn_shared_gate"], x["L0_ffn_shared_up"], x["L0_ffn_shared_down"])]
    w += [packed(x["L0_ffn_routed_gate"][e], x["L0_ffn_routed_up"][e], x["L0_ffn_routed_down"][e])
          for e in range(ROUTED)]
    arrays = {
        "x": x["x"][0], "ctx": x["ctx_1024"][0],
        "g_xattn": _np.broadcast_to(x["g_xattn"].reshape(1, 1), (P, 1)),
        "g_ffn": _np.broadcast_to(x["g_ffn"].reshape(1, 1), (P, 1)),
        "wq": x["L0_xattn_Wq"], "wk": x["L0_xattn_Wk"], "wvT": x["L0_xattn_Wv"].T,
        "wihT": x["L0_xattn_gru_wih"].T, "whhT": x["L0_xattn_gru_whh"].T,
        "bih": halves(x["L0_xattn_gru_bih"]), "bhh": halves(x["L0_xattn_gru_bhh"]),
        "slot_norm_w": halves(x["L0_xattn_slot_norm_w"]), "input_norm_w": halves(x["L0_xattn_input_norm_w"]),
        "routerT": x["L0_ffn_router_w"].T, "w": _np.stack(w),
    }
    nc = _bacc.Bacc("TRN2", target_bir_lowering=False, num_devices=1)
    feeds, aps = {}, {}
    for name, v in arrays.items():
        v = _np.ascontiguousarray(v)
        feeds[f"in_{name}"] = v
        aps[name] = nc.dram_tensor(f"in_{name}", v.shape, _mybir.dt.from_np(v.dtype), kind="ExternalInput").ap()
    out = nc.dram_tensor("out", (S, D), _mybir.dt.float32, kind="ExternalOutput").ap()
    build_kernel(nc, aps, out)
    r = _run(nc, [feeds], core_ids=[0])
    return r.results[0]["out"].reshape(1, S, D)
```

```python
import concourse.bass as bass
from concourse import mybir
from contextlib import ExitStack

F32 = mybir.dt.float32
F32R = mybir.dt.float32r
I32 = mybir.dt.int32
U32 = mybir.dt.uint32
ALU = mybir.AluOpType
ACT = mybir.ActivationFunctionType
AX = mybir.AxisListType

P = 128
S = 2048
M = 1601
D = 256
DH = D // P
CW = 512
NC = S // CW
NT = S // P
TPC = CW // P
MT = -(-M // P)
MPAD = M + 1
ITERS = 3
EPS_NORM = 1e-6
EPS_ATTN = 1e-6
EPS_LN = 1e-5
EPS_TOP = 1e-9
SCALE = float(D) ** -0.5
DFF = 1024
FT = DFF // P
ROUTED = 7
WCOLS = 3 * DH * DFF
PIECE = 768
PIECES = WCOLS // PIECE
GATE_PIECES = -(-DH * DFF // PIECE)
UP_PIECES = -(-2 * DH * DFF // PIECE)
UW = 256
TPU = UW // P
HIDDEN = 4
SPLITS = 8
LAG = 3
POOL_PLACE = 2
RAW = 4
UP_AT, DOWN_AT = DH * DFF, 2 * DH * DFF
SLOT_UNITS = 2 * S // UW + ROUTED - 1
HEAD = S // UW - 1
UNITS = S // UW + SLOT_UNITS
PLACES = UNITS * UW
MAGIC = float(0x5F3759DF)


class Store:
    pass


def rows_of(t):
    return min(P, M - t * P)


BLOCKS = [(0, 1, 2), (3, 4, 5), (6, 7, 8), (9, 10), (11, 12)]
E_SLOTS = 6
E_SLOT = {t: 3 * (b % 2) + i for b, ts in enumerate(BLOCKS) for i, t in enumerate(ts)}
ITEMS = [(b, c) for b in range(len(BLOCKS)) for c in range(NC)]
AFTER = {3: [0], 4: [1], 5: [2, 3], 6: [4], 7: [5], 8: [6, 7], 9: [8], 10: [9, 10, 11],
         11: [12], 12: [13, 14, 15]}
TAIL = [16, 17, 18, 19]
PAIRS = [(i, t) for i, (b, _) in enumerate(ITEMS) for t in BLOCKS[b]]
PAIRS_OF = {i: [n for n, (k, _) in enumerate(PAIRS) if k == i] for i in range(len(ITEMS))}
NPAIR, NITEM = len(PAIRS), len(ITEMS)
OWN = NC - 2
RING = 4


def rsqrt(nc, dve, g, y, x, n):
    i, t, u = g.ni[:, 0:n], g.na[:, 0:n], g.nb[:, 0:n]
    dve.drain()
    nc.vector.tensor_scalar(i, x.bitcast(I32), 1, None, ALU.logical_shift_right)
    dve.drain()
    nc.vector.tensor_scalar(y.bitcast(I32), i, -1.0, MAGIC, ALU.mult, ALU.add)
    for _ in range(3):
        dve.drain()
        nc.vector.tensor_tensor(t, y, y, ALU.mult)
        dve.drain()
        nc.vector.scalar_tensor_tensor(u, t, -0.5, x, ALU.mult, ALU.mult)
        dve.drain()
        nc.vector.scalar_tensor_tensor(y, u, 1.5, y, ALU.add, ALU.mult)
    dve.drain()


def diagonal(nc, g, dst, col, n):
    return nc.vector.tensor_tensor(dst, g.ident[:].unsqueeze(1).broadcast_to([P, n, P]),
                                   col.unsqueeze(2).broadcast_to([P, n, P]), ALU.mult)


def split3(nc, dst, w_hi, w_lo, m_hi, m_lo, start, stop):
    nc.tensor.matmul(dst, w_hi, m_hi, start=start, stop=False)
    nc.tensor.matmul(dst, w_lo, m_hi, start=False, stop=False)
    return nc.tensor.matmul(dst, w_hi, m_lo, start=False, stop=stop)


def build_kernel(nc, a, out):
    g = Store()
    with ExitStack() as ctx:
        base = -(-nc.sbuf_base // 32) * 32

        def place(name, shape, dt, at):
            return nc.alloc_sbuf_tensor_at(name, shape, dt, offset=base + at)

        def semaphores(*names):
            return [ctx.enter_context(nc.semaphore(n)) for n in names]

        g.psum = [ctx.enter_context(nc.psum_tensor(f"quad{i}", [P, 4, CW], F32)) for i in range(2)]

        g.h_at = 0
        g.acc_at = g.h_at + 2 * DH * S * 4
        g.rstd_at = g.acc_at + DH * S * 4
        g.k_at = g.rstd_at + S * 4
        g.k_size = -(-DH * MPAD * 4 // 32) * 32
        g.v_at = g.k_at + 2 * g.k_size
        g.v_size = MT * D * 4
        g.gw_at = g.v_at + 2 * g.v_size
        g.gw_size = DH * 3 * D * 4
        g.e_at = g.gw_at + 4 * g.gw_size
        g.racc_at = g.e_at + E_SLOTS * S * 4
        g.ring_at = g.racc_at + S * 4
        g.small_at = g.ring_at + RING * 2 * CW * 4
        small = [g.small_at]

        def tiny(name, shape, dt=F32):
            at = small[0]
            n = 4
            for k in shape[1:]:
                n *= k
            small[0] += -(-n // 32) * 32
            return place(name, shape, dt, at)

        g.h_hi = place("h_hi", [P, DH, S], F32R, g.h_at)
        g.h_lo = place("h_lo", [P, DH, S], F32R, g.h_at + DH * S * 4)
        g.acc = place("acc", [P, DH, S], F32, g.acc_at)
        g.rstd_all = place("rstd_all", [P, S], F32, g.rstd_at)
        g.k_hi = place("k_hi", [P, DH, MPAD], F32R, g.k_at)
        g.k_lo = place("k_lo", [P, DH, MPAD], F32R, g.k_at + g.k_size)
        g.v_hi = place("v_hi", [P, MT, D], F32R, g.v_at)
        g.v_lo = place("v_lo", [P, MT, D], F32R, g.v_at + g.v_size)
        g.wih_hi, g.wih_lo, g.whh_hi, g.whh_lo = (
            place(n, [P, DH, 3 * D], F32R, g.gw_at + i * g.gw_size)
            for i, n in enumerate(("wih_hi", "wih_lo", "whh_hi", "whh_lo")))
        g.E = place("E", [P, E_SLOTS, S], F32, g.e_at)
        g.racc = place("racc", [P, S], F32, g.racc_at)
        g.ring_hi = place("ring_hi", [P, RING, CW], F32R, g.ring_at)
        g.ring_lo = place("ring_lo", [P, RING, CW], F32R, g.ring_at + RING * CW * 4)

        g.h_new = place("h_new", [P, 2, DH, CW], F32, g.e_at + (E_SLOTS - 1) * S * 4)

        g.ident = tiny("ident", [P, P])
        g.ones = tiny("ones", [P, P])
        g.tg_x = tiny("tg_x", [P, 1])
        g.tg_f = tiny("tg_f", [P, 1])
        g.bih = tiny("bih", [P, 3 * DH])
        g.bhh = tiny("bhh", [P, 3 * DH])
        g.b_gate = tiny("b_gate", [P, 2 * DH])
        g.w_in = tiny("w_in", [P, DH])
        g.w_slot = tiny("w_slot", [P, DH])
        g.k_scale = tiny("k_scale", [P, DH])
        g.rw_raw = tiny("rw_raw", [P, DH, 8])
        g.rw_hi = tiny("rw_hi", [P, DH, 8], F32R)
        g.rw_lo = tiny("rw_lo", [P, DH, 8], F32R)
        g.mean_var = tiny("mean_var", [P, NT, 2])
        g.rstd_col = tiny("rstd_col", [P, NT])
        g.nx = tiny("nx", [P, NT])
        g.ny = tiny("ny", [P, NT])
        g.na = tiny("na", [P, NT])
        g.nb = tiny("nb", [P, NT])
        g.ni = tiny("ni", [P, NT], I32)
        g.c_ssq = tiny("c_ssq", [P, NT])
        g.c_rstd = tiny("c_rstd", [P, NT])
        g.mx = tiny("mx", [P, 2, 2])
        g.neg_max = tiny("neg_max", [P, 2])
        g.zsum = tiny("zsum", [P, 2])
        g.rz = tiny("rz", [P, 1])
        g.zeros = tiny("zeros", [P, P])
        g.in_dram = nc.dram_tensor("expert_in", (PLACES, D), F32).ap()
        g.out_dram = nc.dram_tensor("expert_out", (PLACES, D), F32).ap()
        g.cleared = semaphores("cleared")[0]

        g.place, g.semaphores, g.tiny = place, semaphores, tiny
        prepare(nc, a, g)
        attention(nc, g)
        handover(nc, a, g)
        experts(nc, a, out, g)


def prepare(nc, a, g):
    place, semaphores, psum = g.place, g.semaphores, g.psum
    E_AT, ACC_AT, RACC_AT, RING_AT = g.e_at, g.acc_at, g.racc_at, g.ring_at
    ident, ones = g.ident, g.ones
    h_hi, h_lo, k_hi, k_lo, v_hi, v_lo = g.h_hi, g.h_lo, g.k_hi, g.k_lo, g.v_hi, g.v_lo
    mean_var, rstd_col, c_ssq, c_rstd, nx = g.mean_var, g.rstd_col, g.c_ssq, g.c_rstd, g.nx

    x_rows = place("x_rows", [P, NT, D], F32, ACC_AT)
    at = E_AT
    ctx_rows = place("ctx_rows", [P, MT, D], F32, at)
    at += MT * D * 4
    p_hi = place("p_hi", [P, DH, MPAD], F32R, at)
    at += g.k_size
    p_lo = place("p_lo", [P, DH, MPAD], F32R, at)
    at += g.k_size
    wv_hi = place("wv_hi", [P, DH, D], F32R, g.rstd_at + 4096)
    wv_lo = place("wv_lo", [P, DH, D], F32R, g.rstd_at + 6144)
    kq_hi = place("kq_hi", [P, DH, D], F32R, RING_AT + 12288)
    kq_lo = place("kq_lo", [P, DH, D], F32R, RING_AT + 14336)
    wih = place("wih_raw", [P, DH, 3 * D], F32, RING_AT)
    whh = place("whh_raw", [P, DH, 3 * D], F32, RING_AT + 6144)
    wq = place("wq_raw", [P, DH, D], F32, RACC_AT)
    wk = place("wk_raw", [P, DH, D], F32, RACC_AT + 2048)
    wv = place("wv_raw", [P, DH, D], F32, RACC_AT + 4096)
    diag = place("diag0", [P, TPC, P], F32, RACC_AT + 6144)
    ln_stats = place("ln_stats", [P, NT, 6], F32, RACC_AT + 6144)
    junk = place("junk0", [P, D], F32, g.rstd_at)

    (ld_w, ld_wv, ld_small, ld_gw, const0, const1, sq_done, c_norm, ln_even, ln_odd, mean_rstd, p_zero, w_hi_done,
     w_lo_done, kq_in, job_pe, job_hi, job_done, dg_done, spread_pe, spread_done, zeroed) = semaphores(
        "ld_w", "ld_wv", "ld_small", "ld_gw", "const0", "const1", "sq_done", "c_norm", "ln_even", "ln_odd",
        "mean_rstd", "p_zero", "w_hi_done", "w_lo_done", "kq_in", "job_pe", "job_hi", "job_done",
        "dg_done", "spread_pe", "spread_done", "zeroed")
    ld_x = semaphores(*(f"ld_x_rows{c}" for c in range(NC)))
    ld_ctx = semaphores(*(f"ld_ctx{c}" for c in range(NC)))

    jobs = [("kq", 0, ch) for ch in range(DH)]
    jobs += [("slot", c, dh) for c in range(NC) for dh in range(DH)]
    jobs += [("ctx", m, dh) for m in range(NC) for dh in range(DH)]
    KEYS_AT = len(jobs)
    jobs += [("key", m, dh) for m in range(NC) for dh in range(DH)]
    jobs += [("value", t, 0) for t in range(MT)]

    def width(m, even=False):
        w = min(CW, M - m * CW)
        return w + (w % 2 if even else 0)

    def bank(n):
        return psum[n % 8 // 4][:, n % 4, :]

    def source(n):
        kind, m, dh = jobs[n]
        if kind == "value":
            return bank(n)[0:rows_of(m), 0:D]
        if kind == "kq":
            return bank(n)[:, 0:D]
        return bank(n)[:, 0:{"slot": CW, "ctx": width(m), "key": width(m, True)}[kind]]

    def target(n):
        kind, m, dh = jobs[n]
        if kind == "slot":
            return tuple(h[:, dh, m * CW:(m + 1) * CW] for h in (h_hi, h_lo))
        if kind == "ctx":
            return tuple(p[:, dh, m * CW:m * CW + width(m)] for p in (p_hi, p_lo))
        if kind == "kq":
            return kq_hi[:, dh, :], kq_lo[:, dh, :]
        if kind == "value":
            return v_hi[0:rows_of(m), m, :], v_lo[0:rows_of(m), m, :]
        return tuple(k[:, dh, m * CW:m * CW + width(m, True)] for k in (k_hi, k_lo))

    def factor(n):
        kind, _, dh = jobs[n]
        return {"ctx": g.w_in, "key": g.k_scale}[kind][:, dh:dh + 1] if kind in ("ctx", "key") else None

    def normalise(ops, t):
        return ops.tensor_scalar(x_rows[:, t, :], x_rows[:, t, :], mean_var[:, t, 0:1], rstd_col[:, t:t + 1],
                                 ALU.subtract, ALU.mult)

    with nc.Block() as block:
        @block.sync
        def _(sp):
            for c in range(NC):
                sp.dma_start(x_rows[:, c * TPC:(c + 1) * TPC, :], a["x"][c * CW:(c + 1) * CW, :].rearrange(
                    "(t p) d -> p t d", p=P)).then_inc(ld_x[c], 16)
            for dst, name in ((wk, "wk"), (wq, "wq")):
                sp.dma_start(dst[:], a[name].rearrange("(h p) d -> p h d", p=P)).then_inc(ld_w, 16)
            last = MT - 1
            for c in range(NC - 1):
                sp.dma_start(ctx_rows[:, c * TPC:(c + 1) * TPC, :], a["ctx"][c * CW:(c + 1) * CW, :].rearrange(
                    "(t p) d -> p t d", p=P)).then_inc(ld_ctx[c], 16)
            sp.dma_start(ctx_rows[0:rows_of(last), last, :], a["ctx"][last * P:M, :]).then_inc(ld_ctx[NC - 1], 16)
            sp.dma_start(wv[:], a["wvT"].rearrange("(h p) d -> p h d", p=P)).then_inc(ld_wv, 16)
            for dst, name in ((wih, "wihT"), (whh, "whhT")):
                sp.dma_start(dst[:], a[name].rearrange("(h p) d -> p h d", p=P)).then_inc(ld_gw, 16)
            sp.wait_ge(zeroed, 1)
            for h in range(D // P):
                n = SLOT_UNITS * UW // P
                sp.dma_start(g.in_dram[HEAD * UW:PLACES - UW, h * P:(h + 1) * P].rearrange("(t p) d -> p t d", p=P),
                             g.zeros[:].unsqueeze(1).broadcast_to([P, n, P])).then_inc(g.cleared, 16)

        @block.gpsimd
        def _(pool):
            nc.gpsimd.memset(ident[:], 0.0).then_inc(const0, 1)
            nc.gpsimd.memset(ones[:], 1.0).then_inc(const1, 1)
            nc.gpsimd.memset(g.zeros[:], 0.0).then_inc(zeroed, 1)
            nc.gpsimd.memset(g.rw_raw[:], 0.0).then_inc(const1, 1)
            pool.wait_ge(const0, 1)
            nc.gpsimd.affine_select(out=ident[:], in_=ident[:], compare_op=ALU.not_equal, fill=1.0,
                                    base=0, pattern=[[-1, P]], channel_multiplier=1).then_inc(const1, 1)
            pool.wait_ge(mean_rstd, 1)
            for t in range(1, NT, 2):
                normalise(nc.gpsimd, t).then_inc(ln_odd, 1)
            for i, (raw, hi, lo) in enumerate(((wv, wv_hi, wv_lo), (wih, g.wih_hi, g.wih_lo),
                                               (whh, g.whh_hi, g.whh_lo))):
                pool.wait_ge(w_hi_done, 2 + i)
                nc.gpsimd.tensor_tensor(lo[:], raw[:], hi[:].bitcast(F32), ALU.subtract).then_inc(w_lo_done, 1)

        @block.scalar
        def _(act):
            for dst, name in ((g.w_in, "input_norm_w"), (g.w_slot, "slot_norm_w"), (g.bih, "bih"),
                              (g.bhh, "bhh"), (g.tg_x, "g_xattn"), (g.tg_f, "g_ffn")):
                act.dma_start(dst[:], a[name]).then_inc(ld_small, 16)
            act.wait_ge(const1, 3)
            act.dma_start(g.rw_raw[:, :, 0:ROUTED], a["routerT"].rearrange("(h p) e -> p h e", p=P)
                          ).then_inc(ld_small, 16)
            for t in range(MT):
                act.wait_ge(ld_ctx[t // TPC], 16)
                if t:
                    act.drain()
                r = rows_of(t)
                nc.scalar.activation(junk[0:r, :], ctx_rows[0:r, t, :], ACT.Square,
                                     accum_out=c_ssq[0:r, t:t + 1]).then_inc(sq_done, 1)
            act.wait_ge(ld_small, 16 * 7)
            act.drain()
            for t in (g.tg_x, g.tg_f):
                nc.scalar.activation(t[:], t[:], ACT.Tanh)
            nc.scalar.activation(g.rw_hi[:], g.rw_raw[:], ACT.Copy).then_inc(w_hi_done, 1)
            for n in range(len(jobs)):
                kind, m, dh = jobs[n]
                if n == KEYS_AT - 2:
                    act.wait_ge(ld_wv, 16)
                    nc.scalar.activation(wv_hi[:], wv[:], ACT.Copy).then_inc(w_hi_done, 1)
                if n == KEYS_AT:
                    act.wait_ge(ld_gw, 32)
                    nc.scalar.activation(g.wih_hi[:], wih[:], ACT.Copy).then_inc(w_hi_done, 1)
                    nc.scalar.activation(g.whh_hi[:], whh[:], ACT.Copy).then_inc(w_hi_done, 1)
                act.wait_ge(job_pe, n + 1)
                if kind == "slot" and m >= OWN:
                    nc.scalar.activation(g.h_new[:, m % 2, dh, :], source(n), ACT.Copy)
                if factor(n) is None:
                    nc.scalar.activation(target(n)[0], source(n), ACT.Copy).then_inc(job_hi, 1)
                else:
                    if kind == "key":
                        act.wait_ge(kq_in, 1)
                    nc.scalar.activation(target(n)[0], source(n), ACT.Copy, scale=factor(n)).then_inc(job_hi, 1)
            for c in range(OWN):
                act.wait_ge(spread_pe, c + 1)
                nc.scalar.activation(g.rstd_all[:, c * CW:(c + 1) * CW], bank(len(jobs) + c), ACT.Copy
                                     ).then_inc(spread_done, 1)

        @block.vector
        def _(dve):
            for p in (p_hi, p_lo):
                nc.vector.memset(p[:, :, M:MPAD].bitcast(F32), 0.0).then_inc(p_zero, 1)
            for c in range(NC):
                dve.wait_ge(ld_x[c], 16)
                for t in range(c * TPC, (c + 1) * TPC):
                    nc.vector.bn_stats(ln_stats[:, t, :], x_rows[:, t, :])
            dve.drain()
            for t in range(NT):
                nc.vector.bn_aggr(mean_var[:, t, :], ln_stats[:, t, :])
            dve.drain()
            nc.vector.tensor_scalar(nx[:], mean_var[:, :, 1], EPS_LN, None, ALU.add)
            rsqrt(nc, dve, g, rstd_col[:], nx[:], NT)
            dve.sem_inc(mean_rstd, 1)
            for t in range(0, NT, 2):
                normalise(nc.vector, t).then_inc(ln_even, 1)
            dve.wait_ge(sq_done, MT)
            last = rows_of(MT - 1)
            nc.vector.memset(nx[:], 1.0)
            dve.drain()
            nc.vector.tensor_scalar(nx[:, 0:MT - 1], c_ssq[:, 0:MT - 1], 1.0 / D, EPS_NORM, ALU.mult, ALU.add)
            nc.vector.tensor_scalar(nx[0:last, MT - 1:MT], c_ssq[0:last, MT - 1:MT], 1.0 / D, EPS_NORM,
                                    ALU.mult, ALU.add)
            rsqrt(nc, dve, g, c_rstd[:, 0:MT], nx[:, 0:MT], MT)

            def low_part(n):
                dve.wait_ge(job_hi, n + 1)
                hi, lo = target(n)
                if factor(n) is None:
                    nc.vector.tensor_tensor(lo, source(n), hi.bitcast(F32), ALU.subtract).then_inc(job_done, 1)
                else:
                    nc.vector.scalar_tensor_tensor(lo, source(n), factor(n), hi.bitcast(F32), ALU.mult, ALU.subtract
                                                   ).then_inc(job_done, 1)

            dve.wait_ge(ld_small, 16 * 7)
            nc.vector.tensor_scalar(g.k_scale[:], g.w_slot[:], SCALE, None, ALU.mult).then_inc(kq_in, 1)
            nc.vector.tensor_tensor(g.b_gate[:], g.bih[:, 0:2 * DH], g.bhh[:, 0:2 * DH], ALU.add)
            dve.drain()
            nc.vector.tensor_scalar(g.b_gate[:], g.b_gate[:], 0.5, None, ALU.mult)
            dve.wait_ge(w_hi_done, 1)
            nc.vector.tensor_tensor(g.rw_lo[:], g.rw_raw[:], g.rw_hi[:].bitcast(F32), ALU.subtract)
            for n in range(len(jobs)):
                if jobs[n][0] == "slot":
                    k = n - DH
                    for t in range(MT * k // (NC * DH), MT * (k + 1) // (NC * DH)):
                        r = rows_of(t)
                        nc.vector.tensor_scalar(ctx_rows[0:r, t, :], ctx_rows[0:r, t, :], c_rstd[0:r, t:t + 1], None,
                                                ALU.mult).then_inc(c_norm, 1)
                low_part(n)
                if n == KEYS_AT:
                    own = OWN * TPC
                    nc.vector.tensor_tensor(c_ssq[:, 0:own], rstd_col[:, 0:own], rstd_col[:, 0:own], ALU.mult)
                    dve.drain()
                    nc.vector.tensor_tensor(c_ssq[:, 0:own], c_ssq[:, 0:own], mean_var[:, 0:own, 1], ALU.mult)
                    dve.drain()
                    nc.vector.tensor_scalar(nx[:, 0:own], c_ssq[:, 0:own], EPS_NORM, None, ALU.add)
                    rsqrt(nc, dve, g, rstd_col[:, 0:own], nx[:, 0:own], own)
            for c in range(OWN):
                if c:
                    dve.wait_ge(spread_pe, c)
                diagonal(nc, g, diag[:], rstd_col[:, c * TPC:(c + 1) * TPC], TPC).then_inc(dg_done, 1)
            dve.drain()

        @block.tensor
        def _(pe):
            pe.wait_ge(const1, 3)
            for n, (kind, m, dh) in enumerate(jobs):
                b = bank(n)
                if n >= 8:
                    pe.wait_ge(job_done, n - 7)
                if kind == "ctx":
                    tiles = range(m * TPC, min((m + 1) * TPC, MT))
                    pe.wait_ge(c_norm, tiles[-1] + 1)
                    for i, t in enumerate(tiles):
                        r = rows_of(t)
                        ins = nc.tensor.transpose(b[:, i * P:i * P + r], ctx_rows[0:r, t, dh * P:(dh + 1) * P],
                                                  ident[0:r, 0:r])
                elif kind == "slot":
                    pe.wait_ge(ln_even, (m + 1) * TPC // 2)
                    pe.wait_ge(ln_odd, (m + 1) * TPC // 2)
                    for i in range(TPC):
                        ins = nc.tensor.transpose(b[:, i * P:(i + 1) * P],
                                                  x_rows[:, m * TPC + i, dh * P:(dh + 1) * P], ident[:])
                elif kind == "kq":
                    pe.wait_ge(ld_w, 32)
                    for e in range(DH):
                        ins = nc.tensor.matmul(b[:, 0:D], wk[:, e, dh * P:(dh + 1) * P], wq[:, e, :],
                                               start=(e == 0), stop=(e == DH - 1))
                elif kind == "key":
                    pe.wait_ge(job_done, KEYS_AT)
                    pe.wait_ge(p_zero, 2)
                    w = width(m, True)
                    for e in range(DH):
                        ins = split3(nc, b[:, 0:w], kq_hi[:, e, dh * P:(dh + 1) * P], kq_lo[:, e, dh * P:(dh + 1) * P],
                                     p_hi[:, e, m * CW:m * CW + w], p_lo[:, e, m * CW:m * CW + w],
                                     e == 0, e == DH - 1)
                else:
                    pe.wait_ge(w_lo_done, 1)
                    r = rows_of(m)
                    for e in range(DH):
                        ins = split3(nc, b[0:r, 0:D], p_hi[:, e, m * P:m * P + r], p_lo[:, e, m * P:m * P + r],
                                     wv_hi[:, e, :], wv_lo[:, e, :], e == 0, e == DH - 1)
                ins.then_inc(job_pe, 1)
            for c in range(OWN):
                pe.wait_ge(job_done, len(jobs) + c - 7)
                pe.wait_ge(dg_done, c + 1)
                nc.tensor.matmul(bank(len(jobs) + c), ones[:], diag[:].rearrange("p a b -> p (a b)"),
                                 start=True, stop=True).then_inc(spread_pe, 1)


def attention(nc, g):
    place = g.place
    h_hi, h_lo, acc, rstd_all, k_hi, k_lo, v_hi, v_lo, E, racc, ring_hi, ring_lo = (
        g.h_hi, g.h_lo, g.acc, g.rstd_all, g.k_hi, g.k_lo, g.v_hi, g.v_lo, g.E, g.racc, g.ring_hi, g.ring_lo)
    scores, sums = g.psum
    mx, neg_max, zsum, rz, ones = g.mx, g.neg_max, g.zsum, g.rz, g.ones
    slot = lambda s: g.e_at + s * S * 4
    u_hi = place("u_hi", [P, 2, DH, CW], F32R, slot(2))
    u_lo = place("u_lo", [P, 2, DH, CW], F32R, slot(3))
    r_diag = place("r_diag", [P, NC, TPC, P], F32, slot(4))
    sq = place("sq", [P, 2, DH, CW], F32, slot(4))
    n_diag2 = place("n_diag2", [P, 2, TPC, P], F32, slot(3))
    h_new = g.h_new
    n_diag = place("n_diag", [P, TPC, P], F32, slot(4) + 4096)
    t_r = place("t_r", [P, 2, CW], F32, slot(0))
    t_z = place("t_z", [P, 2, CW], F32, slot(0) + 4096)
    n_in = place("n_in", [P, 2, CW], F32, slot(1))
    n_out = place("n_out", [P, 2, CW], F32, slot(1) + 4096)
    h_half = place("h_half", [P, 2, CW], F32, g.ring_at)
    rsum = g.c_ssq
    rinv = g.c_rstd

    (score_pe, drained, nmax, exped, scaled, rsummed, hi_done, lo_done, pair_pe, item_done, rs_pe, rdiag_done,
     rspread_pe, rinv_done, u_done, u_hi_done, u_lo_done, hn_pe, r_pe, z_pe, xn_pe, tr_done, tz_done, n_in_done,
     n_done, half_done, hn_read, h_done, h_hi_done, h_lo_done, sq_done, ss_pe, ndiag_done, nspread_pe, rstd_done, seen
     ) = g.semaphores(
        "score_pe", "drained", "nmax", "exped", "scaled_e", "rsummed", "hi_done", "lo_done", "pair_pe", "item_done",
        "rs_pe", "rdiag_done", "rspread_pe", "rinv_done", "u_done", "u_hi_done", "u_lo_done", "hn_pe", "r_pe",
        "z_pe", "xn_pe", "tr_done", "tz_done", "n_in_done", "n_done", "half_done", "hn_read", "h_done", "h_hi_done",
        "h_lo_done", "sq_done1", "ss_pe", "ndiag_done", "nspread_pe", "rstd_done", "seen")
    GRU = NC * DH

    def chunk(c):
        return slice(c * CW, (c + 1) * CW)

    def nth(c):
        return (c - OWN) % NC + 1

    def sq_at(c):
        return int(c == NC - 1)

    def pairs_until(item):
        return PAIRS_OF[item][-1] + 1

    def last_use(t):
        return max(n for n, (_, k) in enumerate(PAIRS) if k == t) + 1

    def staged(t, n):
        pairs = [k for i in AFTER.get(t, []) for k in PAIRS_OF[i]]
        return pairs[:n], pairs[n:]

    def before_in_slot(t):
        return max((k for k in range(t) if E_SLOT[k] == E_SLOT[t]), default=None)

    with nc.Block() as block:
        @block.tensor
        def _(pe):
            def item(i, it):
                b, c = ITEMS[i]
                if i >= 2:
                    pe.wait_ge(item_done, it * NITEM + i - 1)
                for n in PAIRS_OF[i]:
                    t = PAIRS[n][1]
                    r = rows_of(t)
                    pe.wait_ge(hi_done, it * NPAIR + n + 1)
                    pe.wait_ge(lo_done, it * NPAIR + n + 1)
                    for dh in range(DH):
                        ins = split3(nc, sums[:, 2 * (i % 2) + dh, :], v_hi[0:r, t, dh * P:(dh + 1) * P],
                                     v_lo[0:r, t, dh * P:(dh + 1) * P], ring_hi[0:r, n % RING, :],
                                     ring_lo[0:r, n % RING, :], n == PAIRS_OF[i][0], n == PAIRS_OF[i][-1])
                    ins.then_inc(pair_pe, 1)

            def spread_rinv(c, it):
                pe.wait_ge(rdiag_done, it * NC + c + 1)
                nc.tensor.matmul(scores[:, (c + 1) % 4, :], ones[:], r_diag[:, c].rearrange("p a b -> p (a b)"),
                                 start=True, stop=True).then_inc(rspread_pe, 1)

            def gates(q, it):
                c, j = q // DH, q % DH
                m_h = [(h_hi[:, e, chunk(c)], h_lo[:, e, chunk(c)]) for e in range(DH)]
                m_u = [(u_hi[:, c % 2, e, :], u_lo[:, c % 2, e, :]) for e in range(DH)]

                def product(bank, gate, w_hi, w_lo, moving, start, stop):
                    at = gate * D + j * P
                    for e in range(DH):
                        ins = split3(nc, scores[:, bank, :], w_hi[:, e, at:at + P], w_lo[:, e, at:at + P],
                                     *moving[e], start and e == 0, stop and e == DH - 1)
                    return ins

                if q == 0:
                    pe.wait_ge(rinv_done, it * NC + 4)
                else:
                    pe.wait_ge(hn_read, it * GRU + q)
                product(0, 2, g.whh_hi, g.whh_lo, m_h, True, True).then_inc(hn_pe, 1)
                if q:
                    pe.wait_ge(tr_done, it * GRU + q)
                product(1, 0, g.whh_hi, g.whh_lo, m_h, True, False)
                if j == 0:
                    pe.wait_ge(u_hi_done, it * NC + c + 1)
                    pe.wait_ge(u_lo_done, it * NC + c + 1)
                product(1, 0, g.wih_hi, g.wih_lo, m_u, False, True).then_inc(r_pe, 1)
                if j == 1 and 0 < c <= OWN:
                    square_sums(c - 1, it)
                if j == 0 and 1 < c <= OWN + 1:
                    spread_rstd(c - 2, it, n_diag[:])
                if q:
                    pe.wait_ge(n_in_done, it * GRU + q)
                product(3, 2, g.wih_hi, g.wih_lo, m_u, True, True).then_inc(xn_pe, 1)
                if q:
                    pe.wait_ge(tz_done, it * GRU + q)
                product(2, 1, g.whh_hi, g.whh_lo, m_h, True, False)
                product(2, 1, g.wih_hi, g.wih_lo, m_u, False, True).then_inc(z_pe, 1)

            def square_sums(c, it):
                pe.wait_ge(sq_done, it * NC + nth(c))
                for i in range(TPC):
                    for e in range(DH):
                        ins = nc.tensor.matmul(sums[:, 0, c * TPC + i:c * TPC + i + 1],
                                               sq[:, sq_at(c), e, i * P:(i + 1) * P],
                                               ones[:, 0:1], start=(e == 0), stop=(e == DH - 1))
                ins.then_inc(ss_pe, 1)

            def spread_rstd(c, it, diag):
                pe.wait_ge(ndiag_done, it * NC + nth(c))
                nc.tensor.matmul(sums[:, 2 + c % 2, :], ones[:], diag.rearrange("p a b -> p (a b)"),
                                 start=True, stop=True).then_inc(nspread_pe, 1)

            with pe.Fori(0, ITERS) as it:
                for t in range(MT):
                    r = rows_of(t)
                    for c in range(NC):
                        if t == 0:
                            if c >= OWN:
                                square_sums(c, it)
                            pe.wait_ge(h_hi_done, it * NC + c + 1)
                            pe.wait_ge(h_lo_done, it * NC + c + 1)
                        elif c % 2 == 0:
                            pe.wait_ge(drained, it * 2 * MT + 2 * (t - 1) + c // 2 + 1)
                        for e in range(DH):
                            ks = slice(t * P, t * P + r)
                            ins = split3(nc, scores[0:r, c, :], k_hi[:, e, ks], k_lo[:, e, ks],
                                         h_hi[:, e, chunk(c)], h_lo[:, e, chunk(c)], e == 0, e == DH - 1)
                        if c % 2:
                            ins.then_inc(score_pe, 1)
                    if t == 0:
                        for c in range(OWN, NC):
                            spread_rstd(c, it, n_diag2[:, c - OWN])
                    for i in AFTER.get(t, []):
                        item(i, it)
                item(TAIL[0], it)
                item(TAIL[1], it)
                pe.wait_ge(rsummed, it * (MT - 1) + MT - 1)
                pe.wait_ge(drained, it * 2 * MT + 2 * MT)
                for i in range(NT):
                    ins = nc.tensor.matmul(scores[:, 0, i:i + 1], racc[:, i * P:(i + 1) * P], ones[:, 0:1],
                                           start=True, stop=True)
                ins.then_inc(rs_pe, 1)
                item(TAIL[2], it)
                spread_rinv(0, it)
                spread_rinv(1, it)
                item(TAIL[3], it)
                spread_rinv(2, it)
                spread_rinv(3, it)
                for q in range(GRU):
                    gates(q, it)
                for read in (hn_read, tr_done, n_in_done, tz_done):
                    pe.wait_ge(read, it * GRU + GRU)

        @block.scalar
        def _(act):
            def high_part(n, it):
                i, t = PAIRS[n]
                r, c = rows_of(t), ITEMS[i][1]
                act.wait_ge(scaled, it * MT + t + 1)
                if n >= RING:
                    act.wait_ge(pair_pe, it * NPAIR + n - RING + 1)
                nc.scalar.activation(ring_hi[0:r, n % RING, :], E[0:r, E_SLOT[t], chunk(c)], ACT.Copy
                                     ).then_inc(hi_done, 1)

            def u_high(c, it):
                act.wait_ge(u_done, it * NC + c + 1)
                if c >= 2:
                    act.wait_ge(z_pe, it * GRU + DH * (c - 1))
                nc.scalar.activation(u_hi[:, c % 2], acc[:, :, chunk(c)], ACT.Copy).then_inc(u_hi_done, 1)

            def high_slots(c, it):
                act.wait_ge(h_done, it * GRU + DH * (c + 1))
                nc.scalar.activation(h_hi[:, :, chunk(c)], h_new[:, c % 2], ACT.Copy).then_inc(h_hi_done, 1)

            def squares(c, it):
                if c == 1:
                    act.wait_ge(ss_pe, it * NC + nth(0))
                nc.scalar.activation(sq[:, sq_at(c)], h_new[:, c % 2], ACT.Square).then_inc(sq_done, 1)

            def rstd_copy(c, it):
                act.wait_ge(nspread_pe, it * NC + nth(c))
                nc.scalar.activation(rstd_all[:, chunk(c)], sums[:, 2 + c % 2, :], ACT.Copy).then_inc(rstd_done, 1)

            act.sem_inc(h_hi_done, NC - 1)
            act.sem_inc(rstd_done, OWN)
            with act.Fori(0, ITERS) as it:
                squares(NC - 2, it)
                high_slots(NC - 1, it)
                squares(NC - 1, it)
                for c in range(OWN, NC):
                    rstd_copy(c, it)
                for t in range(MT):
                    r = rows_of(t)
                    first, others = staged(t, RING)
                    for n in first:
                        high_part(n, it)
                    act.wait_ge(nmax, it * MT + t + 1)
                    nc.scalar.activation(E[0:r, E_SLOT[t], :], E[0:r, E_SLOT[t], :], ACT.Exp,
                                         bias=neg_max[0:r, t % 2:t % 2 + 1],
                                         accum_out=zsum[0:r, t % 2:t % 2 + 1]).then_inc(exped, 1)
                    for n in others:
                        high_part(n, it)
                for i in TAIL:
                    for n in PAIRS_OF[i]:
                        high_part(n, it)
                for c in range(NC):
                    act.wait_ge(rspread_pe, it * NC + c + 1)
                    nc.scalar.activation(racc[:, chunk(c)], scores[:, (c + 1) % 4, :], ACT.Copy).then_inc(rinv_done, 1)
                u_high(0, it)
                for q in range(GRU):
                    c, j = q // DH, q % DH
                    p = q % 2
                    if q >= 2:
                        act.wait_ge(n_in_done, it * GRU + q - 1)
                    act.wait_ge(r_pe, it * GRU + q + 1)
                    nc.scalar.activation(t_r[:, p], scores[:, 1, :], ACT.Tanh, bias=g.b_gate[:, j:j + 1],
                                         scale=0.5).then_inc(tr_done, 1)
                    act.wait_ge(n_in_done, it * GRU + q + 1)
                    if q >= 2:
                        act.wait_ge(h_done, it * GRU + GRU + q - 1)
                    nc.scalar.activation(n_out[:, p], n_in[:, p], ACT.Tanh, bias=g.bih[:, 2 * DH + j:2 * DH + j + 1]
                                         ).then_inc(n_done, 1)
                    if c and j == 0:
                        high_slots(c - 1, it + 1)
                    act.wait_ge(z_pe, it * GRU + q + 1)
                    nc.scalar.activation(t_z[:, p], scores[:, 2, :], ACT.Tanh, bias=g.b_gate[:, DH + j:DH + j + 1],
                                         scale=0.5).then_inc(tz_done, 1)
                    if 0 < c <= OWN and j == 0:
                        squares(c - 1, it)
                    if 1 < c <= OWN + 1 and j == 0:
                        rstd_copy(c - 2, it)
                    if j == 0 and c + 1 < NC:
                        u_high(c + 1, it)
            high_slots(NC - 1, ITERS)

        @block.vector
        def _(dve):
            def low_part(n, it):
                i, t = PAIRS[n]
                r, c = rows_of(t), ITEMS[i][1]
                dve.wait_ge(hi_done, it * NPAIR + n + 1)
                nc.vector.tensor_tensor(ring_lo[0:r, n % RING, :], E[0:r, E_SLOT[t], chunk(c)],
                                        ring_hi[0:r, n % RING, :].bitcast(F32), ALU.subtract).then_inc(lo_done, 1)

            def add_sums(i, it):
                b, c = ITEMS[i]
                dve.wait_ge(pair_pe, it * NPAIR + pairs_until(i))
                src = sums[:, 2 * (i % 2):2 * (i % 2) + DH, :]
                dst = acc[:, :, chunk(c)]
                if b == 0:
                    nc.vector.tensor_copy(dst, src).then_inc(item_done, 1)
                else:
                    nc.vector.tensor_tensor(dst, src, dst, ALU.add).then_inc(item_done, 1)

            def scale(t, it):
                r, p = rows_of(t), t % 2
                dve.wait_ge(exped, it * MT + t + 1)
                nc.vector.reciprocal(rz[0:r, :], zsum[0:r, p:p + 1])
                dve.drain()
                nc.vector.tensor_scalar(E[0:r, E_SLOT[t], :], E[0:r, E_SLOT[t], :], rz[0:r, :], None, ALU.mult
                                        ).then_inc(scaled, 1)

            def u_sums(c, it):
                dve.wait_ge(rinv_done, it * NC + c + 1)
                nc.vector.tensor_tensor(acc[:, :, chunk(c)], acc[:, :, chunk(c)],
                                        racc[:, chunk(c)].unsqueeze(1).broadcast_to([P, DH, CW]), ALU.mult
                                        ).then_inc(u_done, 1)

            def low_slots(c, it):
                dve.wait_ge(h_hi_done, it * NC + c + 1)
                nc.vector.tensor_tensor(h_lo[:, :, chunk(c)], h_new[:, c % 2], h_hi[:, :, chunk(c)].bitcast(F32),
                                        ALU.subtract).then_inc(h_lo_done, 1)

            def rstd(c, it, n, diag):
                dve.wait_ge(ss_pe, it * NC + nth(c) + n - 1)
                if c == 1:
                    dve.wait_ge(nspread_pe, it * NC + nth(0))
                cols = n * TPC
                nc.vector.tensor_scalar(g.nx[:, 0:cols], sums[:, 0, c * TPC:c * TPC + cols], 1.0 / D, EPS_NORM,
                                        ALU.mult, ALU.add)
                rsqrt(nc, dve, g, g.ny[:, 0:cols], g.nx[:, 0:cols], cols)
                diagonal(nc, g, diag, g.ny[:, 0:cols], cols).then_inc(ndiag_done, n)

            dve.sem_inc(h_lo_done, NC - 1)
            dve.sem_inc(h_done, GRU)
            with dve.Fori(0, ITERS) as it:
                low_slots(NC - 1, it)
                for t in range(MT):
                    r, s, p = rows_of(t), E_SLOT[t], t % 2
                    first, others = staged(t, RING - 1)
                    at_once = t and any(t - 1 in BLOCKS[ITEMS[i][0]] for i in AFTER.get(t, []))
                    if at_once:
                        scale(t - 1, it)
                    dve.drain()
                    for n in first:
                        low_part(n, it)
                    if before_in_slot(t) is not None:
                        k = before_in_slot(t)
                        dve.wait_ge(hi_done, it * NPAIR + last_use(k))
                        dve.wait_ge(rsummed, it * (MT - 1) + max(k, 1))
                    for i in range(2):
                        if t == 0 and i == 1:
                            rstd(OWN, it, NC - OWN, n_diag2[:].rearrange("p c a b -> p (c a) b"))
                        if t == 0:
                            dve.wait_ge(rstd_done, it * NC + 2 * i + 2)
                        dve.wait_ge(score_pe, it * 2 * MT + 2 * t + i + 1)
                        dve.sem_inc(seen, 1)
                        half = slice(i * 2 * CW, (i + 1) * 2 * CW)
                        nc.vector.tensor_tensor_reduce(
                            out=E[0:r, s, half], in0=scores[0:r, 2 * i:2 * i + 2, :].rearrange("p a b -> p (a b)"),
                            in1=rstd_all[0:r, half], scale=1.0, scalar=-3e38, op0=ALU.mult, op1=ALU.max,
                            accum_out=mx[0:r, p, i:i + 1]).then_inc(drained, 1)
                        if i == 0 and t and not at_once:
                            scale(t - 1, it)
                    dve.drain()
                    nc.vector.tensor_scalar(neg_max[0:r, p:p + 1], mx[0:r, p, 0:1], mx[0:r, p, 1:2], -1.0,
                                            ALU.max, ALU.mult).then_inc(nmax, 1)
                    for k, n in enumerate(others):
                        if t == MT - 1 and k == 1:
                            scale(t, it)
                        low_part(n, it)
                        for i in AFTER[t][1:]:
                            if n == PAIRS_OF[i][-1]:
                                add_sums(i - 1, it)
                    if t in AFTER and t < MT - 1:
                        add_sums(AFTER[t][-1], it)
                dve.drain()
                for i in TAIL[0:3]:
                    for n in PAIRS_OF[i]:
                        low_part(n, it)
                    if i < TAIL[2]:
                        add_sums(i - 1, it)
                dve.wait_ge(rs_pe, it + 1)
                nc.vector.tensor_scalar(rsum[:], scores[:, 0, 0:NT], EPS_ATTN, None, ALU.add)
                dve.drain()
                nc.vector.reciprocal(rinv[:], rsum[:])
                dve.drain()
                for c in range(NC):
                    diagonal(nc, g, r_diag[:, c], rinv[:, c * TPC:(c + 1) * TPC], TPC).then_inc(rdiag_done, 1)
                add_sums(TAIL[1], it)
                for n in PAIRS_OF[TAIL[3]]:
                    low_part(n, it)
                add_sums(TAIL[2], it)
                add_sums(TAIL[3], it)
                dve.drain()
                u_sums(0, it)
                for q in range(GRU):
                    c, j, p = q // DH, q % DH, q % 2
                    b_hn = g.bhh[:, 2 * DH + j:2 * DH + j + 1]
                    dve.wait_ge(hn_pe, it * GRU + q + 1)
                    dve.wait_ge(tr_done, it * GRU + q + 1)
                    if q >= 2:
                        dve.wait_ge(n_done, it * GRU + q - 1)
                    nc.vector.scalar_tensor_tensor(n_in[:, p], scores[:, 0, :], b_hn, t_r[:, p], ALU.add, ALU.mult)
                    dve.drain()
                    nc.vector.scalar_tensor_tensor(n_in[:, p], scores[:, 0, :], b_hn, n_in[:, p], ALU.add, ALU.add
                                                   ).then_inc(hn_read, 1)
                    dve.drain()
                    dve.wait_ge(xn_pe, it * GRU + q + 1)
                    nc.vector.scalar_tensor_tensor(n_in[:, p], n_in[:, p], 0.5, scores[:, 3, :], ALU.mult, ALU.add
                                                   ).then_inc(n_in_done, 1)
                    if c and j == 0:
                        low_slots(c - 1, it + 1)
                    if 0 < c <= OWN and j == 1:
                        rstd(c - 1, it, 1, n_diag[:])
                    if j == 0 and c + 1 < NC:
                        u_sums(c + 1, it)
                    dve.wait_ge(half_done, it * GRU + q + 1)
                    dve.wait_ge(tz_done, it * GRU + q + 1)
                    nc.vector.scalar_tensor_tensor(h_half[:, p], t_z[:, p], 1.0, h_half[:, p], ALU.add, ALU.mult)
                    dve.wait_ge(n_done, it * GRU + q + 1)
                    nc.vector.scalar_tensor_tensor(n_out[:, p], t_z[:, p], 1.0, n_out[:, p], ALU.subtract, ALU.mult)
                    dve.drain()
                    if c >= 2 and j == 0:
                        dve.wait_ge(sq_done, it * NC + nth(c - 2))
                    nc.vector.scalar_tensor_tensor(h_new[:, c % 2, j], n_out[:, p], -0.5, h_half[:, p],
                                                   ALU.mult, ALU.add).then_inc(h_done, 1)
            low_slots(NC - 1, ITERS)

        @block.gpsimd
        def _(pool):
            def u_low(c, it):
                pool.wait_ge(u_hi_done, it * NC + c + 1)
                for e in range(DH):
                    ins = nc.gpsimd.tensor_tensor(u_lo[:, c % 2, e, :], acc[:, e, chunk(c)],
                                                  u_hi[:, c % 2, e, :].bitcast(F32), ALU.subtract)
                ins.then_inc(u_lo_done, 1)

            with pool.Fori(0, ITERS) as it:
                for t in range(1, MT):
                    r = rows_of(t)
                    pool.wait_ge(scaled, it * MT + t + 1)
                    first = E[0:r, E_SLOT[0], :] if t == 1 else racc[0:r, :]
                    nc.gpsimd.tensor_tensor(racc[0:r, :], first, E[0:r, E_SLOT[t], :], ALU.add).then_inc(rsummed, 1)
                    pool.drain()
                u_low(0, it)
                for q in range(GRU):
                    c, j, p = q // DH, q % DH, q % 2
                    if q == 0:
                        pool.wait_ge(pair_pe, it * NPAIR + NPAIR)
                    if q >= 2:
                        pool.wait_ge(h_done, it * GRU + GRU + q - 1)
                    nc.gpsimd.tensor_tensor(h_half[:, p], h_hi[:, j, chunk(c)].bitcast(F32),
                                            h_lo[:, j, chunk(c)].bitcast(F32), ALU.add)
                    pool.drain()
                    nc.gpsimd.tensor_scalar(h_half[:, p], h_half[:, p], 0.5, None, ALU.mult).then_inc(half_done, 1)
                    if j == 0 and c + 1 < NC:
                        u_low(c + 1, it)


def weight_piece(nc, a, eng, step, g, w, expert, cols, count, base=0):
    k = count % RAW
    raw = g.w_raw[:, k, :]
    if step == "load":
        if count >= RAW:
            eng.wait_ge(g.w_split[k], count // RAW)
        eng.dma_start(raw, a["w"][expert, :, cols] if isinstance(expert, int)
                      else a["w"][bass.ds(expert, 1), :, cols].rearrange("e p c -> (e p) c")
                      ).then_inc(g.w_loaded[k], 16)
    elif step == "high":
        eng.wait_ge(g.w_loaded[k], base * (16 // RAW) + (count - k) * (16 // RAW) + 16)
        nc.scalar.activation(g.w_hi[w][:, cols], raw, ACT.Copy).then_inc(g.w_hi_done, 1)
    else:
        ops = nc.gpsimd if step == "low on gpsimd" else nc.vector
        eng.wait_ge(g.w_hi_done, base + count + 1)
        ops.tensor_tensor(g.w_lo[w][:, cols], raw, g.w_hi[w][:, cols].bitcast(F32), ALU.subtract
                                ).then_inc(g.w_split[k], 1)


def piece_cols(i):
    return slice(i * PIECE, (i + 1) * PIECE)


def handover(nc, a, g):
    place = g.place
    g.x1 = place("x1", [P, NT, D], F32, g.acc_at)
    at = g.rstd_at
    g.xn_at = at
    g.xn = place("xn", [P, NT, D], F32, at)
    at += NT * D * 4
    g.w_raw = place("w_raw", [P, RAW, PIECE], F32, at)
    at += RAW * PIECE * 4
    g.w_at = at
    g.w_hi, g.w_lo = [], []
    for w in range(2):
        g.w_hi.append(place(f"w_hi{w}", [P, WCOLS], F32R, at))
        g.w_lo.append(place(f"w_lo{w}", [P, WCOLS], F32R, at + WCOLS * 4))
        at += 2 * WCOLS * 4
    g.x_hi = place("x_hi", [P, 2, DH, UW], F32R, g.h_at)
    g.x_lo = place("x_lo", [P, 2, DH, UW], F32R, g.h_at + 8192)
    size = 2 * DH * UW * 4
    xn_hi2 = [place(f"xn_hi{c}", [P, 2, DH, UW], F32R, at - c * size) for c in range(1, NC)]
    xn_lo2 = [place(f"xn_lo{c}", [P, 2, DH, UW], F32R, at - (NC - 1 + c) * size) for c in range(1, NC)]
    g.tmp_at = at
    ident_r = place("ident_r", [P, P], F32R, at)
    by_expert = place("by_expert", [8, NC, CW], F32, at + P * 4)
    g.probs = place("probs", [P, NT, 8], F32, g.h_at + 16384)
    tiny = g.tiny
    stats = tiny("stats", [P, NT, 6])
    g.place_of = tiny("place_of", [P, 2, NT], U32)
    g.share = tiny("share", [P, 2, NT])
    g.expert_of = tiny("expert_of", [P, SLOT_UNITS + 1], I32)
    g.w_loaded = g.semaphores(*(f"w_loaded{i}" for i in range(RAW)))
    g.w_split = g.semaphores(*(f"w_split{i}" for i in range(RAW)))
    g.w_hi_done, g.rows_stored = g.semaphores("w_hi_done1", "rows_stored")
    ld_x = g.semaphores(*(f"ld_x{c}" for c in range(NC)))
    (ident_done, rows_pe, x1_done, norm_done, cols_pe, hi_done, lo_done, by_expert_pe, by_expert_done, logit_pe
     ) = g.semaphores(
        "ident_done", "rows_pe", "x1_done", "norm_done", "cols_pe", "hi_done1", "lo_done1", "by_expert_pe",
        "by_expert_done", "logit_pe")
    low, high = g.psum
    flat = lambda x: x.rearrange("p a b -> p (a b)")

    def chunk(x, c):
        return x[:, c * TPC:(c + 1) * TPC, :]

    def rows_bank(c):
        return [low, high][c // 2][:, 2 * (c % 2):2 * (c % 2) + 2, :]

    def cols_bank(c):
        return low[:, 2 * (c % 2):2 * (c % 2) + 2, :]

    def columns(c):
        return (xn_hi2[c - 1], xn_lo2[c - 1]) if c else (g.x_hi, g.x_lo)

    def by_unit(cols):
        return cols.rearrange("p e (u w) -> p u e w", w=UW)

    with nc.Block() as block:
        @block.sync
        def _(sp):
            for c in range(NC):
                sp.dma_start(chunk(g.x1, c), a["x"][c * CW:(c + 1) * CW, :].rearrange("(t p) d -> p t d", p=P)
                             ).then_inc(ld_x[c], 16)
            for i in range(PIECES):
                weight_piece(nc, a, sp, "load", g, 0, 0, piece_cols(i), i)
            for u in range(S // UW):
                sp.wait_ge(norm_done, u * UW // CW + 1)
                at = (u if u < HEAD else UNITS - 1) * UW
                sp.dma_start(g.in_dram[at:at + UW, :].rearrange("(t p) d -> p t d", p=P),
                             g.xn[:, u * TPU:(u + 1) * TPU, :]).then_inc(g.rows_stored, 16)

        @block.gpsimd
        def _(pool):
            for i in range(PIECES):
                weight_piece(nc, a, pool, "low on gpsimd", g, 0, 0, piece_cols(i), i)

        @block.scalar
        def _(act):
            nc.scalar.activation(ident_r[:], g.ident[:], ACT.Copy).then_inc(ident_done, 1)
            for i in range(PIECES):
                weight_piece(nc, a, act, "high", g, 0, 0, piece_cols(i), i)
            def take_logits(c):
                act.wait_ge(by_expert_pe, c + 1)
                nc.scalar.activation(by_expert[:, c, :], high[0:8, c % 2, :], ACT.Copy).then_inc(by_expert_done, 1)

            for c in range(NC):
                act.wait_ge(cols_pe, c + 1)
                for u in range(CW // UW):
                    ins = nc.scalar.activation(columns(c)[0][:, u], by_unit(cols_bank(c))[:, u], ACT.Copy)
                ins.then_inc(hi_done, 1)
                if c >= 2:
                    take_logits(c - 2)
            for c in range(NC - 2, NC):
                take_logits(c)

        @block.vector
        def _(dve):
            for c in range(NC):
                x1 = chunk(g.x1, c)
                dve.wait_ge(ld_x[c], 16)
                dve.wait_ge(rows_pe, c + 1)
                nc.vector.scalar_tensor_tensor(flat(x1), flat(rows_bank(c)), g.tg_x[:], flat(x1), ALU.mult, ALU.add
                                               ).then_inc(x1_done, 1)
                dve.drain()
                for i in range(TPC):
                    nc.vector.bn_stats(stats[:, c * TPC + i, :], x1[:, i, :])
            dve.drain()
            for t in range(NT):
                nc.vector.bn_aggr(g.mean_var[:, t, :], stats[:, t, :])
            dve.drain()
            nc.vector.tensor_scalar(g.nx[:], g.mean_var[:, :, 1], EPS_LN, None, ALU.add)
            rsqrt(nc, dve, g, g.ny[:], g.nx[:], NT)

            def low_columns(c):
                dve.wait_ge(hi_done, c + 1)
                hi, lo = columns(c)
                for u in range(CW // UW):
                    ins = nc.vector.tensor_tensor(lo[:, u], by_unit(cols_bank(c))[:, u], hi[:, u].bitcast(F32),
                                                  ALU.subtract)
                ins.then_inc(lo_done, 1)

            for c in range(NC):
                for t in range(c * TPC, (c + 1) * TPC):
                    ins = nc.vector.tensor_scalar(g.xn[:, t, :], g.x1[:, t, :], g.mean_var[:, t, 0:1], g.ny[:, t:t + 1],
                                                  ALU.subtract, ALU.mult)
                ins.then_inc(norm_done, 1)
                if c >= 2:
                    low_columns(c - 2)
            for c in range(NC - 2, NC):
                low_columns(c)
            dve.wait_ge(logit_pe, NC)
            nc.vector.memset(g.probs[:, :, ROUTED:8], -1.0)
            nc.vector.tensor_copy(g.probs[:, :, 0:ROUTED],
                                  high[:, 2, 0:NT * 8].rearrange("p (t e) -> p t e", e=8)[:, :, 0:ROUTED])
            dve.drain()

        @block.tensor
        def _(pe):
            def turn_columns(c):
                pe.wait_ge(norm_done, c + 1)
                if c >= 2:
                    pe.wait_ge(lo_done, c - 1)
                for e in range(DH):
                    for i in range(TPC):
                        ins = nc.tensor.transpose(cols_bank(c)[:, e, i * P:(i + 1) * P],
                                                  g.xn[:, c * TPC + i, e * P:(e + 1) * P], g.ident[:])
                ins.then_inc(cols_pe, 1)

            def logits(c):
                pe.wait_ge(lo_done, c + 1)
                if c >= 2:
                    pe.wait_ge(by_expert_done, c - 1)
                hi, lo = columns(c)
                for u in range(CW // UW):
                    for e in range(DH):
                        ins = split3(nc, high[0:8, c % 2, u * UW:(u + 1) * UW], g.rw_hi[:, e, :], g.rw_lo[:, e, :],
                                     hi[:, u, e, :], lo[:, u, e, :], e == 0, e == DH - 1)
                ins.then_inc(by_expert_pe, 1)

            def logits_by_token(c):
                pe.wait_ge(by_expert_done, c + 1)
                for i in range(TPC):
                    t = c * TPC + i
                    ins = nc.tensor.transpose(high[:, 2, t * 8:(t + 1) * 8], by_expert[:, c, i * P:(i + 1) * P],
                                              g.ident[0:8, 0:8])
                ins.then_inc(logit_pe, 1)

            pe.wait_ge(ident_done, 1)
            for c in range(NC):
                for i in range(TPC):
                    ts = slice(c * CW + i * P, c * CW + (i + 1) * P)
                    for e in range(DH):
                        dst = rows_bank(c)[:, i // 2, (i % 2) * D + e * P:(i % 2) * D + (e + 1) * P]
                        nc.tensor.matmul(dst, g.h_hi[:, e, ts], ident_r[:], start=True, stop=False)
                        ins = nc.tensor.matmul(dst, g.h_lo[:, e, ts], ident_r[:], start=False, stop=True)
                ins.then_inc(rows_pe, 1)
            turn_columns(0)
            for c in range(1, NC):
                turn_columns(c)
                logits(c - 1)
                if c >= 2:
                    logits_by_token(c - 2)
            logits(NC - 1)
            logits_by_token(NC - 2)
            logits_by_token(NC - 1)


def experts(nc, a, out, g):
    t_g, act_g, hid = (g.place(n, [P, HIDDEN, UW], F32, g.tmp_at + i * HIDDEN * UW * 4)
                       for i, n in enumerate(("t_g", "act_g", "hid")))
    hid_hi, hid_lo = (g.place(n, [P, SPLITS, UW], F32R, g.tmp_at + (3 * HIDDEN + i * SPLITS) * UW * 4)
                      for i, n in enumerate(("hid_hi", "hid_lo")))
    x_hi, x_lo = g.x_hi, g.x_lo
    x_rows = g.place("ex_rows", [P, 2, TPU, D], F32, g.h_at + 20480)
    y_rows = g.place("y_rows", [P, TPU, D], F32, g.h_at + 28672)
    TURNS = UNITS // 2
    STEPS = 2 * FT
    (gate_pe, up_pe, tanh_done, act_done, hid_done, hi_done, lo_done, down_pe, y_rows_done,
     x_cols_pe, x_hi_done, x_lo_done, stored, scattered) = g.semaphores(
        "gate_pe", "up_pe", "tanh_done", "act_done", "hid_done", "hid_hi_done", "hid_lo_done", "down_pe",
        "y_rows_done", "x_cols_pe", "x_hi_done", "x_lo_done", "stored", "scattered")
    x_loaded = g.semaphores("x_loaded0", "x_loaded1")
    gates, outs = g.psum
    y_out = outs[:, 0:2, :].rearrange("p v (i d) -> p v i d", d=D)
    turned = outs[:, 2, :].rearrange("p (e w) -> p e w", w=UW)
    gates = gates[:, :, 0:UW]
    flat = lambda x: x.rearrange("p a b -> p (a b)")
    assert UNITS % 2 == 0
    probs, row = g.probs, g.c_ssq
    best, chosen0, chosen1, taken, pos, best_at, tri = (
        g.place(n, [P, P] if n == "tri" else [P, NT, 8], dt, g.h_at + 16384 + (i + 1) * 512)
        for i, (n, dt) in enumerate((("best", F32), ("chosen0", F32), ("chosen1", F32), ("taken", F32), ("pos", F32),
                                     ("best_at", U32), ("tri", F32))))
    chosen = [chosen0[:, :, 0:ROUTED], chosen1[:, :, 0:ROUTED]]
    tiny = g.tiny
    where = tiny("where", [P, NT, 2])
    spot, is_first, weight, part = (tiny(n, [P, 2, NT]) for n in ("spot", "is_first", "weight", "part"))
    numbers = tiny("numbers", [P, 8])
    unit_no = tiny("unit_no", [P, SLOT_UNITS])
    unit_of = tiny("unit_of", [P, SLOT_UNITS])
    first = tiny("first", [P, 8])
    after = tiny("after", [P, 8])
    (max_done, exp_done, taken_done, rank_pe, consts, tri_one, placed, units_known) = g.semaphores(
        "max_done", "exp_done", "taken_done", "rank_pe", "consts", "tri_one", "placed", "units_known")
    ranks = outs[:, 3, 0:(NT + 1) * ROUTED].rearrange("p (t e) -> p t e", e=ROUTED)
    total = ranks[:, NT, :]
    SCATTER_AT, SCATTER_STEPS = 11, 34
    LOW_AT, ADD_AT = 4, 10
    y_low = g.place("y_low", [P, NT, D], F32, g.xn_at)
    y_high = g.place("y_high", [P, NT, D], F32, g.w_at)
    y_shared = g.place("y_shared", [P, HEAD * TPU, D], F32, g.w_at + NT * D * 4)
    half = g.rz
    got_low, got_high, got_shared = ([g.semaphores(f"{n}{c}")[0] for c in range(NC)]
                                     for n in ("got_low", "got_high", "got_shared"))
    res_done, result_stored = g.semaphores("res_done", "result_stored")

    def wide(x):
        return x.unsqueeze(2).broadcast_to([P, NT, ROUTED])

    def turns(eng, body):
        body(0, True, False)
        body(1, False, False)
        body(2, False, False)
        with eng.Fori(3, TURNS - 1) as n:
            body(n, False, False)
        body(TURNS - 1, False, True)

    def low(eng, ops, n, k):
        eng.wait_ge(hi_done, n * STEPS + k + 1)
        ops.tensor_tensor(hid_lo[:, k % SPLITS], hid[:, k % HIDDEN], hid_hi[:, k % SPLITS].bitcast(F32), ALU.subtract
                          ).then_inc(lo_done, 1)

    def rows(dram, u):
        return dram[u * UW:(u + 1) * UW, :].rearrange("(t p) d -> p t d", p=P)

    with nc.Block() as block:
        @block.sync
        def _(sp):
            def load_rows(u):
                if u >= 4:
                    sp.wait_ge(x_cols_pe, u - 1)
                if u == HEAD:
                    sp.wait_ge(scattered, 16 * 2 * NT)
                sp.dma_start(x_rows[:, u % 2], rows(g.in_dram, u)).then_inc(x_loaded[u % 2], 16)

            sp.wait_ge(g.rows_stored, 16 * (S // UW))
            load_rows(2)
            for u in range(UNITS):
                if u + 1 == HEAD:
                    sp.wait_ge(units_known, 1)
                if u + 1 < UNITS:
                    e = 0 if u + 1 < HEAD else sp.value_load(g.expert_of[0:1, u + 1 - HEAD:u + 2 - HEAD],
                                                             min_val=0, max_val=ROUTED)
                    for i in range(PIECES):
                        weight_piece(nc, a, sp, "load", g, 1 - u % 2, e, piece_cols(i), PIECES * (u + 1) + i)
                        if i == 5 and u:
                            sp.wait_ge(y_rows_done, u)
                            sp.dma_start(rows(g.out_dram, u - 1), y_rows[:]).then_inc(stored, 16)
                        if i == (3 if u + 1 == HEAD else 1) and 2 <= u < UNITS - 1:
                            load_rows(u + 1)
            sp.wait_ge(y_rows_done, UNITS - 1)
            sp.dma_start(rows(g.out_dram, UNITS - 2), y_rows[:]).then_inc(stored, 16)
            sp.wait_ge(stored, 16 * (UNITS - 2))
            for c in range(NC):
                last = min((c + 1) * TPC, HEAD * TPU)
                sp.dma_start(y_shared[:, c * TPC:last, :], g.out_dram[c * CW:last * P, :].rearrange(
                    "(t p) d -> p t d", p=P)).then_inc(got_shared[c], 16)
            for t in range(NT):
                sp.wait_ge(res_done, t + 1)
                sp.dma_start(out[t * P:(t + 1) * P, :], g.x1[:, t, :]).then_inc(result_stored, 16)
            sp.wait_ge(stored, 16 * (UNITS - 1))
            sp.wait_ge(result_stored, 16 * NT)

        @block.tensor
        def _(pe):
            def x_transposes(n, v):
                pe.wait_ge(x_lo_done, 2 * n + v)
                pe.wait_ge(x_loaded[v % 2], (n + v // 2) * 16)
                for e in range(DH):
                    for i in range(TPU):
                        ins = nc.tensor.transpose(turned[:, e, i * P:(i + 1) * P],
                                                  x_rows[:, v % 2, i, e * P:(e + 1) * P], g.ident[:])
                ins.then_inc(x_cols_pe, 1)

            def weights_split(n, v, first, last):
                for i in range(first, last):
                    if i + RAW >= last:
                        pe.wait_ge(g.w_split[i % RAW], (2 * n + v) * (PIECES // RAW) + i // RAW + 1)

            def down(n, k, started):
                w, f = k // FT % 2, k % FT
                cols = slice(DOWN_AT + f * D, DOWN_AT + (f + 1) * D)
                pe.wait_ge(hi_done, n * STEPS + k + 1)
                pe.wait_ge(lo_done, n * STEPS + k + 1)
                if f == 0:
                    weights_split(n, w, 0, PIECES)
                    if started:
                        pe.wait_ge(y_rows_done, 2 * n + w - 1)
                for i in range(TPU):
                    ts = slice(i * P, (i + 1) * P)
                    ins = split3(nc, y_out[:, w, i, :], hid_hi[:, k % SPLITS, ts], hid_lo[:, k % SPLITS, ts],
                                 g.w_hi[w][:, cols], g.w_lo[w][:, cols],
                                 f == 0 and i == 0, f == FT - 1 and i == TPU - 1)
                ins.then_inc(down_pe, 1)

            def up_or_gate(k, bank, first):
                w, f = k // FT, k % FT
                for e in range(DH):
                    cols = slice(first + e * DFF + f * P, first + e * DFF + (f + 1) * P)
                    ins = split3(nc, gates[:, bank, :], g.w_hi[w][:, cols], g.w_lo[w][:, cols],
                                 x_hi[:, w, e, :], x_lo[:, w, e, :], e == 0, e == DH - 1)
                return ins

            def body(n, begins, ends):
                for k in range(STEPS):
                    v, f = k // FT, k % FT
                    if f == 0:
                        weights_split(n, v, 0, GATE_PIECES)
                        pe.wait_ge(x_lo_done, 2 * n + v + 1)
                    if not (begins and k < 2):
                        pe.wait_ge(act_done, n * STEPS + k - 1)
                    up_or_gate(k, k % 2, 0).then_inc(gate_pe, 1)
                    if not (begins and k < 2):
                        pe.wait_ge(hid_done, n * STEPS + k - 1)
                    if f == 0:
                        weights_split(n, v, GATE_PIECES, UP_PIECES)
                    up_or_gate(k, 2 + k % 2, UP_AT).then_inc(up_pe, 1)
                    if k >= LAG:
                        down(n, k - LAG, not begins)
                    elif not begins:
                        down(n - 1, STEPS + k - LAG, True)
                    if begins and k == 7:
                        count_tokens()
                    if f == 5 and not (ends and v == 1 or begins and v == 0):
                        x_transposes(n, v + 1)

            def count_tokens():
                pe.wait_ge(consts, 8 + SLOT_UNITS + 1)
                pe.wait_ge(taken_done, 1)
                nc.tensor.matmul(ranks[:, 0:NT, :], tri[:], taken[:, :, 0:ROUTED], start=True, stop=False)
                nc.tensor.matmul(total, g.ones[:], taken[:, 0, 0:ROUTED], start=False, stop=False)
                for t in range(NT):
                    to = NT + 1 if t else NT
                    ins = nc.tensor.matmul(ranks[:, t + 1:to, :], g.ones[:],
                                           taken[:, t:t + 1, 0:ROUTED].broadcast_to([P, to - t - 1, ROUTED]),
                                           start=False, stop=(t == NT - 1))
                ins.then_inc(rank_pe, 1)

            pe.sem_inc(x_cols_pe, 2)
            turns(pe, body)
            for k in range(STEPS - LAG, STEPS):
                down(TURNS - 1, k, True)

        @block.scalar
        def _(act):
            def high(n, k):
                if not (isinstance(n, int) and n * STEPS + k < SPLITS):
                    act.wait_ge(down_pe, n * STEPS + k + 1 - SPLITS)
                act.wait_ge(hid_done, n * STEPS + k + 1)
                nc.scalar.activation(hid_hi[:, k % SPLITS], hid[:, k % HIDDEN], ACT.Copy).then_inc(hi_done, 1)

            def take_y_rows(n, v, begins):
                act.wait_ge(down_pe, n * STEPS + (v + 1) * FT)
                if not begins:
                    act.wait_ge(stored, (2 * n + v) * 16)
                nc.scalar.activation(flat(y_rows[:]), outs[:, v % 2, :], ACT.Copy).then_inc(y_rows_done, 1)

            def x_high(n, v):
                act.wait_ge(x_cols_pe, 2 * n + v + 1)
                nc.scalar.activation(x_hi[:, v % 2], turned, ACT.Copy).then_inc(x_hi_done, 1)

            def body(n, begins, ends):
                for k in range(STEPS):
                    v, f = k // FT, k % FT
                    if not (begins and k < HIDDEN):
                        act.wait_ge(act_done, n * STEPS + k + 1 - HIDDEN)
                    act.wait_ge(gate_pe, n * STEPS + k + 1)
                    nc.scalar.activation(t_g[:, k % HIDDEN], gates[:, k % 2, :], ACT.Tanh, scale=0.5
                                         ).then_inc(tanh_done, 1)
                    if f == LAG and not (begins and v == 0):
                        take_y_rows(n + (v - 1) // 2, (v - 1) % 2, begins)
                    if begins and k == 1:
                        act.wait_ge(max_done, 1)
                        nc.scalar.activation(flat(probs[:]), flat(probs[:]), ACT.Exp).then_inc(exp_done, 1)
                    if k:
                        high(n, k - 1)
                    elif not begins:
                        high(n - 1, STEPS - 1)
                    if f == 6 and not (begins and v == 0 or ends and v == 1):
                        x_high(n, v + 1)
                    if not (ends and v == 1):
                        weight_piece(nc, a, act, "high", g, 1 - v, None, piece_cols(f), PIECES * (v + 1) + f,
                                     n * 2 * PIECES)

            act.sem_inc(x_hi_done, 2)
            turns(act, body)
            high(TURNS - 1, STEPS - 1)

        @block.vector
        def _(dve):
            def add_low(t):
                dve.wait_ge(got_low[t // TPC], 16 * TPC)
                nc.vector.scalar_tensor_tensor(g.x1[:, t, :], y_low[:, t, :], g.share[:, 0, t:t + 1], g.x1[:, t, :],
                                               ALU.mult, ALU.add)

            def add_high(t):
                dve.wait_ge(got_high[t // TPC], 16 * TPC)
                nc.vector.scalar_tensor_tensor(g.x1[:, t, :], y_high[:, t, :], g.share[:, 1, t:t + 1], g.x1[:, t, :],
                                               ALU.mult, ALU.add).then_inc(res_done, 1)

            def add_shared(c):
                if c < NC:
                    ts = slice(c * TPC, min((c + 1) * TPC, HEAD * TPU))
                    x1 = flat(g.x1[:, ts, :])
                    dve.wait_ge(got_shared[c], 16)
                    src = flat(y_shared[:, ts, :])
                else:
                    x1 = flat(g.x1[:, HEAD * TPU:NT, :])
                    dve.wait_ge(down_pe, TURNS * STEPS)
                    src = outs[:, 1, :]
                nc.vector.scalar_tensor_tensor(x1, src, half[:], x1, ALU.mult, ALU.add)

            def x_low(n, v):
                dve.wait_ge(x_hi_done, 2 * n + v + 1)
                nc.vector.tensor_tensor(x_lo[:, v % 2], turned, x_hi[:, v % 2].bitcast(F32), ALU.subtract
                                        ).then_inc(x_lo_done, 1)

            def body(n, begins, ends):
                for k in range(STEPS):
                    v, f = k // FT, k % FT
                    dve.wait_ge(tanh_done, n * STEPS + k + 1)
                    nc.vector.scalar_tensor_tensor(act_g[:, k % HIDDEN], t_g[:, k % HIDDEN], 1.0, gates[:, k % 2, :],
                                                   ALU.add, ALU.mult).then_inc(act_done, 1)
                    b, i = ((k - 1) // FT, (k - 1) % FT)
                    if not (begins and b < 0 or ends and b == 1) and i % RAW != POOL_PLACE:
                        weight_piece(nc, a, dve, "low", g, (1 - b) % 2, None, piece_cols(i), PIECES * (b + 1) + i,
                                     n * 2 * PIECES)
                    dve.drain()
                    if not (begins and k < HIDDEN):
                        dve.wait_ge(lo_done, n * STEPS + k + 1 - HIDDEN)
                    dve.wait_ge(up_pe, n * STEPS + k + 1)
                    nc.vector.tensor_tensor(hid[:, k % HIDDEN], act_g[:, k % HIDDEN], gates[:, 2 + k % 2, :], ALU.mult
                                            ).then_inc(hid_done, 1)
                    if f == 6 and not (begins and v == 0 or ends and v == 1):
                        x_low(n, v + 1)
                    if ends and k == FT + 1:
                        dve.wait_ge(lo_done, n * STEPS + FT)
                    if ends and k > FT:
                        low(dve, nc.vector, n, k - 1)
                    if begins and k == 0:
                        softmax_max()
                    if begins and k == 2:
                        softmax_norm()
                    if begins and k == 3:
                        best_two()
                    if begins and k == 4:
                        best_indices()
                    if begins and k == 5:
                        choices()
                    if begins and k == 8:
                        units_each()
                    if begins and k == 9:
                        units_up_to()
                    if begins and k == 10:
                        places()
                    if begins and k == 12:
                        unit_experts()
                    if begins and k == 14:
                        shares()
                    if ends and k >= ADD_AT:
                        for t in range(2 * (k - ADD_AT), 2 * (k - ADD_AT) + 2):
                            add_low(t)

            def softmax_max():
                nc.vector.reduce_max(row[:], probs[:, :, 0:ROUTED], AX.X)
                dve.drain()
                nc.vector.tensor_tensor(probs[:, :, 0:ROUTED], probs[:, :, 0:ROUTED], wide(row[:]), ALU.subtract
                                        ).then_inc(max_done, 1)

            def softmax_norm():
                valid = probs[:, :, 0:ROUTED]
                dve.wait_ge(exp_done, 1)
                nc.vector.reduce_sum(row[:], valid, AX.X)
                dve.drain()
                nc.vector.reciprocal(g.ny[:], row[:])
                dve.drain()
                nc.vector.tensor_tensor(valid, valid, wide(g.ny[:]), ALU.mult)
                nc.vector.memset(probs[:, :, ROUTED:8], -1.0)
                dve.drain()

            def best_two():
                for t in range(NT):
                    nc.vector.max(best[:, t, :], probs[:, t, :])
                dve.drain()

            def best_indices():
                for t in range(NT):
                    nc.vector.max_index(best_at[:, t, :], best[:, t, :], probs[:, t, :])
                dve.drain()
                nc.vector.tensor_copy(where[:], best_at[:, :, 0:2])
                dve.drain()

            def choices():
                dve.wait_ge(consts, 8 + SLOT_UNITS + 1)
                for k in range(2):
                    nc.vector.tensor_tensor(chosen[k], numbers[:, 0:ROUTED].unsqueeze(1).broadcast_to([P, NT, ROUTED]),
                                            wide(where[:, :, k]), ALU.is_equal)
                dve.drain()
                nc.vector.tensor_tensor(taken[:, :, 0:ROUTED], chosen[0], chosen[1], ALU.add).then_inc(taken_done, 1)

            def shares():
                nc.vector.tensor_tensor(row[:], best[:, :, 0], best[:, :, 1], ALU.add)
                dve.drain()
                nc.vector.tensor_scalar(row[:], row[:], EPS_TOP, 2.0, ALU.add, ALU.mult)
                dve.drain()
                nc.vector.reciprocal(g.ny[:], row[:])
                dve.drain()
                for k in range(2):
                    nc.vector.scalar_tensor_tensor(weight[:, k, :], best[:, :, k], g.tg_f[:], g.ny[:],
                                                   ALU.mult, ALU.mult)
                for k, order in enumerate((ALU.is_lt, ALU.is_gt)):
                    nc.vector.tensor_tensor(is_first[:, k, :], spot[:, 0, :], spot[:, 1, :], order)
                dve.drain()
                for k in range(2):
                    nc.vector.tensor_tensor(g.share[:, k, :], is_first[:, k, :], weight[:, 0, :], ALU.mult)
                    nc.vector.tensor_tensor(part[:, k, :], is_first[:, 1 - k, :], weight[:, 1, :], ALU.mult)
                dve.drain()
                nc.vector.tensor_tensor(g.share[:], g.share[:], part[:], ALU.add)

            def units_each():
                nc.vector.memset(after[:], 0.0)
                nc.vector.memset(first[:], 0.0)
                dve.wait_ge(rank_pe, 1)
                for j in range(S // UW):
                    dve.drain()
                    nc.vector.scalar_tensor_tensor(after[:, 0:ROUTED], total, float(j * UW), after[:, 0:ROUTED],
                                                   ALU.is_gt, ALU.add)
                dve.drain()

            def units_up_to():
                for e in range(1, ROUTED):
                    nc.vector.tensor_tensor(after[:, e:e + 1], after[:, e - 1:e], after[:, e:e + 1], ALU.add)
                    dve.drain()
                nc.vector.tensor_scalar(first[:, 1:ROUTED], after[:, 0:ROUTED - 1], float(UW), None, ALU.mult)
                dve.drain()
                nc.vector.tensor_scalar(first[:], first[:], float(HEAD * UW), None, ALU.add)
                dve.drain()

            def places():
                nc.vector.tensor_tensor(taken[:, :, 0:ROUTED], ranks[:, 0:NT, :],
                                        first[:, 0:ROUTED].unsqueeze(1).broadcast_to([P, NT, ROUTED]), ALU.add)
                dve.drain()
                for k in range(2):
                    nc.vector.tensor_tensor(pos[:, :, 0:ROUTED], taken[:, :, 0:ROUTED], chosen[k], ALU.mult)
                    dve.drain()
                    nc.vector.reduce_sum(spot[:, k, :], pos[:, :, 0:ROUTED], AX.X)
                    dve.drain()
                for k, order in enumerate((ALU.min, ALU.max)):
                    ins = nc.vector.tensor_tensor(g.place_of[:, k, :], spot[:, 0, :], spot[:, 1, :], order)
                ins.then_inc(placed, 1)

            def unit_experts():
                nc.vector.memset(unit_of[:], 0.0)
                for e in range(ROUTED - 1):
                    dve.drain()
                    nc.vector.scalar_tensor_tensor(unit_of[:], unit_no[:], after[:, e:e + 1], unit_of[:],
                                                   ALU.is_ge, ALU.add)
                dve.drain()
                nc.vector.memset(g.expert_of[:, SLOT_UNITS:], 0)
                nc.vector.tensor_scalar(g.expert_of[:, 0:SLOT_UNITS], unit_of[:], 1.0, None, ALU.add
                                        ).then_inc(units_known, 1)

            dve.sem_inc(x_lo_done, 2)
            nc.vector.tensor_scalar(half[:], g.tg_f[:], 0.5, None, ALU.mult)
            turns(dve, body)
            dve.drain()
            low(dve, nc.vector, TURNS - 1, STEPS - 1)
            for t in range(2 * (STEPS - ADD_AT), NT):
                add_low(t)
            dve.drain()
            for c in range(NC):
                add_shared(c)
            dve.drain()
            for t in range(HEAD * TPU):
                add_high(t)
            add_shared(NC)
            dve.drain()
            for t in range(HEAD * TPU, NT):
                add_high(t)

        @block.gpsimd
        def _(pool):
            def gather(dst, k, t, got):
                pool.wait_ge(stored, 16 * (UNITS - 2 + k))
                nc.gpsimd.indirect_dma_start(
                    dst[:, t, :], None, g.out_dram[0:(UNITS - 2 + k) * UW, :],
                    bass.IndirectOffsetOnAxis(ap=g.place_of[:, k, t:t + 1], axis=0)).then_inc(got[t // TPC], 16)

            def scatter(i):
                k, t = i % 2, i // 2
                pool.wait_ge(placed, 1)
                nc.gpsimd.indirect_dma_start(
                    g.in_dram[:, :], bass.IndirectOffsetOnAxis(ap=g.place_of[:, k, t:t + 1], axis=0),
                    g.xn[:, t, :], None).then_inc(scattered, 16)

            def body(n, begins, ends):
                for k in range(STEPS):
                    if not (ends and k >= FT):
                        low(pool, nc.gpsimd, n, k)
                    if k % RAW == POOL_PLACE and not (ends and k >= FT):
                        v, f = k // FT, k % FT
                        weight_piece(nc, a, pool, "low on gpsimd", g, 1 - v, None, piece_cols(f), PIECES * (v + 1) + f,
                                     n * 2 * PIECES)
                    j = n * STEPS + k - SCATTER_AT if isinstance(n, int) else -1
                    if 0 <= j < SCATTER_STEPS:
                        for i in range(2 * NT * j // SCATTER_STEPS, 2 * NT * (j + 1) // SCATTER_STEPS):
                            scatter(i)
                    if ends and LOW_AT <= k < LOW_AT + NT // 2:
                        for t in range(2 * (k - LOW_AT), 2 * (k - LOW_AT) + 2):
                            gather(y_low, 0, t, got_low)

            for e in range(8):
                nc.gpsimd.memset(numbers[:, e:e + 1], float(e)).then_inc(consts, 1)
            for u in range(SLOT_UNITS):
                nc.gpsimd.memset(unit_no[:, u:u + 1], float(u)).then_inc(consts, 1)
            nc.gpsimd.memset(tri[:], 1.0).then_inc(tri_one, 1)
            pool.wait_ge(tri_one, 1)
            nc.gpsimd.affine_select(out=tri[:], in_=tri[:], compare_op=ALU.is_gt, fill=0.0,
                                    base=0, pattern=[[1, P]], channel_multiplier=-1).then_inc(consts, 1)
            pool.wait_ge(g.cleared, 16 * (D // P))
            turns(pool, body)
            for t in range(NT):
                gather(y_high, 1, t, got_high)


def kernel(**inputs):
    import numpy as _np
    import concourse.bacc as _bacc
    from concourse import mybir as _mybir
    from concourse.bass_utils import run_bass_kernel_spmd as _run

    x = {k: _np.asarray(v) for k, v in inputs.items()}

    def halves(v):
        return v.reshape(-1, P).T

    def packed(gate, up, down):
        parts = [gate.T.reshape(DH, P, DFF), up.T.reshape(DH, P, DFF)]
        cols = [p.transpose(1, 0, 2).reshape(P, DH * DFF) for p in parts]
        cols.append(down.T.reshape(FT, P, D).transpose(1, 0, 2).reshape(P, FT * D))
        return _np.concatenate(cols, axis=1)

    w = [packed(x["L0_ffn_shared_gate"], x["L0_ffn_shared_up"], x["L0_ffn_shared_down"])]
    w += [packed(x["L0_ffn_routed_gate"][e], x["L0_ffn_routed_up"][e], x["L0_ffn_routed_down"][e])
          for e in range(ROUTED)]
    arrays = {
        "x": x["x"][0], "ctx": x["ctx_1024"][0],
        "g_xattn": _np.broadcast_to(x["g_xattn"].reshape(1, 1), (P, 1)),
        "g_ffn": _np.broadcast_to(x["g_ffn"].reshape(1, 1), (P, 1)),
        "wq": x["L0_xattn_Wq"], "wk": x["L0_xattn_Wk"], "wvT": x["L0_xattn_Wv"].T,
        "wihT": x["L0_xattn_gru_wih"].T, "whhT": x["L0_xattn_gru_whh"].T,
        "bih": halves(x["L0_xattn_gru_bih"]), "bhh": halves(x["L0_xattn_gru_bhh"]),
        "slot_norm_w": halves(x["L0_xattn_slot_norm_w"]), "input_norm_w": halves(x["L0_xattn_input_norm_w"]),
        "routerT": x["L0_ffn_router_w"].T, "w": _np.stack(w),
    }
    nc = _bacc.Bacc("TRN2", target_bir_lowering=False, num_devices=1)
    feeds, aps = {}, {}
    for name, v in arrays.items():
        v = _np.ascontiguousarray(v)
        feeds[f"in_{name}"] = v
        aps[name] = nc.dram_tensor(f"in_{name}", v.shape, _mybir.dt.from_np(v.dtype), kind="ExternalInput").ap()
    out = nc.dram_tensor("out", (S, D), _mybir.dt.float32, kind="ExternalOutput").ap()
    build_kernel(nc, aps, out)
    r = _run(nc, [feeds], core_ids=[0])
    return r.results[0]["out"].reshape(1, S, D)
```
